# Optimizing a Trainium2 kernel written in Bass

```python
import numpy as np
import jax
import jax.numpy as jnp

def _softmax(x, axis=-1):
    return jax.nn.softmax(x, axis=axis)

def _gelu(x):
    return jax.nn.gelu(x, approximate=True)

def _silu(x):
    return jax.nn.silu(x)

def _sigmoid(x):
    return jax.nn.sigmoid(x)

def _layernorm(x, axis=-1, eps=1e-05):
    m = jnp.mean(x, axis=axis, keepdims=True)
    v = jnp.var(x, axis=axis, keepdims=True)
    return (x - m) / jnp.sqrt(v + eps)

def _scatter_add(tgt, idx, src, axis=0):
    return tgt.at[idx].add(src)

def _segment_sum(src, seg, n):
    return jax.ops.segment_sum(src, seg, n)
kernel_name = 'mk_gnn_ffn_d1_gnn_r32_b0f516'

def setup_inputs(seed: int=0):
    np.random.seed(seed)
    _w = jnp.asarray

    def _rec_inputs():
        import jax
        import jax.numpy as jnp
        _gk = jax.random.key(seed)
        x = -8.776e-05 + 1 * jax.random.normal(jax.random.fold_in(_gk, 1), (3125, 256), jnp.float32)
        _s = jax.random.randint(jax.random.fold_in(_gk, 2), (25000,), 0, 3125, jnp.int32)
        _d = jax.random.randint(jax.random.fold_in(_gk, 3), (25000,), 0, 3125, jnp.int32)
        _loop = jnp.arange(3125, dtype=jnp.int32)
        src = jnp.concatenate([_s, _d, _loop])
        dst = jnp.concatenate([_d, _s, _loop])
        _o = jnp.argsort(dst, stable=True)
        src = src[_o]
        dst = dst[_o]
        return (x, src, dst)
    x, src, dst = _rec_inputs()

    def _L0_gnn_setup():
        import jax, jax.numpy as jnp
        import numpy as np
        N = 625
        E = 10000
        HID = 256
        H = 4
        D = HID // H
        FF = 4 * HID

        def _layernorm(x, g, b, eps=1e-05):
            mu = jnp.mean(x, axis=-1, keepdims=True)
            var = jnp.var(x, axis=-1, keepdims=True)
            return (x - mu) * jax.lax.rsqrt(var + eps) * g + b

        def _transformer_conv(x, edge_index, Wq, bq, Wk, bk, Wv, bv, Wskip, bskip):
            src, dst = (edge_index[0], edge_index[1])
            n = x.shape[0]
            q = (x @ Wq + bq).reshape(n, H, D)
            k = (x @ Wk + bk).reshape(n, H, D)
            v = (x @ Wv + bv).reshape(n, H, D)
            qi = q[dst]
            kj = k[src]
            vj = v[src]
            alpha = jnp.sum(qi * kj, axis=-1) / jnp.sqrt(jnp.float32(D))
            m = jax.ops.segment_max(alpha, dst, num_segments=n)
            ex = jnp.exp(alpha - m[dst])
            denom = jax.ops.segment_sum(ex, dst, num_segments=n)
            a = ex / (denom[dst] + 1e-16)
            out = jax.ops.segment_sum(a[..., None] * vj, dst, num_segments=n)
            out = out.reshape(n, H * D)
            return out + x @ Wskip + bskip
        key = jax.random.key(seed)
        ks = jax.random.split(key, 20)
        w = lambda i, sh: jax.random.normal(ks[i], sh, dtype=jnp.float32) * 0.02
        return {'x': jax.random.normal(ks[0], (N, HID), dtype=jnp.float32), 'edge_index': jax.random.randint(ks[1], (2, E), 0, N, dtype=jnp.int64), 'Wq': w(2, (HID, HID)), 'bq': jnp.zeros((HID,), jnp.float32), 'Wk': w(3, (HID, HID)), 'bk': jnp.zeros((HID,), jnp.float32), 'Wv': w(4, (HID, HID)), 'bv': jnp.zeros((HID,), jnp.float32), 'Wskip': w(5, (HID, HID)), 'bskip': jnp.zeros((HID,), jnp.float32), 'ln1_g': jnp.ones((HID,), jnp.float32), 'ln1_b': jnp.zeros((HID,), jnp.float32), 'W1': w(6, (HID, FF)), 'b1': jnp.zeros((FF,), jnp.float32), 'W2': w(7, (FF, HID)), 'b2': jnp.zeros((HID,), jnp.float32), 'ln2_g': jnp.ones((HID,), jnp.float32), 'ln2_b': jnp.zeros((HID,), jnp.float32)}
    _L0_gnn_all = _L0_gnn_setup()
    _L0_gnn_in = {k: v for k, v in _L0_gnn_all.items() if k in ('Wq', 'bq', 'Wk', 'bk', 'Wv', 'bv', 'Wskip', 'bskip', 'ln1_g', 'ln1_b', 'W1', 'b1', 'W2', 'b2', 'ln2_g', 'ln2_b')}
    del _L0_gnn_all

    def _L0_ffn_setup():
        import jax, jax.numpy as jnp
        import numpy as np
        BN_EPS = 0.001

        def _bn(h, g, b, m, v):
            return g * (h - m) * jax.lax.rsqrt(v + BN_EPS) + b
        key = jax.random.key(seed)
        ks = jax.random.split(key, 8)
        B, F, Df = (256, 64, 256)
        E, H, D = (8, 256, 256)
        s1 = 1.0 / np.sqrt(Df)
        s2 = 1.0 / np.sqrt(H)
        return {'x': jax.random.normal(ks[0], (B, F, Df), jnp.float32), 'Wr': jax.random.normal(ks[1], (Df, E), jnp.float32) * s1, 'br': jnp.zeros((E,), jnp.float32), 'W1': jax.random.normal(ks[2], (E, Df, H), jnp.float32) * s1, 'b1': jnp.zeros((E, H), jnp.float32), 'g1': jnp.ones((E, H), jnp.float32), 'be1': jnp.zeros((E, H), jnp.float32), 'm1': jnp.zeros((E, H), jnp.float32), 'v1': jnp.ones((E, H), jnp.float32), 'W2': jax.random.normal(ks[3], (E, H, H), jnp.float32) * s2, 'b2': jnp.zeros((E, H), jnp.float32), 'g2': jnp.ones((E, H), jnp.float32), 'be2': jnp.zeros((E, H), jnp.float32), 'm2': jnp.zeros((E, H), jnp.float32), 'v2': jnp.ones((E, H), jnp.float32), 'Wo': jax.random.normal(ks[4], (E, H, D), jnp.float32) * s2, 'bo': jnp.zeros((E, D), jnp.float32)}
    _L0_ffn_all = _L0_ffn_setup()
    _L0_ffn_in = {k: v for k, v in _L0_ffn_all.items() if k in ('Wr', 'br', 'W1', 'b1', 'g1', 'be1', 'm1', 'v1', 'W2', 'b2', 'g2', 'be2', 'm2', 'v2', 'Wo', 'bo')}
    del _L0_ffn_all
    return {'x': x, 'src': src, 'dst': dst, 'L0_gnn_Wq': _L0_gnn_in['Wq'], 'L0_gnn_bq': _L0_gnn_in['bq'], 'L0_gnn_Wk': _L0_gnn_in['Wk'], 'L0_gnn_bk': _L0_gnn_in['bk'], 'L0_gnn_Wv': _L0_gnn_in['Wv'], 'L0_gnn_bv': _L0_gnn_in['bv'], 'L0_gnn_Wskip': _L0_gnn_in['Wskip'], 'L0_gnn_bskip': _L0_gnn_in['bskip'], 'L0_gnn_ln1_g': _L0_gnn_in['ln1_g'], 'L0_gnn_ln1_b': _L0_gnn_in['ln1_b'], 'L0_gnn_W1': _L0_gnn_in['W1'], 'L0_gnn_b1': _L0_gnn_in['b1'], 'L0_gnn_W2': _L0_gnn_in['W2'], 'L0_gnn_b2': _L0_gnn_in['b2'], 'L0_gnn_ln2_g': _L0_gnn_in['ln2_g'], 'L0_gnn_ln2_b': _L0_gnn_in['ln2_b'], 'L0_ffn_Wr': _L0_ffn_in['Wr'], 'L0_ffn_br': _L0_ffn_in['br'], 'L0_ffn_W1': _L0_ffn_in['W1'], 'L0_ffn_b1': _L0_ffn_in['b1'], 'L0_ffn_g1': _L0_ffn_in['g1'], 'L0_ffn_be1': _L0_ffn_in['be1'], 'L0_ffn_m1': _L0_ffn_in['m1'], 'L0_ffn_v1': _L0_ffn_in['v1'], 'L0_ffn_W2': _L0_ffn_in['W2'], 'L0_ffn_b2': _L0_ffn_in['b2'], 'L0_ffn_g2': _L0_ffn_in['g2'], 'L0_ffn_be2': _L0_ffn_in['be2'], 'L0_ffn_m2': _L0_ffn_in['m2'], 'L0_ffn_v2': _L0_ffn_in['v2'], 'L0_ffn_Wo': _L0_ffn_in['Wo'], 'L0_ffn_bo': _L0_ffn_in['bo']}

def reference(x, src, dst, L0_gnn_Wq, L0_gnn_bq, L0_gnn_Wk, L0_gnn_bk, L0_gnn_Wv, L0_gnn_bv, L0_gnn_Wskip, L0_gnn_bskip, L0_gnn_ln1_g, L0_gnn_ln1_b, L0_gnn_W1, L0_gnn_b1, L0_gnn_W2, L0_gnn_b2, L0_gnn_ln2_g, L0_gnn_ln2_b, L0_ffn_Wr, L0_ffn_br, L0_ffn_W1, L0_ffn_b1, L0_ffn_g1, L0_ffn_be1, L0_ffn_m1, L0_ffn_v1, L0_ffn_W2, L0_ffn_b2, L0_ffn_g2, L0_ffn_be2, L0_ffn_m2, L0_ffn_v2, L0_ffn_Wo, L0_ffn_bo):
    import jax
    import jax.numpy as jnp

    def _L0_gnn_ref(x, edge_index, Wq, bq, Wk, bk, Wv, bv, Wskip, bskip, ln1_g, ln1_b, W1, b1, W2, b2, ln2_g, ln2_b):
        import jax, jax.numpy as jnp
        import numpy as np
        N = 625
        E = 10000
        HID = 256
        H = 4
        D = HID // H
        FF = 4 * HID

        def _layernorm(x, g, b, eps=1e-05):
            mu = jnp.mean(x, axis=-1, keepdims=True)
            var = jnp.var(x, axis=-1, keepdims=True)
            return (x - mu) * jax.lax.rsqrt(var + eps) * g + b

        def _transformer_conv(x, edge_index, Wq, bq, Wk, bk, Wv, bv, Wskip, bskip):
            src, dst = (edge_index[0], edge_index[1])
            n = x.shape[0]
            q = (x @ Wq + bq).reshape(n, H, D)
            k = (x @ Wk + bk).reshape(n, H, D)
            v = (x @ Wv + bv).reshape(n, H, D)
            qi = q[dst]
            kj = k[src]
            vj = v[src]
            alpha = jnp.sum(qi * kj, axis=-1) / jnp.sqrt(jnp.float32(D))
            m = jax.ops.segment_max(alpha, dst, num_segments=n)
            ex = jnp.exp(alpha - m[dst])
            denom = jax.ops.segment_sum(ex, dst, num_segments=n)
            a = ex / (denom[dst] + 1e-16)
            out = jax.ops.segment_sum(a[..., None] * vj, dst, num_segments=n)
            out = out.reshape(n, H * D)
            return out + x @ Wskip + bskip
        x_new = _transformer_conv(x, edge_index, Wq, bq, Wk, bk, Wv, bv, Wskip, bskip)
        h = _layernorm(x + x_new, ln1_g, ln1_b)
        ffn = jax.nn.gelu(h @ W1 + b1, approximate=False) @ W2 + b2
        return _layernorm(h + ffn, ln2_g, ln2_b)

    def _L0_ffn_ref(x, Wr, br, W1, b1, g1, be1, m1, v1, W2, b2, g2, be2, m2, v2, Wo, bo):
        import jax, jax.numpy as jnp
        import numpy as np
        BN_EPS = 0.001

        def _bn(h, g, b, m, v):
            return g * (h - m) * jax.lax.rsqrt(v + BN_EPS) + b
        feat = jnp.mean(x, axis=0)
        w = jax.nn.softmax(feat @ Wr + br, axis=-1)
        h = jnp.einsum('bfd,edh->bfeh', x, W1) + b1
        h = jax.nn.relu(_bn(h, g1, be1, m1, v1))
        h = jnp.einsum('bfeh,ehk->bfek', h, W2) + b2
        h = jax.nn.relu(_bn(h, g2, be2, m2, v2))
        y = jnp.einsum('bfeh,ehd->bfed', h, Wo) + bo
        return jnp.einsum('bfed,fe->bfd', y, w)
    edge_index = jnp.stack([src, dst])
    x = x + _L0_gnn_ref(_layernorm(x, axis=-1), edge_index, L0_gnn_Wq, L0_gnn_bq, L0_gnn_Wk, L0_gnn_bk, L0_gnn_Wv, L0_gnn_bv, L0_gnn_Wskip, L0_gnn_bskip, L0_gnn_ln1_g, L0_gnn_ln1_b, L0_gnn_W1, L0_gnn_b1, L0_gnn_W2, L0_gnn_b2, L0_gnn_ln2_g, L0_gnn_ln2_b)
    x = x + _L0_ffn_ref(_layernorm(x, axis=-1)[None], L0_ffn_Wr, L0_ffn_br, L0_ffn_W1, L0_ffn_b1, L0_ffn_g1, L0_ffn_be1, L0_ffn_m1, L0_ffn_v1, L0_ffn_W2, L0_ffn_b2, L0_ffn_g2, L0_ffn_be2, L0_ffn_m2, L0_ffn_v2, L0_ffn_Wo, L0_ffn_bo)[0]
    return x

_drawn_inputs = setup_inputs


def setup_inputs(seed=0):
    import zlib

    import numpy as np

    out = dict(_drawn_inputs(seed))
    spreads = {'L0_gnn_bq': (0.0, 0.8),
     'L0_gnn_bk': (0.0, 0.8),
     'L0_gnn_bv': (0.0, 0.1),
     'L0_gnn_bskip': (0.0, 0.1),
     'L0_gnn_ln1_g': (1.0, 0.2),
     'L0_gnn_ln1_b': (0.0, 0.1),
     'L0_gnn_b1': (0.0, 0.448),
     'L0_gnn_b2': (0.0, 0.1),
     'L0_gnn_ln2_g': (1.0, 0.2),
     'L0_gnn_ln2_b': (0.0, 0.1),
     'L0_ffn_br': (0.0, 0.45),
     'L0_ffn_b1': (0.0, 0.612),
     'L0_ffn_g1': (1.0, 0.592),
     'L0_ffn_be1': (0.0, 0.626),
     'L0_ffn_m1': (0.0, 0.605),
     'L0_ffn_v1': (1.0, 0.6),
     'L0_ffn_b2': (0.0, 0.439),
     'L0_ffn_g2': (1.0, 0.565),
     'L0_ffn_be2': (0.0, 0.457),
     'L0_ffn_m2': (0.0, 0.45),
     'L0_ffn_v2': (1.0, 0.6),
     'L0_ffn_bo': (0.0, 0.328)}
    factors = {'L0_gnn_Wq': 8.0, 'L0_gnn_Wk': 8.0}
    for name, (base, spread) in spreads.items():
        noise = np.random.default_rng([zlib.crc32(name.encode()), seed]).standard_normal(out[name].shape)
        drawn = base * np.exp(spread * noise) if base else spread * noise
        out[name] = jnp.asarray(drawn.astype(out[name].dtype))
    for name, factor in factors.items():
        out[name] = (out[name] * factor).astype(out[name].dtype)
    return out
```

```python
from contextlib import ExitStack

import concourse.bass as bass
from concourse import mybir

F32 = mybir.dt.float32
BF16 = mybir.dt.bfloat16
I32 = mybir.dt.int32
ALU = mybir.AluOpType
ACT = mybir.ActivationFunctionType
AX = mybir.AxisListType

P = 128
N, HID, E = 3125, 256, 53125
H, D = 4, 64
FF = 4 * HID
NB, BP = 25, 125
KC = HID // P
TILES = (E + P - 1) // P
TG, TP = 4, TILES // 4
STEPS = TILES + NB - 1
SG, SP_ = 4, STEPS // 4
W = 20
C = STEPS // W
PAIRS = STEPS // 2
CP = W // 2
SLOT_PAIRS = 2 * CP
R = H * W
KVW = HID + H + HID
VO = HID + H
HW_ = D + 1
NEG = -1.0e30
FAR = 8192.0
LAG = 15
GU = 5
G = NB // GU
GN = GU * BP
HALF = 313
HALVES = [(0, HALF), (HALF, GN)]
NE = 8
LN_EPS = 1e-5
BN_EPS = 1e-3
SCALE = float(D) ** -0.5


def held(eng, turn):
    eng.sem_inc(turn, 1)


def project(nc, ctx, io, keep):
    c = ExitStack()
    with c:
        def sb(name, shape, dt=F32):
            return c.enter_context(nc.sbuf_tensor(name, shape, dt))

        def pb(name, shape):
            return c.enter_context(nc.psum_tensor(name, shape, F32))

        def sem(name):
            return ctx.enter_context(nc.semaphore(name))

        xs = sb("xs", [BP, NB, HID])
        wqk = sb("wqk", [P, KC, 2 * HID])
        wvs = sb("wvs", [P, KC, 2 * HID])
        bqk = sb("bqk", [BP, 2 * HID])
        bvs = sb("bvs", [BP, 2 * HID])
        st = sb("st", [BP, NB, 6])
        mv = sb("mv", [BP, NB, 2])
        ve = sb("ve", [BP, NB])
        mh = sb("mh", [BP, NB])
        rs = sb("rs", [BP, NB])
        xn = sb("xn", [BP, 2, HID])
        xnT = sb("xnT", [P, 2, KC, BP])
        q32 = sb("q32", [BP, 2, HID])
        r32 = sb("r32", [BP, 2, HID])
        kvst = sb("kvst", [BP, 2, KVW])
        resst = sb("resst", [BP, 2, HID])
        rest = sb("rest", [BP, 2, HID])
        dint = sb("dint", [TP, TG, P], I32)
        sint = sb("sint", [TP, TG, P], I32)
        pint = sb("pint", [TP, TG, 1], I32)
        pf = sb("pf", [TP, TG, 1])
        ne = sb("ne", [TP, TG, P])
        rec = sb("rec", [TP, TG, 3 * P])
        io25 = sb("io25", [TP, NB], I32)
        io25f = sb("io25f", [TP, NB])
        before = sb("before", [TP, TG, NB])
        ioS = sb("ioS", [NB, STEPS], I32)
        ioSf = sb("ioSf", [NB, STEPS])
        ioG = sb("ioG", [SP_, SG], I32)
        ioGf = sb("ioGf", [SP_, SG])
        first = sb("first", [NB, 1])
        begun = sb("begun", [NB, STEPS])
        bs = sb("bs", [SP_, SG])
        bm = sb("bm", [SP_, SG])
        tidx = sb("tidx", [SP_, SG], I32)
        grec = sb("grec", [SP_, SG, 3 * P])
        drel = sb("drel", [SP_, SG, P])
        drelb = sb("drelb", [SP_, SG, P], BF16)
        mins = sb("mins", [SP_, 3, SG])
        n0row = sb("n0row", [1, STEPS + 1])
        v1 = sb("v1", [P, STEPS])
        v2 = sb("v2", [P, STEPS])
        iop = sb("iop", [P, 1], I32)
        iof = sb("iof", [P, P], I32)

        psW = [[pb(f"psW{b}{k}", [P, 512]) for k in range(2)] for b in range(2)]
        psT = [pb(f"psT{b}", [P, 512]) for b in range(2)]
        psX = [pb(f"psX{b}", [P, 512]) for b in range(2)]

        s_x, s_w, s_b = sem("s_x"), sem("s_w"), sem("s_b")
        s_ed, s_rec, s_grec = sem("s_ed"), sem("s_rec"), sem("s_grec")
        s_drel = sem("s_drel")
        s_kvo = [sem("s_kvo0"), sem("s_kvo1")]
        s_reso = [sem("s_reso0"), sem("s_reso1")]
        s_init, s_iota, s_const = sem("s_init"), sem("s_iota"), sem("s_const")
        s_tab, s_tabpe = sem("s_tab"), sem("s_tabpe")
        s_st, s_mv, s_ve, s_rs = sem("s_st"), sem("s_mv"), sem("s_ve"), sem("s_rs")
        s_xn, s_tr, s_xt, s_pr = sem("s_xn"), sem("s_tr"), sem("s_xt"), sem("s_pr")
        s_q, s_rest, s_row, s_pad = sem("s_q"), sem("s_rest"), sem("s_row"), sem("s_pad")
        s_qh, s_r1, s_qm, s_ql = sem("s_qh"), sem("s_r1"), sem("s_qm"), sem("s_ql")

        ident, iotaF, iotaP, one = keep["ident"], keep["iotaF"], keep["iotaP"], keep["one"]
        ones = keep["ones"]
        q3 = keep["q3"]
        x_v = io["x"].rearrange("(t p) d -> p t d", p=BP)
        kv_v = io["kv"].rearrange("(t p) d -> p t d", p=BP)
        res_v = io["res"].rearrange("(t p) d -> p t d", p=BP)
        rec_v = io["rec"].rearrange("(g p) d -> p g d", p=TP)
        drel_v = io["drel"].rearrange("(g p) d -> p g d", p=SP_)
        dst, src = io["dst"], io["src"]
        FULL = 3 * TP * P
        LAST = (TILES - 1) * P

        block = c.enter_context(nc.Block())

        @block.sync
        def _(sp):
            sp.wait_ge(s_init, 3)
            for t, a in ((dint, dst), (sint, src)):
                sp.dma_start(t[:, 0:3, :], a[0:FULL].rearrange("(g p l) -> p g l", g=3, p=TP)).then_inc(s_ed, 16)
                sp.dma_start(t[0:TP - 1, 3, :], a[FULL:LAST].rearrange("(p l) -> p l", l=P)).then_inc(s_ed, 16)
                sp.dma_start(t[TP - 1:TP, 3, 0:E - LAST], a[LAST:E].rearrange("(p l) -> p l", p=1)).then_inc(s_ed, 16)
            lasts = dst[0:LAST].rearrange("(t l) -> t l", l=P)[:, P - 1:P]
            with nc.allow_non_contiguous_dma(reason="one word per edge tile"):
                sp.dma_start(pint[1:TP, 0, :], lasts[0:TP - 1, :]).then_inc(s_ed, 16)
                for g in range(1, TG):
                    sp.dma_start(pint[0:TP, g, :], lasts[g * TP - 1:(g + 1) * TP - 1, :]).then_inc(s_ed, 16)
            sp.dma_start(xs[:, :, :], x_v).then_inc(s_x, 16)
            for w, a, b in ((wqk, "L0_gnn_Wq", "L0_gnn_Wk"), (wvs, "L0_gnn_Wv", "L0_gnn_Wskip")):
                sp.dma_start(w[:, :, 0:HID], io[a].rearrange("(k p) n -> p k n", p=P)).then_inc(s_w, 16)
                sp.dma_start(w[:, :, HID:2 * HID], io[b].rearrange("(k p) n -> p k n", p=P)).then_inc(s_w, 16)
            for t, a, b in ((bqk, "L0_gnn_bq", "L0_gnn_bk"), (bvs, "L0_gnn_bv", "L0_gnn_bskip")):
                sp.dma_start(t[:, 0:HID], io[a].partition_broadcast(BP)).then_inc(s_b, 16)
                sp.dma_start(t[:, HID:2 * HID], io[b].partition_broadcast(BP)).then_inc(s_b, 16)
            sp.wait_ge(s_tab, 6)
            sp.dma_start(rec_v, rec[:, :, :]).then_inc(s_rec, 16)

            def store(t, b):
                sp.wait_ge(s_row, t + 1)
                sp.dma_start(kv_v[:, t, :], kvst[:, b, :]).then_inc(s_kvo[b], 16)
                sp.dma_start(res_v[:, t, :], resst[:, b, :]).then_inc(s_reso[b], 16)

            with sp.Fori(0, NB - 1, 2) as t:
                store(t, 0)
                store(t + 1, 1)
            store(NB - 1, 0)
            sp.wait_ge(s_tab, 21)
            sp.dma_start(drel_v, drelb[:, :, :]).then_inc(s_drel, 16)
            sp.wait_ge(s_drel, 16)
            for b in range(2):
                sp.wait_ge(s_kvo[b], 16 * ((NB + 1 - b) // 2))
                sp.wait_ge(s_reso[b], 16 * ((NB + 1 - b) // 2))

        @block.gpsimd
        def _(pool):
            nc.gpsimd.memset(dint[:, :, :], int(FAR)).then_inc(s_init, 1)
            nc.gpsimd.memset(sint[:, :, :], 0).then_inc(s_init, 1)
            nc.gpsimd.memset(pint[:, :, :], -1).then_inc(s_init, 1)
            nc.gpsimd.iota(io25[:, :], pattern=[[BP, NB]], base=0, channel_multiplier=0).then_inc(s_iota, 1)
            nc.gpsimd.iota(ioS[:, :], pattern=[[1, STEPS]], base=0, channel_multiplier=0).then_inc(s_iota, 1)
            nc.gpsimd.iota(ioG[:, :], pattern=[[SP_, SG]], base=0, channel_multiplier=1).then_inc(s_iota, 1)
            nc.gpsimd.iota(iop[:, :], pattern=[[0, 1]], base=0, channel_multiplier=1).then_inc(s_iota, 1)
            nc.gpsimd.iota(iof[:, :], pattern=[[1, P]], base=0, channel_multiplier=0).then_inc(s_iota, 1)
            nc.gpsimd.memset(mh[:, :], -0.5).then_inc(s_pad, 1)
            nc.gpsimd.memset(kvst[:, :, HID:VO], 0.0).then_inc(s_pad, 1)
            pool.wait_ge(s_pad, 1)
            pool.wait_ge(s_mv, NB)
            nc.gpsimd.tensor_scalar(ve[:, :], mv[:, :, 1], LN_EPS, None, ALU.add).then_inc(s_ve, 1)
            pool.wait_ge(s_ve, 1)
            nc.gpsimd.tensor_tensor(rs[:, :], ve[:, :], mh[:, :], ALU.pow).then_inc(s_rs, 1)
            pool.wait_ge(s_tab, 15)
            pool.wait_ge(s_rec, 16)
            for g in range(SG):
                nc.gpsimd.indirect_dma_start(
                    out=grec[:, g, :], out_offset=None, in_=io["rec"],
                    in_offset=bass.IndirectOffsetOnAxis(ap=tidx[:, g:g + 1], axis=0)).then_inc(s_grec, 16)

            def split(t, b, first_use):
                pool.wait_ge(s_qh, t + 1)
                nc.gpsimd.tensor_tensor(r32[:, b, :], q32[:, b, :], q3[:, 0, bass.ds(t, 1), :].rearrange("p a d -> p (a d)"),
                                        ALU.subtract).then_inc(s_r1, 1)
                pool.wait_ge(s_qm, t + 1)
                nc.gpsimd.tensor_tensor(q3[:, 2, bass.ds(t, 1), :].rearrange("p a d -> p (a d)"), r32[:, b, :],
                                        q3[:, 1, bass.ds(t, 1), :].rearrange("p a d -> p (a d)"),
                                        ALU.subtract).then_inc(s_ql, 1)

            with pool.Fori(0, NB - 1, 2) as t:
                split(t, 0, False)
                split(t + 1, 1, False)
            split(NB - 1, 0, False)

        @block.scalar
        def _(act):
            def part(t, b):
                act.wait_ge(s_tr, t + 1)
                nc.scalar.activation(xnT[:, b, :, :], psT[b][:, 0:KC * BP].rearrange("p (k n) -> p k n", k=KC),
                                     ACT.Copy).then_inc(s_xt, 1)

            def high(t, b):
                act.wait_ge(s_q, t + 1)
                nc.scalar.activation(q3[:, 0, bass.ds(t, 1), :].rearrange("p a d -> p (a d)"), q32[:, b, :],
                                     ACT.Copy).then_inc(s_qh, 1)

            def middle(t, b):
                act.wait_ge(s_r1, t + 1)
                nc.scalar.activation(q3[:, 1, bass.ds(t, 1), :].rearrange("p a d -> p (a d)"), r32[:, b, :],
                                     ACT.Copy).then_inc(s_qm, 1)

            part(0, 0)
            with act.Fori(0, NB - 1, 2) as t:
                part(t + 1, 1)
                high(t, 0)
                middle(t, 0)
                part(t + 2, 0)
                high(t + 1, 1)
                middle(t + 1, 1)
            high(NB - 1, 0)
            middle(NB - 1, 0)

        @block.tensor
        def _(pe):
            pe.wait_ge(s_const, 4)
            pe.wait_ge(s_tab, 7)
            for g in range(TG):
                last = nc.tensor.matmul(psX[0][0:NB, 0:1], before[:, g, :], ones[0:TP, 0:1], start=(g == 0), stop=(g == TG - 1))
            last.then_inc(s_tabpe, 1)
            pe.wait_ge(s_tab, 9)
            for g in range(SG):
                nc.tensor.matmul(psX[1][0:SP_, g:g + 1], begun[:, g * SP_:(g + 1) * SP_], ones[0:NB, 0:1], start=True, stop=True)
            nc.tensor.matmul(psX[0][0:1, 0:STEPS], ones[0:NB, 0:1], begun[:, :], start=True, stop=True).then_inc(s_tabpe, 1)

            pe.wait_ge(s_w, 64)

            def rows(t, b):
                pe.wait_ge(s_xn, t + 1)
                for k in range(KC):
                    last = nc.tensor.transpose(psT[b][:, k * BP:(k + 1) * BP], xn[:, b, k * P:(k + 1) * P],
                                               ident[0:BP, 0:BP])
                last.then_inc(s_tr, 1)

            def products(t, b, fresh):
                pe.wait_ge(s_xt, t + 1)
                if not fresh:
                    pe.wait_ge(s_row, t - 1)
                for w, ps in ((wqk, psW[b][0]), (wvs, psW[b][1])):
                    for k in range(KC):
                        last = nc.tensor.matmul(ps[0:BP, :], xnT[:, b, k, :], w[:, k, :], start=(k == 0), stop=(k == KC - 1))
                last.then_inc(s_pr, 1)

            rows(0, 0)
            rows(1, 1)
            products(0, 0, True)
            rows(2, 0)
            products(1, 1, True)
            with pe.Fori(2, NB - 1, 2) as t:
                rows(t + 1, 1)
                products(t, 0, False)
                rows(t + 2, 0)
                products(t + 1, 1, False)
            products(NB - 1, 0, False)

            pe.wait_ge(s_tab, 24)
            pe.wait_ge(s_row, NB)
            for k, ps in ((0, psW[0][0]), (1, psW[0][1]), (2, psW[1][0])):
                for g in range(SG):
                    a = drel[:, g, :] if k == 1 else grec[:, g, k * P:(k + 1) * P]
                    nc.tensor.transpose(ps[:, g * SP_:(g + 1) * SP_], a, ident[0:SP_, 0:SP_])
            for k, ps in ((0, psT[0]), (1, psT[1]), (2, psW[1][1])):
                for g in range(SG):
                    last = nc.tensor.matmul(ps[0:1, g * SP_:(g + 1) * SP_], mins[:, k, g:g + 1], ident[0:SP_, 0:SP_],
                                            start=True, stop=True)
            last.then_inc(s_tabpe, 1)

        @block.vector
        def _(dve):
            dve.wait_ge(s_iota, 5)
            nc.vector.tensor_copy(iotaP[:, :], iop[:, :]).then_inc(s_const, 1)
            nc.vector.tensor_copy(iotaF[:, :], iof[:, :]).then_inc(s_const, 1)
            nc.vector.memset(ones[:, :], 1.0).then_inc(s_const, 1)
            dve.wait_ge(s_const, 3)
            nc.vector.tensor_scalar(ident[:, :], iotaF[:, :], iotaP[:, 0:1], None, ALU.is_equal).then_inc(s_const, 1)
            dve.wait_ge(s_ed, 160)
            nc.vector.tensor_copy(rec[:, :, 0:P], sint[:, :, :]).then_inc(s_tab, 1)
            nc.vector.tensor_copy(rec[:, :, P:2 * P], dint[:, :, :]).then_inc(s_tab, 1)
            nc.vector.tensor_copy(pf[:, :, :], pint[:, :, :]).then_inc(s_tab, 1)
            dve.wait_ge(s_tab, 3)
            nc.vector.tensor_tensor(ne[:, :, 1:P], rec[:, :, P + 1:2 * P], rec[:, :, P:2 * P - 1], ALU.not_equal).then_inc(s_tab, 1)
            nc.vector.tensor_tensor(ne[:, :, 0:1], rec[:, :, P:P + 1], pf[:, :, :], ALU.not_equal).then_inc(s_tab, 1)
            dve.wait_ge(s_tab, 5)
            nc.vector.tensor_scalar(rec[:, :, 2 * P:3 * P], ne[:, :, :], NEG, None, ALU.mult).then_inc(s_tab, 1)
            nc.vector.tensor_copy(io25f[:, :], io25[:, :]).then_inc(s_const, 1)
            nc.vector.tensor_copy(ioSf[:, :], ioS[:, :]).then_inc(s_const, 1)
            nc.vector.tensor_copy(ioGf[:, :], ioG[:, :]).then_inc(s_const, 1)
            dve.wait_ge(s_const, 7)
            nc.vector.tensor_tensor(before[:, :, :], io25f[:, :].unsqueeze(1).broadcast_to([TP, TG, NB]),
                                    rec[:, :, 2 * P - 1:2 * P].broadcast_to([TP, TG, NB]), ALU.is_gt).then_inc(s_tab, 1)
            dve.wait_ge(s_tabpe, 1)
            nc.vector.tensor_tensor(first[:, :], psX[0][0:NB, 0:1], iotaP[0:NB, :], ALU.add).then_inc(s_tab, 1)
            dve.wait_ge(s_tab, 8)
            nc.vector.tensor_scalar(begun[:, :], ioSf[:, :], first[:, 0:1], None, ALU.is_ge).then_inc(s_tab, 1)
            dve.wait_ge(s_tabpe, 2)
            nc.vector.tensor_scalar(bs[:, :], psX[1][0:SP_, 0:SG], -1.0, None, ALU.add).then_inc(s_tab, 1)
            nc.vector.tensor_scalar(keep["brow"][:, :], psX[0][0:1, 0:STEPS], -1.0, None, ALU.add).then_inc(s_tab, 1)
            dve.wait_ge(s_tab, 11)
            nc.vector.tensor_tensor(tidx[:, :], ioGf[:, :], bs[:, :], ALU.subtract).then_inc(s_tab, 1)
            nc.vector.tensor_scalar(bm[:, :], bs[:, :], -float(BP), None, ALU.mult).then_inc(s_tab, 1)
            nc.vector.memset(n0row[:, :], NEG).then_inc(s_tab, 1)
            nc.vector.memset(one[:, :], 1.0).then_inc(s_tab, 1)

            dve.wait_ge(s_x, 16)
            with dve.Fori(0, NB) as t:
                nc.vector.bn_stats(st[:, t, :], xs[:, t, :]).then_inc(s_st, 1)
            dve.wait_ge(s_st, NB)
            for t in range(NB):
                nc.vector.bn_aggr(mv[:, t, :], st[:, t, :]).then_inc(s_mv, 1)
            dve.wait_ge(s_b, 64)
            dve.wait_ge(s_pad, 2)
            dve.wait_ge(s_rs, 1)

            def norm(t, b):
                nc.vector.tensor_scalar(xn[:, b, :], xs[:, t, :], mv[:, t, 0:1], rs[:, bass.ds(t, 1)],
                                        ALU.subtract, ALU.mult).then_inc(s_xn, 1)

            def rows(t, b, fresh):
                dve.wait_ge(s_pr, t + 1)
                if not fresh:
                    dve.wait_ge(s_r1, t - 1)
                    if b == 0:
                        dve.wait_ge(s_kvo[0], 8 * t)
                        dve.wait_ge(s_reso[0], 8 * t)
                    else:
                        dve.wait_ge(s_kvo[1], 8 * t - 8)
                        dve.wait_ge(s_reso[1], 8 * t - 8)
                nc.vector.tensor_tensor(rest[:, b, :], psW[b][1][0:BP, HID:2 * HID], xn[:, b, :], ALU.add).then_inc(s_rest, 1)
                nc.vector.tensor_tensor(q32[:, b, :], psW[b][0][0:BP, 0:HID], bqk[:, 0:HID], ALU.add).then_inc(s_q, 1)
                nc.vector.tensor_tensor(kvst[:, b, 0:HID], psW[b][0][0:BP, HID:2 * HID], bqk[:, HID:2 * HID], ALU.add)
                nc.vector.tensor_tensor(kvst[:, b, VO:KVW], psW[b][1][0:BP, 0:HID], bvs[:, 0:HID], ALU.add)
                dve.wait_ge(s_rest, t + 1)
                nc.vector.tensor_tensor(resst[:, b, :], rest[:, b, :], bvs[:, HID:2 * HID], ALU.add).then_inc(s_row, 1)

            norm(0, 0)
            norm(1, 1)
            rows(0, 0, True)
            norm(2, 0)
            rows(1, 1, True)
            norm(3, 1)
            with dve.Fori(2, NB - 3, 2) as t:
                rows(t, 0, False)
                norm(t + 2, 0)
                rows(t + 1, 1, False)
                norm(t + 3, 1)
            rows(NB - 3, 0, False)
            norm(NB - 1, 0)
            rows(NB - 2, 1, False)
            rows(NB - 1, 0, False)

            dve.wait_ge(s_grec, 64)
            dve.wait_ge(s_tab, 15)
            for g in range(SG):
                nc.vector.tensor_scalar(drel[:, g, :], grec[:, g, P:2 * P], bm[:, g:g + 1], None, ALU.add).then_inc(s_tab, 1)
            dve.wait_ge(s_tab, 19)
            nc.vector.tensor_copy(drelb[:, 0:2, :], drel[:, 0:2, :]).then_inc(s_tab, 1)
            nc.vector.tensor_copy(drelb[:, 2:4, :], drel[:, 2:4, :]).then_inc(s_tab, 1)
            nc.vector.tensor_reduce(mins[:, 0, :], grec[:, :, 2 * P:3 * P], AX.X, ALU.min).then_inc(s_tab, 1)
            nc.vector.tensor_reduce(mins[:, 1, :], grec[:, :, 2 * P + 1:3 * P], AX.X, ALU.min).then_inc(s_tab, 1)
            nc.vector.tensor_copy(mins[:, 2, :], grec[:, :, 2 * P]).then_inc(s_tab, 1)
            nc.vector.memset(keep["fwd"][:, :, :, :], NEG).then_inc(s_tab, 1)
            nc.vector.memset(keep["bwd"][:, :, :, :], NEG).then_inc(s_tab, 1)
            dve.wait_ge(s_tabpe, 3)
            nc.vector.tensor_copy(keep["srcI"][:, :], psW[0][0][:, 0:STEPS])
            nc.vector.tensor_copy(keep["dstR"][:, :], psW[0][1][:, 0:STEPS])
            nc.vector.tensor_copy(keep["startN"][:, :], psW[1][0][:, 0:STEPS])
            nc.vector.tensor_scalar(v1[:, :], psW[0][1][:, 0:STEPS], 0.0, NEG, ALU.is_lt, ALU.mult).then_inc(s_tab, 1)
            nc.vector.tensor_scalar(v2[:, :], psW[0][1][:, 0:STEPS], BP - 1.0, NEG, ALU.is_gt, ALU.mult).then_inc(s_tab, 1)
            nc.vector.tensor_copy(n0row[:, 0:STEPS], psW[1][1][0:1, 0:STEPS]).then_inc(s_tab, 1)
            dve.wait_ge(s_tab, 29)
            nc.vector.tensor_tensor(keep["valN"][:, :], v1[:, :], v2[:, :], ALU.add)
            nxt = n0row[:, 1:STEPS + 1].rearrange("p (c w) -> p c w", w=W)
            for h in range(H):
                nc.vector.tensor_copy(keep["fwd"][:, :, h, 1:W + 1], psT[0][0:1, 0:STEPS].rearrange("p (c w) -> p c w", w=W))
                nc.vector.tensor_tensor(keep["bwd"][:, :, h, 1:W + 1],
                                        psT[1][0:1, 0:STEPS].rearrange("p (c w) -> p c w", w=W)[:, :, ::-1],
                                        nxt[:, :, ::-1], ALU.add)
                nc.vector.tensor_copy(keep["nxt"][:, :, h, :], nxt)


(V_ALPHA, V_F1, V_TAIL, V_CARRY, V_INH, V_CIN, V_F2, V_B1, V_HEAD, V_BACK, V_IV, V_FD, V_FMIN, V_NEXT, V_OH0, V_BIN, V_G,
 V_DIFF, V_FAC, V_RESC) = range(1, 21)
NV = 20
(T_IN, T_TAIL, T_CARRY, T_HEAD, T_IV, T_OUT, T_FAC) = range(1, 8)
NT = 7


def attend(nc, ctx, io, keep):
    c = ExitStack()
    with c:
        def sb(name, shape, dt=F32):
            return c.enter_context(nc.sbuf_tensor(name, shape, dt))

        def pb(name, shape):
            return c.enter_context(nc.psum_tensor(name, shape, F32))

        def sem(name):
            return ctx.enter_context(nc.semaphore(name))

        ident, iotaF, iotaP, one = keep["ident"], keep["iotaF"], keep["iotaP"], keep["one"]
        q3, acc, brow = keep["q3"], keep["acc"], keep["brow"]
        dstR, valN = keep["dstR"], keep["valN"]

        kv = sb("kvring", [P, 2 * SLOT_PAIRS, KVW])
        idx = sb("idx", [P, 2, W], I32)
        stc = sb("stc", [P, 2, H, W])
        ohT = [sb(f"ohT{b}", [BP, W * P], BF16) for b in range(2)]
        noh = sb("noh", [BP, 2])
        oh = sb("oh", [P, 2, 2, BP])
        oh0 = sb("oh0", [1, BP])
        prod = sb("prod", [P, 2, 2 * HID])
        alpha = sb("alpha", [P, 2, H, W])
        alm = sb("alm", [P, H, W])
        dif = sb("dif", [P, H, W])
        nrow = sb("nrow", [R, P + 1])
        F1 = sb("F1", [R, P])
        F2 = sb("F2", [R, P])
        B1 = sb("B1", [R, P])
        Gm = sb("Gm", [R, P])
        cin = sb("cin", [R, 1])
        bin_ = sb("bin_", [R, 1])
        tails = sb("tails", [1, H, W + 1])
        heads = sb("heads", [1, H, W + 1])
        carry = sb("carry", [1, H, W + 1])
        back = sb("back", [1, H, W + 1])
        iv = sb("iv", [1, H, W])
        inh = sb("inh", [1, H, W])
        fd = sb("fd", [1, H])
        fm = sb("fm", [1, H])
        fx = sb("fx", [1, H])
        fac = sb("fac", [BP, H])

        psQ = [pb(f"psQ{b}", [P, 512]) for b in range(2)]
        psA = [[pb(f"psA{b}{k}", [P, 512]) for k in range(2)] for b in range(2)]
        psM = pb("psM", [P, 512])
        psR = pb("psR", [P, 512])

        s_set = sem("s_set")
        s_turn = [sem("s_turn_sp"), sem("s_turn_pool")]
        s_idx = sem("s_idx")
        s_kv = [sem(f"s_kv{k}") for k in range(SLOT_PAIRS)]
        s_bc = [sem("s_bc0"), sem("s_bc1")]
        s_oht, s_noh = sem("s_oht"), sem("s_noh")
        s_qe, s_prod, s_alpha = sem("s_qe"), sem("s_prod"), sem("s_alpha")
        s_mv, s_mp = sem("s_maxv"), sem("s_maxp")
        s_nrow, s_exp, s_fx = sem("s_nrow"), sem("s_exp"), sem("s_fx")
        s_pv, s_oh, s_agg, s_acc = sem("s_pv"), sem("s_oh"), sem("s_agg"), sem("s_acc")

        drel_row = io["drel"].rearrange("s l -> (s l)")
        block = c.enter_context(nc.Block())

        def walk(eng, at):
            for j in range(SLOT_PAIRS):
                at(0, j, True)
            with eng.Fori(1, PAIRS // SLOT_PAIRS) as i:
                for j in range(SLOT_PAIRS):
                    at(i, j, False)
            for j in range(LAG + 1):
                at(PAIRS // SLOT_PAIRS, j, False)

        def scored(i):
            return not (isinstance(i, int) and i >= PAIRS // SLOT_PAIRS)

        @block.sync
        def _(sp):
            def fetch(cc, par, fresh):
                if not fresh:
                    sp.wait_ge(s_qe, CP * cc - CP)
                    held(sp, s_turn[0])
                    sp.wait_ge(s_noh, cc - 1)
                    held(sp, s_turn[0])
                sp.dma_start(ohT[par][:, :], drel_row[bass.ds(cc * (W * P), W * P)].partition_broadcast(BP)
                             ).then_inc(s_bc[par], 16)

            fetch(0, 0, True)
            fetch(1, 1, True)
            with sp.Fori(1, C // 2) as i:
                fetch(2 * i, 0, False)
                fetch(2 * i + 1, 1, False)
            sp.wait_ge(s_qe, CP * (C - 1))
            sp.wait_ge(s_noh, C - 1)
            sp.dma_start(ohT[0][:, :], drel_row[0:W * P].partition_broadcast(BP)).then_inc(s_bc[0], 16)

        @block.gpsimd
        def _(pool):
            def at(i, j, fresh):
                if not scored(i):
                    return
                pair = SLOT_PAIRS * i + j
                cc, par = 2 * i + j // CP, j // CP
                if j % CP == 0:
                    if not fresh:
                        pool.wait_ge(s_alpha, CP * cc - CP)
                        held(pool, s_turn[1])
                        pool.wait_ge(s_mp, NT * (cc - 2) + T_IN)
                        held(pool, s_turn[1])
                    nc.gpsimd.tensor_copy(idx[:, par, :], keep["srcI"][:, bass.ds(W * cc, W)]).then_inc(s_idx, 1)
                    nc.gpsimd.tensor_copy(stc[:, par, :, :], keep["startN"][:, bass.ds(W * cc, W)].unsqueeze(1)
                                          .broadcast_to([P, H, W])).then_inc(s_idx, 1)
                    pool.wait_ge(s_idx, 2 * cc + 2)
                    held(pool, s_turn[1])
                if not fresh:
                    pool.wait_ge(s_agg, pair - SLOT_PAIRS + 1)
                    held(pool, s_turn[1])
                for k in range(2):
                    slot = 2 * j + k
                    nc.gpsimd.indirect_dma_start(
                        out=kv[:, slot, :], out_offset=None, in_=io["kv"],
                        in_offset=bass.IndirectOffsetOnAxis(ap=idx[:, par, (slot % W):(slot % W) + 1], axis=0)
                    ).then_inc(s_kv[j], 16)

            walk(pool, at)

        @block.scalar
        def _(act):
            def at(i, j, fresh):
                pair = SLOT_PAIRS * i + j
                m = 2 * i + j // CP - 1
                mpar = (j // CP + 1) % 2
                jj = j % CP
                if not (fresh and j < CP):
                    if jj == 0 and not (isinstance(m, int) and m >= C):
                        act.wait_ge(s_mp, NT * m + T_IN)
                        nc.scalar.activation(nrow[:, 0:P], psM[0:R, P:2 * P], ACT.Copy).then_inc(s_nrow, 1)
                    if jj == 3 and not (isinstance(m, int) and m >= C):
                        act.wait_ge(s_mv, NV * m + V_DIFF)
                        out = kv[:, W * mpar:W * mpar + W, 0:H * HW_].rearrange("p w (h e) -> p h w e", h=H)[:, :, :, D]
                        nc.scalar.activation(out, dif[:, :, :], ACT.Exp, scale=SCALE).then_inc(s_exp, 1)
                        nc.scalar.activation(fx[:, :], fm[:, :], ACT.Exp, scale=SCALE).then_inc(s_fx, 1)
                if fresh and j < LAG or not fresh and isinstance(i, int) and j >= LAG:
                    return
                b = pair - LAG
                sj = (j - LAG) % SLOT_PAIRS
                bc = 2 * i + (j - LAG) // CP
                act.wait_ge(s_exp, bc + 1)
                for k in range(2):
                    s = 2 * sj + k
                    for h in range(H):
                        last = nc.scalar.activation(kv[:, s, h * HW_:h * HW_ + D], kv[:, s, VO + h * D:VO + (h + 1) * D],
                                                    ACT.Copy, scale=kv[:, s, h * HW_ + D:(h + 1) * HW_])
                last.then_inc(s_pv, 1)

            walk(act, at)

        @block.tensor
        def _(pe):
            pe.wait_ge(s_set, 5)

            def at(i, j, fresh):
                pair = SLOT_PAIRS * i + j
                cc, par, jj = 2 * i + j // CP, j // CP, j % CP
                m = cc - 1
                mpar = (par + 1) % 2
                staged = not (fresh and j < CP) and not (isinstance(m, int) and m >= C)
                if scored(i):
                    pe.wait_ge(s_oht, cc + 1)
                    if not (fresh and j < 2):
                        pe.wait_ge(s_prod, pair - 1)
                    for k in range(2):
                        blk = nc.tensor.value_load(brow[0:1, bass.ds(2 * pair + k, 1)], min_val=0, max_val=NB - 1)
                        w = 2 * jj + k
                        for part in range(3):
                            last = nc.tensor.matmul(psQ[j % 2][:, k * HID:(k + 1) * HID], ohT[par][:, w * P:(w + 1) * P],
                                                    q3[:, part, bass.ds(blk, 1), :].rearrange("p a d -> p (a d)"),
                                                    start=(part == 0), stop=(part == 2))
                    last.then_inc(s_qe, 1)
                if staged and jj == 0:
                    pe.wait_ge(s_mv, NV * m + V_ALPHA)
                    pe.wait_ge(s_idx, 2 * m + 2)
                    nc.tensor.transpose(psM[0:R, 0:P], alm[:, :, :].rearrange("p h w -> p (h w)"), ident[:, :])
                    nc.tensor.transpose(psM[0:R, P:2 * P], stc[:, mpar, :, :].rearrange("p h w -> p (h w)"),
                                        ident[:, :]).then_inc(s_mp, 1)
                    pe.wait_ge(s_mv, NV * m + V_F1)
                    nc.tensor.matmul(psR[0:1, 0:R], F1[:, P - 1:P], ident[0:R, 0:R], start=True, stop=True).then_inc(s_mp, 1)
                if staged and jj == 1:
                    pe.wait_ge(s_mv, NV * m + V_INH)
                    nc.tensor.matmul(psR[0:R, 128:129], inh[:, :, :].rearrange("p h w -> p (h w)"), one[0:1, 0:1], start=True, stop=True).then_inc(s_mp, 1)
                    pe.wait_ge(s_mv, NV * m + V_B1)
                    nc.tensor.matmul(psR[0:1, 256:256 + R], B1[:, 0:1], ident[0:R, 0:R], start=True, stop=True).then_inc(s_mp, 1)
                if staged and jj == 2:
                    pe.wait_ge(s_mv, NV * m + V_IV)
                    nc.tensor.matmul(psR[0:R, 384:385], iv[:, :, :].rearrange("p h w -> p (h w)"), one[0:1, 0:1],
                                     start=True, stop=True).then_inc(s_mp, 1)
                    pe.wait_ge(s_mv, NV * m + V_G)
                    nc.tensor.transpose(psM[:, 256:256 + R], Gm[:, :], ident[0:R, 0:R]).then_inc(s_mp, 1)
                if staged and jj == 4:
                    pe.wait_ge(s_fx, m + 1)
                    nc.tensor.matmul(psM[0:BP, 400:400 + H], oh0[:, :], fx[:, :], start=True, stop=True).then_inc(s_mp, 1)
                if fresh and j < LAG or not fresh and isinstance(i, int) and j >= LAG:
                    return
                b = pair - LAG
                sj = (j - LAG) % SLOT_PAIRS
                pe.wait_ge(s_pv, b + 1)
                pe.wait_ge(s_oh, b + 1)
                if not (fresh and j < LAG + 2):
                    pe.wait_ge(s_acc, 2 * b - 2)
                for k in range(2):
                    last = nc.tensor.matmul(psA[sj % 2][k][0:BP, 0:H * HW_], oh[:, sj % 2, k, :], kv[:, 2 * sj + k, 0:H * HW_],
                                            start=True, stop=True)
                last.then_inc(s_agg, 1)

            walk(pe, at)

        @block.vector
        def _(dve):
            nc.vector.memset(acc[:, 0:12, :], 0.0).then_inc(s_set, 1)
            nc.vector.memset(acc[:, 12:NB, :], 0.0).then_inc(s_set, 1)
            nc.vector.memset(nrow[:, P:P + 1], 0.0).then_inc(s_set, 1)
            nc.vector.memset(tails[:, :, :], NEG).then_inc(s_set, 1)
            nc.vector.memset(heads[:, :, :], NEG).then_inc(s_set, 1)
            dve.wait_ge(s_set, 5)

            def build(half, cc, par):
                dve.wait_ge(s_bc[par], 16 * half + 16)
                nc.vector.tensor_scalar(ohT[par][:, :], ohT[par][:, :], iotaP[0:BP, 0:1], None, ALU.is_equal).then_inc(s_oht, 1)
                dve.wait_ge(s_oht, cc + 1)
                nc.vector.tensor_scalar(noh[:, par:par + 1], ohT[par][:, 0:1], -1.0, 1.0, ALU.mult, ALU.add).then_inc(s_noh, 1)

            build(0, 0, 0)

            def at(i, j, fresh):
                pair = SLOT_PAIRS * i + j
                cc, par, jj = 2 * i + j // CP, j // CP, j % CP
                m = cc - 1
                mpar = (par + 1) % 2
                mv = NV * m
                mp = NT * m
                staged = not (fresh and j < CP) and not (isinstance(m, int) and m >= C)

                def seen(step):
                    dve.wait_ge(s_mv, mv + step)

                if staged and jj == 0:
                    dve.wait_ge(s_alpha, CP * m + CP)
                    if not (fresh and j < 2 * CP):
                        seen(0)
                    nc.vector.tensor_tensor(alm[:, :, :], alpha[:, mpar, :, :],
                                            valN[:, bass.ds(W * m, W)].unsqueeze(1).broadcast_to([P, H, W]), ALU.add).then_inc(s_mv, 1)
                if staged and jj == 1:
                    dve.wait_ge(s_mp, mp + T_TAIL)
                    nc.vector.tensor_copy(tails[:, :, 1:W + 1], psR[0:1, 0:R].rearrange("p (h w) -> p h w", h=H)).then_inc(s_mv, 1)
                    seen(V_TAIL)
                    nc.vector.tensor_tensor_scan(out=carry[:, :, :].rearrange("p h w -> p (h w)"),
                                                 data0=keep["fwd"][:, bass.ds(m, 1), :, :].rearrange("p c h w -> p (c h w)"),
                                                 data1=tails[:, :, :].rearrange("p h w -> p (h w)"),
                                                 initial=NEG, op0=ALU.add, op1=ALU.max).then_inc(s_mv, 1)
                    seen(V_CARRY)
                    nc.vector.tensor_copy(inh[:, :, :], carry[:, :, 0:W]).then_inc(s_mv, 1)
                if staged and jj == 2:
                    dve.wait_ge(s_mp, mp + T_HEAD)
                    nc.vector.tensor_copy(heads[:, :, 0:W], psR[0:1, 256:256 + R].rearrange("p (h w) -> p h w", h=H)).then_inc(s_mv, 1)
                    seen(V_HEAD)
                    nc.vector.tensor_tensor_scan(out=back[:, :, :].rearrange("p h w -> p (h w)")[:, ::-1],
                                                 data0=keep["bwd"][:, bass.ds(m, 1), :, :].rearrange("p c h w -> p (c h w)"),
                                                 data1=heads[:, :, :].rearrange("p h w -> p (h w)")[:, ::-1],
                                                 initial=NEG, op0=ALU.add, op1=ALU.max).then_inc(s_mv, 1)
                    seen(V_BACK)
                    nc.vector.tensor_tensor(iv[:, :, :], back[:, :, 1:W + 1],
                                            keep["nxt"][:, bass.ds(m, 1), :, :].rearrange("p c h w -> p (c h) w"), ALU.add).then_inc(s_mv, 1)
                    nc.vector.tensor_tensor(fd[:, :], tails[:, :, 0], back[:, :, 0], ALU.subtract).then_inc(s_mv, 1)
                    seen(V_FD)
                    nc.vector.tensor_scalar(fm[:, :], fd[:, :], 0.0, None, ALU.min).then_inc(s_mv, 1)
                    nc.vector.tensor_copy(tails[:, :, 0], carry[:, :, W]).then_inc(s_mv, 1)
                    nc.vector.tensor_scalar(oh0[:, :], iotaF[0:1, 0:BP], dstR[0:1, bass.ds(W * m, 1)], None,
                                            ALU.is_equal).then_inc(s_mv, 1)
                if staged and jj == 3:
                    dve.wait_ge(s_mp, mp + T_OUT)
                    nc.vector.tensor_tensor(dif[:, :, :], alm[:, :, :], psM[:, 256:256 + R].rearrange("p (h w) -> p h w", h=H),
                                            ALU.subtract).then_inc(s_mv, 1)
                if scored(i):
                    dve.wait_ge(s_kv[j], 32 * i + 32)
                    dve.wait_ge(s_qe, pair + 1)
                    if not (fresh and j < 2):
                        dve.wait_ge(s_alpha, pair - 1)
                    nc.vector.tensor_tensor(prod[:, j % 2, :].rearrange("p (k d) -> p k d", k=2),
                                            psQ[j % 2][:, :].rearrange("p (k d) -> p k d", k=2),
                                            kv[:, 2 * j:2 * j + 2, 0:HID], ALU.mult).then_inc(s_prod, 1)
                if staged and jj == 0:
                    dve.wait_ge(s_mp, mp + T_IN)
                    dve.wait_ge(s_nrow, m + 1)
                    nc.vector.tensor_tensor_scan(out=F1[:, :], data0=nrow[:, 0:P], data1=psM[0:R, 0:P], initial=NEG,
                                                 op0=ALU.add, op1=ALU.max).then_inc(s_mv, 1)
                if staged and jj == 1:
                    dve.wait_ge(s_mp, mp + T_CARRY)
                    nc.vector.tensor_copy(cin[:, :], psR[0:R, 128:129]).then_inc(s_mv, 1)
                    seen(V_CIN)
                    nc.vector.tensor_tensor_scan(out=F2[:, :], data0=nrow[:, 0:P], data1=psM[0:R, 0:P], initial=cin[:, 0:1],
                                                 op0=ALU.add, op1=ALU.max).then_inc(s_mv, 1)
                    seen(V_F2)
                    nc.vector.tensor_tensor_scan(out=B1[:, ::-1], data0=nrow[:, 1:P + 1][:, ::-1], data1=F2[:, ::-1], initial=NEG,
                                                 op0=ALU.add, op1=ALU.max).then_inc(s_mv, 1)
                if staged and jj == 2:
                    dve.wait_ge(s_mp, mp + T_IV)
                    nc.vector.tensor_copy(bin_[:, :], psR[0:R, 384:385]).then_inc(s_mv, 1)
                    seen(V_BIN)
                    nc.vector.tensor_tensor_scan(out=Gm[:, ::-1], data0=nrow[:, 1:P + 1][:, ::-1], data1=F2[:, ::-1],
                                                 initial=bin_[:, 0:1], op0=ALU.add, op1=ALU.max).then_inc(s_mv, 1)
                if jj == CP - 2 and scored(i):
                    build(i + par, cc + 1, 1 - par)
                if not (fresh and j < LAG) and not (not fresh and isinstance(i, int) and j >= LAG):
                    b = pair - LAG
                    sj = (j - LAG) % SLOT_PAIRS
                    if not (fresh and j < LAG + 2):
                        dve.wait_ge(s_agg, b - 1)
                    nc.vector.tensor_tensor(oh[:, sj % 2, :, :], iotaF[:, 0:BP].unsqueeze(1).broadcast_to([P, 2, BP]),
                                            dstR[:, bass.ds(2 * b, 2)].unsqueeze(2).broadcast_to([P, 2, BP]),
                                            ALU.is_equal).then_inc(s_oh, 1)
                if staged and jj == 6:
                    seen(V_RESC)
                if not (fresh and j < LAG + 1):
                    b = pair - LAG - 1
                    sj = (j - LAG - 1) % SLOT_PAIRS
                    dve.wait_ge(s_agg, b + 1)
                    if not (fresh and j < LAG + 2):
                        dve.wait_ge(s_acc, 2 * b)
                    for k in range(2):
                        blk = nc.vector.value_load(brow[0:1, bass.ds(2 * b + k, 1)], min_val=0, max_val=NB - 1)
                        if k == 1:
                            dve.wait_ge(s_acc, 2 * b + 1)
                        row = acc[:, bass.ds(blk, 1), :].rearrange("p a d -> p (a d)")
                        nc.vector.tensor_tensor(row, row, psA[sj % 2][k][0:BP, 0:H * HW_], ALU.add).then_inc(s_acc, 1)
                if staged and jj == 5:
                    dve.wait_ge(s_mp, mp + T_FAC)
                    nc.vector.tensor_scalar(fac[:, :], psM[0:BP, 400:400 + H], noh[:, mpar:mpar + 1], None, ALU.add).then_inc(s_mv, 1)
                    blk = nc.vector.value_load(brow[0:1, bass.ds(W * m, 1)], min_val=0, max_val=NB - 1)
                    seen(V_FAC)
                    if not (fresh and j < LAG + 1):
                        dve.wait_ge(s_acc, 2 * (pair - LAG))
                    row = acc[:, bass.ds(blk, 1), :].rearrange("p a (h e) -> p (a h) e", h=H)
                    nc.vector.tensor_tensor(row, row, fac[:, :].unsqueeze(2).broadcast_to([BP, H, HW_]), ALU.mult).then_inc(s_mv, 1)
                if scored(i):
                    dve.wait_ge(s_prod, pair + 1)
                    nc.vector.tensor_reduce(alpha[:, par, :, 2 * jj:2 * jj + 2].rearrange("p h w -> p w h"),
                                            prod[:, j % 2, :].rearrange("p (k h d) -> p k h d", k=2, h=H), AX.X, ALU.add
                                            ).then_inc(s_alpha, 1)

            walk(dve, at)


def mlp(nc, ctx, io, keep):
    c = ExitStack()
    with c:
        def sb(name, shape, dt=F32):
            return c.enter_context(nc.sbuf_tensor(name, shape, dt))

        def pb(name, shape):
            return c.enter_context(nc.psum_tensor(name, shape, F32))

        def sem(name):
            return ctx.enter_context(nc.semaphore(name))

        ident, acc, x1, mv3 = keep["ident"], keep["acc"], keep["x1"], keep["mv3"]
        FC = FF // P
        w1 = sb("w1", [P, KC, FF])
        w2 = sb("w2", [P, FC, HID])
        b1r = sb("b1r", [FC, P])
        b1c = sb("b1c", [P, FC])
        g1b = sb("g1b", [BP, HID])
        be1 = sb("be1", [BP, HID])
        b2b = sb("b2b", [BP, HID])
        g2b = sb("g2b", [BP, HID])
        be2 = sb("be2", [BP, HID])
        rec = sb("recden", [BP, NB, H])
        den = sb("den", [BP, NB, H])
        res = sb("resin", [BP, GU, HID])
        xin = sb("xin", [BP, GU, HID])
        y = sb("y", [BP, GU, HID])
        z = sb("z", [BP, GU, HID])
        h = sb("h", [BP, GU, HID])
        hT = sb("hT", [P, KC, GN])
        gT = sb("gT", [P, FC, GN])
        st = sb("st1", [BP, GU, 6])
        mv = sb("mv1", [BP, GU, 2])
        ve = sb("ve1", [BP, 3, GU])
        rs = sb("rs1", [BP, 3, GU])
        mh = sb("mh1", [BP, GU])
        st2 = sb("st2", [BP, GU, 6])
        mv2 = sb("mv2", [BP, GU, 2])
        mvs = sb("mvs", [BP, GU, 2])

        psT = [pb(f"psT2{b}", [P, 512]) for b in range(2)]
        psF = [pb(f"psF{b}", [P, 512]) for b in range(3)]
        psO = [pb(f"psO{b}", [P, 512]) for b in range(2)]
        psB = pb("psB", [P, 512])

        s_w1, s_w2, s_row, s_half = sem("m_w1"), sem("m_w2"), sem("m_row"), sem("m_half")
        s_res, s_xin = sem("m_res"), sem("m_xin")
        s_den, s_resu, s_xinu = sem("m_den"), sem("m_resu"), sem("m_xinu")
        s_ln1, s_mv1, s_rs1, s_h, s_hb = sem("m_ln1"), sem("m_mv1"), sem("m_rs1"), sem("m_h"), sem("m_hb")
        s_ve1, s_ve2 = sem("m_ve1"), sem("m_ve2")
        s_tr, s_hT, s_ff, s_ge, s_fo = sem("m_tr"), sem("m_hT"), sem("m_ff"), sem("m_ge"), sem("m_fo")
        s_y, s_ln2, s_mv2, s_rs2, s_x1, s_mv3 = sem("m_y"), sem("m_ln2"), sem("m_mv2"), sem("m_rs2"), sem("m_x1"), sem("m_mv3")
        s_turn = [sem("m_turn_pool"), sem("m_turn_dve")]
        s_mvs = sem("m_mvs")
        s_bt, s_bc, s_st3, s_we = sem("m_bt"), sem("m_bc"), sem("m_st3"), sem("m_we")

        res_v = io["res"].rearrange("(g u p) d -> p g u d", p=BP, u=GU)
        x_v = io["x"].rearrange("(g u p) d -> p g u d", p=BP, u=GU)
        block = c.enter_context(nc.Block())

        @block.sync
        def _(sp):
            def group(g, fresh):
                if not fresh:
                    sp.wait_ge(s_resu, g)
                sp.dma_start(res[:, :, :], res_v[:, bass.ds(g, 1), :, :].rearrange("p g u d -> p (g u) d")).then_inc(s_res, 16)
                if not fresh:
                    sp.wait_ge(s_xinu, g)
                sp.dma_start(xin[:, :, :], x_v[:, bass.ds(g, 1), :, :].rearrange("p g u d -> p (g u) d")).then_inc(s_xin, 16)

            group(0, True)
            for t, a in ((g1b, "ln1_g"), (be1, "ln1_b"), (b2b, "b2"), (g2b, "ln2_g"), (be2, "ln2_b")):
                sp.dma_start(t[:, :], io["L0_gnn_" + a].partition_broadcast(BP)).then_inc(s_row, 16)
            sp.dma_start(b1r[:, :], io["L0_gnn_b1"].rearrange("(c p) -> c p", p=P)).then_inc(s_row, 16)
            sp.dma_start(w1[:, :, :], io["L0_gnn_W1"].rearrange("(k p) n -> p k n", p=P)).then_inc(s_w1, 16)
            sp.dma_start(w2[:, :, :], io["L0_gnn_W2"].rearrange("(k p) n -> p k n", p=P)).then_inc(s_w2, 16)
            with sp.Fori(1, G) as g:
                group(g, False)
            for l, n in enumerate(("W1", "W2", "Wo")):
                sp.dma_start(keep["we"][l][:, :, :, :], io["L0_ffn_" + n].rearrange("e (k p) n -> p e k n", p=P)).then_inc(s_we, 16)
            sp.wait_ge(s_we, 48)

        @block.gpsimd
        def _(pool):
            nc.gpsimd.memset(mh[:, :], -0.5).then_inc(s_half, 1)
            pool.wait_ge(s_half, 1)

            def root(g, k, m, s_m, s_v, s_r):
                pool.wait_ge(s_m, GU * g + GU)
                held(pool, s_turn[0])
                nc.gpsimd.tensor_scalar(ve[:, k, :], m[:, :, 1], LN_EPS, None, ALU.add).then_inc(s_v, 1)
                pool.wait_ge(s_v, g + 1)
                nc.gpsimd.tensor_tensor(rs[:, k, :], ve[:, k, :], mh[:, :], ALU.pow).then_inc(s_r, 1)

            root(0, 0, mv, s_mv1, s_ve1, s_rs1)
            with pool.Fori(0, G - 1) as g:
                root(g + 1, 0, mv, s_mv1, s_ve1, s_rs1)
                root(g, 1, mv2, s_mv2, s_ve2, s_rs2)
            root(G - 1, 1, mv2, s_mv2, s_ve2, s_rs2)

        @block.scalar
        def _(act):
            def columns(g):
                for u in range(GU):
                    act.wait_ge(s_tr, GU * g + u + 1)
                    nc.scalar.activation(hT[:, :, u * BP:(u + 1) * BP],
                                         psT[u % 2][:, 0:KC * BP].rearrange("p (k n) -> p k n", k=KC), ACT.Copy).then_inc(s_hT, 1)

            def gelu(g, fresh):
                if not fresh:
                    act.wait_ge(s_fo, GU * g)
                for n, (m, (a, b)) in enumerate((m, ab) for m in range(FC) for ab in HALVES):
                    act.wait_ge(s_ff, 2 * FC * g + n + 1)
                    nc.scalar.activation(gT[:, m, a:b], psF[n % 3][:, 0:b - a], ACT.Gelu, bias=b1c[:, m:m + 1]).then_inc(s_ge, 1)

            columns(0)
            act.wait_ge(s_bc, 1)
            gelu(0, True)
            with act.Fori(1, G) as g:
                columns(g)
                gelu(g, False)

        @block.tensor
        def _(pe):
            def columns(g, fresh):
                pe.wait_ge(s_h, g + 1)
                for u in range(GU):
                    if not (fresh and u < 2):
                        pe.wait_ge(s_hT, GU * g + max(u - 1, 0))
                    for k in range(KC):
                        last = nc.tensor.transpose(psT[u % 2][:, k * BP:(k + 1) * BP], h[:, u, k * P:(k + 1) * P],
                                                   ident[0:BP, 0:BP])
                    last.then_inc(s_tr, 1)

            def first(g, fresh):
                pe.wait_ge(s_hT, GU * g + GU)
                for n, (m, (a, b)) in enumerate((m, ab) for m in range(FC) for ab in HALVES):
                    if not (fresh and n < 3):
                        pe.wait_ge(s_ge, 2 * FC * g + n - 2)
                    for k in range(KC):
                        last = nc.tensor.matmul(psF[n % 3][:, 0:b - a], w1[:, k, m * P:(m + 1) * P], hT[:, k, a:b],
                                                start=(k == 0), stop=(k == KC - 1))
                    last.then_inc(s_ff, 1)

            def second(g, fresh):
                pe.wait_ge(s_ge, 2 * FC * g + 2 * FC)
                for u in range(GU):
                    if not (fresh and u < 2):
                        pe.wait_ge(s_y, GU * g + max(u - 1, 0))
                    for m in range(FC):
                        last = nc.tensor.matmul(psO[u % 2][0:BP, 0:HID], gT[:, m, u * BP:(u + 1) * BP], w2[:, m, :],
                                                start=(m == 0), stop=(m == FC - 1))
                    last.then_inc(s_fo, 1)

            pe.wait_ge(s_row, 96)
            nc.tensor.transpose(psB[:, 0:FC], b1r[:, :], ident[0:FC, 0:FC]).then_inc(s_bt, 1)
            columns(0, True)
            pe.wait_ge(s_w1, 16)
            first(0, True)
            pe.wait_ge(s_w2, 16)
            columns(1, False)
            second(0, True)
            with pe.Fori(1, G - 1) as g:
                first(g, False)
                columns(g + 1, False)
                second(g, False)
            first(G - 1, False)
            second(G - 1, False)

        @block.vector
        def _(dve):
            wide = acc[:, :, :].rearrange("p t (h e) -> p t h e", h=H)
            nc.vector.tensor_scalar(den[:, :, :], wide[:, :, :, D], 1e-16, None, ALU.add).then_inc(s_den, 1)
            dve.wait_ge(s_den, 1)
            nc.vector.reciprocal(rec[:, :, :], den[:, :, :]).then_inc(s_den, 1)
            dve.wait_ge(s_row, 96)
            dve.wait_ge(s_bt, 1)
            nc.vector.tensor_copy(b1c[:, :], psB[:, 0:FC]).then_inc(s_bc, 1)
            dve.wait_ge(s_den, 2)

            def rows(t):
                return t[:, :].unsqueeze(1).broadcast_to([BP, GU, HID])

            K1, K2 = 2 * GU + 2, GU + 3

            def norm1(g, fresh):
                for u in range(GU):
                    nc.vector.tensor_tensor(
                        y[:, u, :].rearrange("p (h d) -> p h d", h=H),
                        acc[:, bass.ds(GU * g + u, 1), :].rearrange("p t (h e) -> p (t h) e", h=H)[:, :, 0:D],
                        rec[:, bass.ds(GU * g + u, 1), :].rearrange("p t h -> p (t h)").unsqueeze(2).broadcast_to([BP, H, D]),
                        ALU.mult).then_inc(s_ln1, 1)
                dve.wait_ge(s_res, 16 * g + 16)
                dve.wait_ge(s_ln1, K1 * g + GU)
                nc.vector.tensor_tensor(y[:, :, :], y[:, :, :], res[:, :, :], ALU.add).then_inc(s_resu, 1)
                dve.wait_ge(s_resu, g + 1)
                for u in range(GU):
                    nc.vector.bn_stats(st[:, u, :], y[:, u, :]).then_inc(s_ln1, 1)
                dve.wait_ge(s_ln1, K1 * g + 2 * GU)
                held(dve, s_turn[1])
                for u in range(GU):
                    nc.vector.bn_aggr(mv[:, u, :], st[:, u, :]).then_inc(s_mv1, 1)
                dve.wait_ge(s_rs1, g + 1)
                for u in range(GU):
                    last = nc.vector.tensor_scalar(y[:, u, :], y[:, u, :], mv[:, u, 0:1], rs[:, 0, u:u + 1],
                                                   ALU.subtract, ALU.mult)
                last.then_inc(s_ln1, 1)
                dve.wait_ge(s_ln1, K1 * g + 2 * GU + 1)
                nc.vector.tensor_tensor(y[:, :, :], y[:, :, :], rows(g1b), ALU.mult).then_inc(s_ln1, 1)
                dve.wait_ge(s_ln1, K1 * g + 2 * GU + 2)
                if not fresh:
                    dve.wait_ge(s_tr, GU * g)
                nc.vector.tensor_tensor(h[:, :, :], y[:, :, :], rows(be1), ALU.add).then_inc(s_h, 1)
                dve.wait_ge(s_h, g + 1)
                nc.vector.tensor_tensor(x1[:, bass.ds(GU * g, GU), :], h[:, :, :], rows(b2b), ALU.add).then_inc(s_hb, 1)

            def norm2(g):
                dve.wait_ge(s_hb, g + 1)
                for u in range(GU):
                    dve.wait_ge(s_fo, GU * g + u + 1)
                    nc.vector.tensor_tensor(z[:, u, :], psO[u % 2][0:BP, 0:HID],
                                            x1[:, bass.ds(GU * g + u, 1), :].rearrange("p t d -> p (t d)"), ALU.add).then_inc(s_y, 1)
                for u in range(GU):
                    dve.wait_ge(s_y, GU * g + u + 1)
                    nc.vector.bn_stats(st2[:, u, :], z[:, u, :]).then_inc(s_ln2, 1)
                dve.wait_ge(s_ln2, K2 * g + GU)
                held(dve, s_turn[1])
                for u in range(GU):
                    nc.vector.bn_aggr(mv2[:, u, :], st2[:, u, :]).then_inc(s_mv2, 1)
                dve.wait_ge(s_rs2, g + 1)
                for u in range(GU):
                    last = nc.vector.tensor_scalar(z[:, u, :], z[:, u, :], mv2[:, u, 0:1], rs[:, 1, u:u + 1],
                                                   ALU.subtract, ALU.mult)
                last.then_inc(s_ln2, 1)
                dve.wait_ge(s_ln2, K2 * g + GU + 1)
                nc.vector.tensor_tensor(z[:, :, :], z[:, :, :], rows(g2b), ALU.mult).then_inc(s_ln2, 1)
                dve.wait_ge(s_ln2, K2 * g + GU + 2)
                nc.vector.tensor_tensor(z[:, :, :], z[:, :, :], rows(be2), ALU.add).then_inc(s_ln2, 1)
                dve.wait_ge(s_ln2, K2 * g + GU + 3)
                dve.wait_ge(s_xin, 16 * g + 16)
                nc.vector.tensor_tensor(x1[:, bass.ds(GU * g, GU), :], z[:, :, :], xin[:, :, :], ALU.add).then_inc(s_xinu, 1)
                dve.wait_ge(s_xinu, g + 1)
                held(dve, s_turn[1])
                for u in range(GU):
                    nc.vector.bn_stats(st2[:, u, :], x1[:, bass.ds(GU * g + u, 1), :].rearrange("p t d -> p (t d)")).then_inc(s_st3, 1)
                dve.wait_ge(s_st3, GU * g + GU)
                held(dve, s_turn[1])
                for u in range(GU):
                    nc.vector.bn_aggr(mvs[:, u, :], st2[:, u, :]).then_inc(s_mvs, 1)
                dve.wait_ge(s_mvs, GU * g + GU)
                nc.vector.tensor_copy(mv3[:, bass.ds(GU * g, GU), :], mvs[:, :, :]).then_inc(s_mv3, 1)

            norm1(0, True)
            with dve.Fori(0, G - 1) as g:
                norm1(g + 1, False)
                norm2(g)
            norm2(G - 1)


def experts(nc, ctx, io, keep):
    c = ExitStack()
    with c:
        def sb(name, shape, dt=F32):
            return c.enter_context(nc.sbuf_tensor(name, shape, dt))

        def pb(name, shape):
            return c.enter_context(nc.psum_tensor(name, shape, F32))

        def sem(name):
            return ctx.enter_context(nc.semaphore(name))

        ident, x1, mv3 = keep["ident"], keep["x1"], keep["mv3"]
        we = keep["we"]
        NP = 2 * NE
        prm = sb("prm", [NP, 10, P])
        sc = sb("sc", [NP, 4, P])
        tmp = sb("tmp", [NP, 2, P])
        hv = sb("hv", [NP, 2, P])
        scT = sb("scT", [P, 4, NP])
        wr = sb("wr", [P, KC, NE])
        br = sb("br", [BP, NE])
        bo = sb("bo", [NE, HID])
        ve3 = sb("ve3", [BP, NB])
        rs3 = sb("rs3", [BP, NB])
        mh3 = sb("mh3", [BP, NB])
        xg = sb("xg", [BP, GU, HID])
        xT = sb("xT", [P, KC, GN])
        lg = sb("lg", [BP, GU, NE])
        mx = sb("mx", [BP, GU])
        ex = sb("ex", [BP, GU, NE])
        sm = sb("sm", [BP, GU])
        wt = sb("wt", [BP, GU, NE])
        wT = sb("wT", [NE, GN])
        h1 = sb("h1", [P, 2, KC, GN])
        h2 = sb("h2", [P, 2, KC, GN])
        o = sb("o", [BP, GU, HID])

        psT = [pb(f"psT3{b}", [P, 512]) for b in range(2)]
        psF = [pb(f"psF3{b}", [P, 512]) for b in range(4)]
        psO = [pb(f"psO3{b}", [P, 512]) for b in range(2)]

        s_prm, s_wr, s_half = sem("e_prm"), sem("e_wr"), sem("e_half")
        s_ve, s_rs, s_sc, s_hv, s_scp, s_scT = sem("e_ve"), sem("e_rs"), sem("e_sc"), sem("e_hv"), sem("e_scp"), sem("e_scT")
        s_xg, s_tr, s_xT, s_lg = sem("e_xg"), sem("e_tr"), sem("e_xT"), sem("e_lg")
        s_sx, s_ex, s_wt, s_wtp, s_wT = sem("e_sx"), sem("e_ex"), sem("e_wt"), sem("e_wtp"), sem("e_wT")
        s_sm, s_tm = sem("e_sm"), sem("e_tm")
        s_f, s_r, s_l3, s_cb, s_out = sem("e_f"), sem("e_r"), sem("e_l3"), sem("e_cb"), sem("e_out")

        out_v = io["out"].rearrange("(g u p) d -> p g u d", p=BP, u=GU)
        jobs = [(1, 0)] + [j for e in range(NE) for j in (([(1, e + 1)] if e + 1 < NE else []) + [(2, e)])]
        NJ = len(jobs)
        JF = 4
        parts = [(m, a, b) for m in range(KC) for a, b in HALVES]
        IT = GU * (NE + 1)

        block = c.enter_context(nc.Block())

        @block.sync
        def _(sp):
            for k, n in enumerate(("b1", "g1", "be1", "m1", "v1", "b2", "g2", "be2", "m2", "v2")):
                sp.dma_start(prm[:, k, :], io["L0_ffn_" + n].rearrange("e (m p) -> (e m) p", p=P)).then_inc(s_prm, 16)
            sp.dma_start(wr[:, :, :], io["L0_ffn_Wr"].rearrange("(k p) e -> p k e", p=P)).then_inc(s_wr, 16)
            sp.dma_start(br[:, :], io["L0_ffn_br"].partition_broadcast(BP)).then_inc(s_wr, 16)
            sp.dma_start(bo[:, :], io["L0_ffn_bo"]).then_inc(s_wr, 16)
            with sp.Fori(0, G) as g:
                sp.wait_ge(s_cb, IT * g + IT)
                sp.dma_start(out_v[:, bass.ds(g, 1), :, :].rearrange("p g u d -> p (g u) d"), o[:, :, :]).then_inc(s_out, 16)
            sp.wait_ge(s_out, 16 * G)

        @block.gpsimd
        def _(pool):
            nc.gpsimd.memset(mh3[:, :], -0.5).then_inc(s_half, 1)
            nc.gpsimd.memset(hv[:, :, :], -0.5).then_inc(s_half, 1)
            nc.gpsimd.tensor_scalar(ve3[:, :], mv3[:, :, 1], LN_EPS, None, ALU.add).then_inc(s_ve, 1)
            pool.wait_ge(s_half, 2)
            pool.wait_ge(s_ve, 1)
            nc.gpsimd.tensor_tensor(rs3[:, :], ve3[:, :], mh3[:, :], ALU.pow).then_inc(s_rs, 1)
            pool.wait_ge(s_prm, 160)
            for l in range(2):
                nc.gpsimd.tensor_scalar(tmp[:, l, :], prm[:, 5 * l + 4, :], BN_EPS, None, ALU.add).then_inc(s_ve, 1)
            pool.wait_ge(s_ve, 3)
            nc.gpsimd.tensor_tensor(hv[:, :, :], tmp[:, :, :], hv[:, :, :], ALU.pow).then_inc(s_hv, 1)

        @block.scalar
        def _(act):
            def columns(g):
                for u in range(GU):
                    act.wait_ge(s_tr, GU * g + u + 1)
                    nc.scalar.activation(xT[:, :, u * BP:(u + 1) * BP],
                                         psT[u % 2][:, 0:KC * BP].rearrange("p (k n) -> p k n", k=KC), ACT.Copy).then_inc(s_xT, 1)

            def router(g):
                act.wait_ge(s_sx, 3 * g + 3)
                nc.scalar.activation(ex[:, :, :], lg[:, :, :], ACT.Exp).then_inc(s_ex, 1)

            def group(g, last_group):
                for q, (layer, e) in enumerate(jobs):
                    if q == 1:
                        router(g)
                    if q == NJ - 2 and not last_group:
                        columns(g + 1)
                    for n, (m, a, b) in enumerate(parts):
                        act.wait_ge(s_f, JF * NJ * g + JF * q + n + 1)
                        to = (h1 if layer == 1 else h2)[:, e % 2, m, a:b]
                        col = 2 * e + m
                        nc.scalar.activation(to, psF[n][:, 0:b - a], ACT.Relu, bias=scT[:, 2 * layer - 1, col:col + 1],
                                             scale=scT[:, 2 * layer - 2, col:col + 1]).then_inc(s_r, 1)

            columns(0)
            act.wait_ge(s_scT, 1)
            with act.Fori(0, G - 1) as g:
                group(g, False)
            group(G - 1, True)

        @block.tensor
        def _(pe):
            def columns(g):
                pe.wait_ge(s_xg, g + 1)
                for u in range(GU):
                    if u < 2 and not (isinstance(g, int) and g == 0):
                        pe.wait_ge(s_wT, 2 * g)
                    if u >= 2:
                        pe.wait_ge(s_xT, GU * g + u - 1)
                    for k in range(KC):
                        last = nc.tensor.transpose(psT[u % 2][:, k * BP:(k + 1) * BP], xg[:, u, k * P:(k + 1) * P],
                                                   ident[0:BP, 0:BP])
                    last.then_inc(s_tr, 1)

            def router(g):
                pe.wait_ge(s_xT, GU * g + GU)
                for u in range(GU):
                    for k in range(KC):
                        last = nc.tensor.matmul(psT[0][0:BP, 256 + u * NE:256 + (u + 1) * NE], xT[:, k, u * BP:(u + 1) * BP],
                                                wr[:, k, :], start=(k == 0), stop=(k == KC - 1))
                last.then_inc(s_lg, 1)

            def weights(g):
                pe.wait_ge(s_wt, g + 1)
                for b, us in ((0, (0, 1, 2)), (1, (3, 4))):
                    for n, u in enumerate(us):
                        last = nc.tensor.transpose(psT[b][0:NE, n * BP:(n + 1) * BP], wt[:, u, :], ident[0:BP, 0:BP])
                    last.then_inc(s_wtp, 1)

            def biases(g):
                pe.wait_ge(s_wT, 2 * g + 2)
                for u in range(GU):
                    if u < 2:
                        if not (isinstance(g, int) and g == 0):
                            pe.wait_ge(s_cb, IT * g)
                    else:
                        pe.wait_ge(s_cb, IT * g + u - 1)
                    nc.tensor.matmul(psO[u % 2][0:BP, 0:HID], wT[:, u * BP:(u + 1) * BP], bo[:, :], start=True, stop=True
                                     ).then_inc(s_l3, 1)

            def third(g, e):
                q = jobs.index((2, e))
                pe.wait_ge(s_r, JF * NJ * g + JF * q + JF)
                for u in range(GU):
                    n = GU * (e + 1) + u
                    pe.wait_ge(s_cb, IT * g + n - 1)
                    for k in range(KC):
                        last = nc.tensor.matmul(psO[n % 2][0:BP, 0:HID], h2[:, e % 2, k, u * BP:(u + 1) * BP],
                                                we[2][:, e, k, :], start=(k == 0), stop=(k == KC - 1))
                    last.then_inc(s_l3, 1)

            def group(g, fresh, last_group):
                for q, (layer, e) in enumerate(jobs):
                    if layer == 2 and e >= 1:
                        third(g, e - 1)
                    if layer == 2:
                        pe.wait_ge(s_r, JF * NJ * g + JF * jobs.index((1, e)) + JF)
                    for n, (m, a, b) in enumerate(parts):
                        if q or not fresh:
                            pe.wait_ge(s_r, JF * NJ * g + JF * (q - 1) + n + 1)
                        for k in range(KC):
                            x = xT[:, k, a:b] if layer == 1 else h1[:, e % 2, k, a:b]
                            last = nc.tensor.matmul(psF[n][:, 0:b - a], we[layer - 1][:, e, k, m * P:(m + 1) * P], x,
                                                    start=(k == 0), stop=(k == KC - 1))
                        last.then_inc(s_f, 1)
                    if q == 1:
                        weights(g)
                    if q == 2:
                        biases(g)
                    if (layer, e) == (1, NE - 1) and not last_group:
                        columns(g + 1)
                third(g, NE - 1)
                if not last_group:
                    router(g + 1)

            columns(0)
            pe.wait_ge(s_wr, 48)
            router(0)
            pe.wait_ge(s_sc, 6)
            for k in range(4):
                last = nc.tensor.transpose(psO[0][:, k * NP:(k + 1) * NP], sc[:, k, :], ident[0:NP, 0:NP])
            last.then_inc(s_scp, 1)
            pe.wait_ge(s_scT, 1)
            group(0, True, False)
            with pe.Fori(1, G - 1) as g:
                group(g, False, False)
            group(G - 1, False, True)

        @block.vector
        def _(dve):
            dve.wait_ge(s_rs, 1)

            def normal(g, fresh):
                if not fresh:
                    dve.wait_ge(s_tr, GU * g)
                for u in range(GU):
                    row = x1[:, bass.ds(GU * g + u, 1), :].rearrange("p t d -> p (t d)")
                    last = nc.vector.tensor_scalar(xg[:, u, :], row,
                                                   mv3[:, bass.ds(GU * g + u, 1), 0:1].rearrange("p t s -> p (t s)"),
                                                   rs3[:, bass.ds(GU * g + u, 1)], ALU.subtract, ALU.mult)
                last.then_inc(s_xg, 1)

            def softmax(g):
                dve.wait_ge(s_lg, g + 1)
                nc.vector.tensor_tensor(lg[:, :, :], psT[0][0:BP, 256:256 + GU * NE].rearrange("p (u e) -> p u e", u=GU),
                                        br[:, :].unsqueeze(1).broadcast_to([BP, GU, NE]), ALU.add).then_inc(s_sx, 1)
                dve.wait_ge(s_sx, 3 * g + 1)
                nc.vector.tensor_reduce(mx[:, :], lg[:, :, :], AX.X, ALU.max).then_inc(s_sx, 1)
                dve.wait_ge(s_sx, 3 * g + 2)
                nc.vector.tensor_tensor(lg[:, :, :], lg[:, :, :], mx[:, :].unsqueeze(2).broadcast_to([BP, GU, NE]),
                                        ALU.subtract).then_inc(s_sx, 1)
                dve.wait_ge(s_ex, g + 1)
                nc.vector.tensor_reduce(sm[:, :], ex[:, :, :], AX.X, ALU.add).then_inc(s_sm, 1)
                dve.wait_ge(s_sm, 2 * g + 1)
                nc.vector.reciprocal(mx[:, :], sm[:, :]).then_inc(s_sm, 1)
                dve.wait_ge(s_sm, 2 * g + 2)
                nc.vector.tensor_tensor(wt[:, :, :], ex[:, :, :], mx[:, :].unsqueeze(2).broadcast_to([BP, GU, NE]),
                                        ALU.mult).then_inc(s_wt, 1)
                dve.wait_ge(s_wtp, 2 * g + 1)
                nc.vector.tensor_copy(wT[:, 0:3 * BP], psT[0][0:NE, 0:3 * BP]).then_inc(s_wT, 1)
                dve.wait_ge(s_wtp, 2 * g + 2)
                nc.vector.tensor_copy(wT[:, 3 * BP:GN], psT[1][0:NE, 0:2 * BP]).then_inc(s_wT, 1)

            def sums(g, fresh):
                if not fresh:
                    dve.wait_ge(s_out, 16 * g)
                for n in range(IT):
                    u, e = n % GU, n // GU - 1
                    dve.wait_ge(s_l3, IT * g + n + 1)
                    ps = psO[n % 2][0:BP, 0:HID]
                    if e < 0:
                        nc.vector.tensor_tensor(o[:, u, :], ps, x1[:, bass.ds(GU * g + u, 1), :].rearrange("p t d -> p (t d)"),
                                                ALU.add).then_inc(s_cb, 1)
                    else:
                        dve.wait_ge(s_cb, IT * g + n + 1 - GU)
                        nc.vector.scalar_tensor_tensor(out=o[:, u, :], in0=ps, scalar=wt[:, u, e:e + 1], in1=o[:, u, :],
                                                       op0=ALU.mult, op1=ALU.add).then_inc(s_cb, 1)

            normal(0, True)
            dve.wait_ge(s_hv, 1)
            dve.wait_ge(s_prm, 160)
            for l in range(2):
                nc.vector.tensor_tensor(sc[:, 2 * l, :], prm[:, 5 * l + 1, :], hv[:, l, :], ALU.mult).then_inc(s_sc, 1)
                nc.vector.tensor_tensor(tmp[:, l, :], prm[:, 5 * l, :], prm[:, 5 * l + 3, :], ALU.subtract).then_inc(s_sc, 1)
            dve.wait_ge(s_sc, 4)
            for l in range(2):
                nc.vector.tensor_tensor(tmp[:, l, :], tmp[:, l, :], sc[:, 2 * l, :], ALU.mult).then_inc(s_tm, 1)
            dve.wait_ge(s_tm, 2)
            for l in range(2):
                nc.vector.tensor_tensor(sc[:, 2 * l + 1, :], tmp[:, l, :], prm[:, 5 * l + 2, :], ALU.add).then_inc(s_sc, 1)
            dve.wait_ge(s_scp, 1)
            nc.vector.tensor_copy(scT[:, :, :], psO[0][:, 0:4 * NP].rearrange("p (k n) -> p k n", k=4)).then_inc(s_scT, 1)
            dve.wait_ge(s_wr, 48)
            softmax(0)
            normal(1, False)
            sums(0, True)
            with dve.Fori(1, G - 1) as g:
                softmax(g)
                normal(g + 1, False)
                sums(g, False)
            softmax(G - 1)
            sums(G - 1, False)


def build(nc, io):
    io = dict(io)
    io["kv"] = nc.dram_tensor("kv_rows", [N, KVW], F32, kind="Internal").ap()
    io["res"] = nc.dram_tensor("residual", [N, HID], F32, kind="Internal").ap()
    io["rec"] = nc.dram_tensor("tile_records", [TILES, 3 * P], F32, kind="Internal").ap()
    io["drel"] = nc.dram_tensor("step_destinations", [STEPS, P], BF16, kind="Internal").ap()
    with ExitStack() as ctx:
        keep = {}

        def sb(stack, name, shape, dt=F32):
            keep[name] = stack.enter_context(nc.sbuf_tensor("k_" + name, shape, dt))

        sb(ctx, "ident", [P, P])
        sb(ctx, "iotaF", [P, P])
        sb(ctx, "iotaP", [P, 1])
        sb(ctx, "one", [1, 1])
        sb(ctx, "ones", [P, 1])
        sb(ctx, "acc", [BP, NB, H * HW_])
        with ExitStack() as graph:
            sb(graph, "q3", [BP, 3, NB, HID], BF16)
            sb(graph, "brow", [1, STEPS], I32)
            sb(graph, "srcI", [P, STEPS], I32)
            for n in ("dstR", "startN", "valN"):
                sb(graph, n, [P, STEPS])
            for n in ("fwd", "bwd"):
                sb(graph, n, [1, C, H, W + 1], BF16)
            sb(graph, "nxt", [1, C, H, W], BF16)
            project(nc, ctx, io, keep)
            attend(nc, ctx, io, keep)
        with ExitStack() as dense:
            sb(dense, "x1", [BP, NB, HID])
            sb(dense, "mv3", [BP, NB, 2])
            keep["we"] = [dense.enter_context(nc.sbuf_tensor(f"k_we{l}", [P, NE, KC, HID], F32)) for l in range(3)]
            mlp(nc, ctx, io, keep)
            experts(nc, ctx, io, keep)


_INS = ["x", "src", "dst"] + ["L0_gnn_" + n for n in (
    "Wq", "bq", "Wk", "bk", "Wv", "bv", "Wskip", "bskip", "ln1_g", "ln1_b", "W1", "b1", "W2", "b2", "ln2_g", "ln2_b")] + [
    "L0_ffn_" + n for n in ("Wr", "br", "W1", "b1", "g1", "be1", "m1", "v1", "W2", "b2", "g2", "be2", "m2", "v2", "Wo", "bo")]


def kernel(**inputs):
    import numpy as _np
    import concourse.bacc as _bacc
    from concourse import mybir as _mybir
    from concourse.bass_utils import run_bass_kernel_spmd as _run

    nc = _bacc.Bacc("TRN2", target_bir_lowering=False, num_devices=1)
    arrays, io = {}, {}
    for name in _INS:
        a = _np.ascontiguousarray(inputs[name])
        arrays[f"in_{name}"] = a
        io[name] = nc.dram_tensor(f"in_{name}", a.shape, _mybir.dt.from_np(a.dtype), kind="ExternalInput").ap()
    io["out"] = nc.dram_tensor("out_0", (N, HID), _mybir.dt.float32, kind="ExternalOutput").ap()
    build(nc, io)
    r = _run(nc, [arrays], core_ids=[0])
    return r.results[0]["out_0"]
```

```python
from contextlib import ExitStack

import concourse.bass as bass
from concourse import mybir

F32 = mybir.dt.float32
BF16 = mybir.dt.bfloat16
I32 = mybir.dt.int32
ALU = mybir.AluOpType
ACT = mybir.ActivationFunctionType
AX = mybir.AxisListType

P = 128
N, HID, E = 3125, 256, 53125
H, D = 4, 64
FF = 4 * HID
NB, BP = 25, 125
KC = HID // P
LT = 2
TL = LT * P
TILES = (E + TL - 1) // TL
TG, TP = 2, TILES // 2
STEPS = TILES + NB - 1
CP = 8
C = STEPS // CP
SG, SP_ = 2, STEPS // 2
W = LT * CP
CR = 4
RING = CR * CP
R = H * W
HW_ = D + 1
HALFW = H * HW_
KVW = 2 * HALFW
NEG = -1.0e30
FAR = 8192.0
PV_LAG = CP + 6
SUM_LAG = CP + 8
ADD_LAG = SUM_LAG + 1
NQ, NA, NO = 4, 2, 4
GU = 5
G = NB // GU
GN = GU * BP
HALF = 313
HALVES = [(0, HALF), (HALF, GN)]
NE = 8
LN_EPS = 1e-5
BN_EPS = 1e-3
SCALE = float(D) ** -0.5


def held(eng, turn):
    eng.sem_inc(turn, 1)


def project(nc, ctx, io, keep):
    c = ExitStack()
    with c:
        def sb(name, shape, dt=F32):
            return c.enter_context(nc.sbuf_tensor(name, shape, dt))

        def pb(name, shape):
            return c.enter_context(nc.psum_tensor(name, shape, F32))

        def sem(name):
            return ctx.enter_context(nc.semaphore(name))

        xs = sb("xs", [BP, NB, HID])
        wqk = sb("wqk", [P, KC, 2 * HID])
        wvs = sb("wvs", [P, KC, 2 * HID])
        bqk = sb("bqk", [BP, 2 * HID])
        bvs = sb("bvs", [BP, 2 * HID])
        st = sb("st", [BP, NB, 6])
        mv = sb("mv", [BP, NB, 2])
        ve = sb("ve", [BP, NB])
        mh = sb("mh", [BP, NB])
        rs = sb("rs", [BP, NB])
        xn = sb("xn", [BP, 2, HID])
        xnT = sb("xnT", [P, 2, KC, BP])
        q32 = sb("q32", [BP, 2, HID])
        r32 = sb("r32", [BP, 2, HID])
        kvst = sb("kvst", [BP, 2, KVW])
        resst = sb("resst", [BP, 2, HID])
        rest = sb("rest", [BP, 2, HID])
        dint = sb("dint", [TP, TG, TL], I32)
        sint = sb("sint", [TP, TG, TL], I32)
        pint = sb("pint", [TP, TG, 1], I32)
        pf = sb("pf", [TP, TG, 1])
        ne = sb("ne", [TP, TG, TL])
        rec = sb("rec", [TP, TG, 3 * TL])
        io25 = sb("io25", [TP, NB], I32)
        io25f = sb("io25f", [TP, NB])
        before = sb("before", [TP, TG, NB])
        ioS = sb("ioS", [NB, STEPS], I32)
        ioSf = sb("ioSf", [NB, STEPS])
        ioG = sb("ioG", [SP_, SG], I32)
        ioGf = sb("ioGf", [SP_, SG])
        first = sb("first", [NB, 1])
        begun = sb("begun", [NB, STEPS])
        bs = sb("bs", [SP_, SG])
        bm = sb("bm", [SP_, SG])
        tidx = sb("tidx", [SP_, SG], I32)
        grec = sb("grec", [SP_, SG, 3 * TL])
        drel = sb("drel", [SP_, SG, TL])
        drelb = sb("drelb", [SP_, SG, TL], BF16)
        mins = sb("mins", [SP_, 3, LT, SG])
        n0row = sb("n0row", [1, LT * STEPS + 1])
        pbrow = sb("pbrow", [1, LT * STEPS])
        v1 = sb("v1", [P, LT * STEPS])
        v2 = sb("v2", [P, LT * STEPS])
        iop = sb("iop", [P, 1], I32)
        iof = sb("iof", [P, P], I32)

        psW = [[pb(f"psW{b}{k}", [P, 512]) for k in range(2)] for b in range(2)]
        psT = [pb(f"psT{b}", [P, 512]) for b in range(2)]
        psX = [pb(f"psX{b}", [P, 512]) for b in range(2)]

        s_x, s_w, s_b = sem("s_x"), sem("s_w"), sem("s_b")
        s_ed, s_rec, s_grec = sem("s_ed"), sem("s_rec"), sem("s_grec")
        s_drel = sem("s_drel")
        s_kvo = [sem("s_kvo0"), sem("s_kvo1")]
        s_reso = [sem("s_reso0"), sem("s_reso1")]
        s_init, s_iota, s_const = sem("s_init"), sem("s_iota"), sem("s_const")
        s_tab, s_tabpe = sem("s_tab"), sem("s_tabpe")
        s_st, s_mv, s_ve, s_rs = sem("s_st"), sem("s_mv"), sem("s_ve"), sem("s_rs")
        s_xn, s_tr, s_xt, s_pr = sem("s_xn"), sem("s_tr"), sem("s_xt"), sem("s_pr")
        s_q, s_rest, s_row, s_pad = sem("s_q"), sem("s_rest"), sem("s_row"), sem("s_pad")
        s_qh, s_r1, s_qm, s_ql = sem("s_qh"), sem("s_r1"), sem("s_qm"), sem("s_ql")

        ident, iotaF, iotaP, one = keep["ident"], keep["iotaF"], keep["iotaP"], keep["one"]
        ones = keep["ones"]
        q3 = keep["q3"]
        x_v = io["x"].rearrange("(t p) d -> p t d", p=BP)
        kv_v = io["kv"].rearrange("(t p) d -> p t d", p=BP)
        res_v = io["res"].rearrange("(t p) d -> p t d", p=BP)
        rec_v = io["rec"].rearrange("(g p) d -> p g d", p=TP)
        drel_v = io["drel"].rearrange("(g p) d -> p g d", p=SP_)
        dst, src = io["dst"], io["src"]
        FULL = TP * TL
        LAST = (TILES - 1) * TL

        block = c.enter_context(nc.Block())

        @block.sync
        def _(sp):
            sp.wait_ge(s_init, 3)
            for t, a in ((dint, dst), (sint, src)):
                sp.dma_start(t[:, 0, :], a[0:FULL].rearrange("(p l) -> p l", l=TL)).then_inc(s_ed, 16)
                sp.dma_start(t[0:TP - 1, 1, :], a[FULL:LAST].rearrange("(p l) -> p l", l=TL)).then_inc(s_ed, 16)
                sp.dma_start(t[TP - 1:TP, 1, 0:E - LAST], a[LAST:E].rearrange("(p l) -> p l", p=1)).then_inc(s_ed, 16)
            lasts = dst[0:LAST].rearrange("(t l) -> t l", l=TL)[:, TL - 1:TL]
            with nc.allow_non_contiguous_dma(reason="one word per edge tile"):
                sp.dma_start(pint[1:TP, 0, :], lasts[0:TP - 1, :]).then_inc(s_ed, 16)
                for g in range(1, TG):
                    sp.dma_start(pint[0:TP, g, :], lasts[g * TP - 1:(g + 1) * TP - 1, :]).then_inc(s_ed, 16)
            sp.dma_start(xs[:, :, :], x_v).then_inc(s_x, 16)
            for w, a, b in ((wqk, "L0_gnn_Wq", "L0_gnn_Wk"), (wvs, "L0_gnn_Wv", "L0_gnn_Wskip")):
                sp.dma_start(w[:, :, 0:HID], io[a].rearrange("(k p) n -> p k n", p=P)).then_inc(s_w, 16)
                sp.dma_start(w[:, :, HID:2 * HID], io[b].rearrange("(k p) n -> p k n", p=P)).then_inc(s_w, 16)
            for t, a, b in ((bqk, "L0_gnn_bq", "L0_gnn_bk"), (bvs, "L0_gnn_bv", "L0_gnn_bskip")):
                sp.dma_start(t[:, 0:HID], io[a].partition_broadcast(BP)).then_inc(s_b, 16)
                sp.dma_start(t[:, HID:2 * HID], io[b].partition_broadcast(BP)).then_inc(s_b, 16)
            sp.wait_ge(s_tab, 6)
            sp.dma_start(rec_v, rec[:, :, :]).then_inc(s_rec, 16)

            def store(t, b):
                sp.wait_ge(s_row, t + 1)
                sp.dma_start(kv_v[:, t, :], kvst[:, b, :]).then_inc(s_kvo[b], 16)
                sp.dma_start(res_v[:, t, :], resst[:, b, :]).then_inc(s_reso[b], 16)

            with sp.Fori(0, NB - 1, 2) as t:
                store(t, 0)
                store(t + 1, 1)
            store(NB - 1, 0)
            sp.wait_ge(s_tab, 18)
            sp.dma_start(drel_v, drelb[:, :, :]).then_inc(s_drel, 16)
            sp.wait_ge(s_drel, 16)
            for b in range(2):
                sp.wait_ge(s_kvo[b], 16 * ((NB + 1 - b) // 2))
                sp.wait_ge(s_reso[b], 16 * ((NB + 1 - b) // 2))

        @block.gpsimd
        def _(pool):
            nc.gpsimd.memset(dint[:, :, :], int(FAR)).then_inc(s_init, 1)
            nc.gpsimd.memset(sint[:, :, :], 0).then_inc(s_init, 1)
            nc.gpsimd.memset(pint[:, :, :], -1).then_inc(s_init, 1)
            nc.gpsimd.iota(io25[:, :], pattern=[[BP, NB]], base=0, channel_multiplier=0).then_inc(s_iota, 1)
            nc.gpsimd.iota(ioS[:, :], pattern=[[1, STEPS]], base=0, channel_multiplier=0).then_inc(s_iota, 1)
            nc.gpsimd.iota(ioG[:, :], pattern=[[SP_, SG]], base=0, channel_multiplier=1).then_inc(s_iota, 1)
            nc.gpsimd.iota(iop[:, :], pattern=[[0, 1]], base=0, channel_multiplier=1).then_inc(s_iota, 1)
            nc.gpsimd.iota(iof[:, :], pattern=[[1, P]], base=0, channel_multiplier=0).then_inc(s_iota, 1)
            nc.gpsimd.memset(mh[:, :], -0.5).then_inc(s_pad, 1)
            nc.gpsimd.memset(kvst[:, :, :], 0.0).then_inc(s_pad, 1)
            pool.wait_ge(s_pad, 1)
            pool.wait_ge(s_mv, NB)
            nc.gpsimd.tensor_scalar(ve[:, :], mv[:, :, 1], LN_EPS, None, ALU.add).then_inc(s_ve, 1)
            pool.wait_ge(s_ve, 1)
            nc.gpsimd.tensor_tensor(rs[:, :], ve[:, :], mh[:, :], ALU.pow).then_inc(s_rs, 1)
            pool.wait_ge(s_tab, 15)
            pool.wait_ge(s_rec, 16)
            for g in range(SG):
                nc.gpsimd.indirect_dma_start(
                    out=grec[:, g, :], out_offset=None, in_=io["rec"],
                    in_offset=bass.IndirectOffsetOnAxis(ap=tidx[:, g:g + 1], axis=0)).then_inc(s_grec, 16)

            def split(t, b, first_use):
                pool.wait_ge(s_qh, t + 1)
                nc.gpsimd.tensor_tensor(r32[:, b, :], q32[:, b, :], q3[:, 0, bass.ds(t, 1), :].rearrange("p a d -> p (a d)"),
                                        ALU.subtract).then_inc(s_r1, 1)
                pool.wait_ge(s_qm, t + 1)
                nc.gpsimd.tensor_tensor(q3[:, 2, bass.ds(t, 1), :].rearrange("p a d -> p (a d)"), r32[:, b, :],
                                        q3[:, 1, bass.ds(t, 1), :].rearrange("p a d -> p (a d)"),
                                        ALU.subtract).then_inc(s_ql, 1)

            with pool.Fori(0, NB - 1, 2) as t:
                split(t, 0, False)
                split(t + 1, 1, False)
            split(NB - 1, 0, False)

        @block.scalar
        def _(act):
            def part(t, b):
                act.wait_ge(s_tr, t + 1)
                nc.scalar.activation(xnT[:, b, :, :], psT[b][:, 0:KC * BP].rearrange("p (k n) -> p k n", k=KC),
                                     ACT.Copy).then_inc(s_xt, 1)

            def high(t, b):
                act.wait_ge(s_q, t + 1)
                nc.scalar.activation(q3[:, 0, bass.ds(t, 1), :].rearrange("p a d -> p (a d)"), q32[:, b, :],
                                     ACT.Copy).then_inc(s_qh, 1)

            def middle(t, b):
                act.wait_ge(s_r1, t + 1)
                nc.scalar.activation(q3[:, 1, bass.ds(t, 1), :].rearrange("p a d -> p (a d)"), r32[:, b, :],
                                     ACT.Copy).then_inc(s_qm, 1)

            part(0, 0)
            with act.Fori(0, NB - 1, 2) as t:
                part(t + 1, 1)
                high(t, 0)
                middle(t, 0)
                part(t + 2, 0)
                high(t + 1, 1)
                middle(t + 1, 1)
            high(NB - 1, 0)
            middle(NB - 1, 0)

        @block.tensor
        def _(pe):
            pe.wait_ge(s_const, 4)
            pe.wait_ge(s_tab, 7)
            for g in range(TG):
                last = nc.tensor.matmul(psX[0][0:NB, 0:1], before[:, g, :], ones[0:TP, 0:1], start=(g == 0), stop=(g == TG - 1))
            last.then_inc(s_tabpe, 1)
            pe.wait_ge(s_tab, 9)
            for g in range(SG):
                nc.tensor.matmul(psX[1][0:SP_, g:g + 1], begun[:, g * SP_:(g + 1) * SP_], ones[0:NB, 0:1], start=True, stop=True)
            nc.tensor.matmul(psX[0][0:1, 0:STEPS], ones[0:NB, 0:1], begun[:, :], start=True, stop=True).then_inc(s_tabpe, 1)

            pe.wait_ge(s_w, 64)

            def rows(t, b):
                pe.wait_ge(s_xn, t + 1)
                for k in range(KC):
                    last = nc.tensor.transpose(psT[b][:, k * BP:(k + 1) * BP], xn[:, b, k * P:(k + 1) * P],
                                               ident[0:BP, 0:BP])
                last.then_inc(s_tr, 1)

            def products(t, b, fresh):
                pe.wait_ge(s_xt, t + 1)
                if not fresh:
                    pe.wait_ge(s_row, t - 1)
                for w, ps in ((wqk, psW[b][0]), (wvs, psW[b][1])):
                    for k in range(KC):
                        last = nc.tensor.matmul(ps[0:BP, :], xnT[:, b, k, :], w[:, k, :], start=(k == 0), stop=(k == KC - 1))
                last.then_inc(s_pr, 1)

            rows(0, 0)
            rows(1, 1)
            products(0, 0, True)
            rows(2, 0)
            products(1, 1, True)
            with pe.Fori(2, NB - 1, 2) as t:
                rows(t + 1, 1)
                products(t, 0, False)
                rows(t + 2, 0)
                products(t + 1, 1, False)
            products(NB - 1, 0, False)

            pe.wait_ge(s_tab, 24)
            pe.wait_ge(s_row, NB)
            for k, ps in ((0, psW[0][0]), (1, psW[0][1]), (2, psW[1][0])):
                for l in range(LT):
                    for g in range(SG):
                        a = drel[:, g, l * P:(l + 1) * P] if k == 1 else grec[:, g, k * TL + l * P:k * TL + (l + 1) * P]
                        at = l * STEPS + g * SP_
                        nc.tensor.transpose(ps[:, at:at + SP_], a, ident[0:SP_, 0:SP_])
            for k, ps in ((0, psT[0]), (1, psT[1]), (2, psW[1][1])):
                for l in range(LT):
                    for g in range(SG):
                        at = l * STEPS + g * SP_
                        last = nc.tensor.matmul(ps[0:1, at:at + SP_], mins[:, k, l, g:g + 1], ident[0:SP_, 0:SP_],
                                                start=True, stop=True)
            last.then_inc(s_tabpe, 1)

        @block.vector
        def _(dve):
            dve.wait_ge(s_iota, 5)
            nc.vector.tensor_copy(iotaP[:, :], iop[:, :]).then_inc(s_const, 1)
            nc.vector.tensor_copy(iotaF[:, :], iof[:, :]).then_inc(s_const, 1)
            nc.vector.memset(ones[:, :], 1.0).then_inc(s_const, 1)
            dve.wait_ge(s_const, 3)
            nc.vector.tensor_scalar(ident[:, :], iotaF[:, :], iotaP[:, 0:1], None, ALU.is_equal).then_inc(s_const, 1)
            dve.wait_ge(s_ed, 128)
            nc.vector.tensor_copy(rec[:, :, 0:TL], sint[:, :, :]).then_inc(s_tab, 1)
            nc.vector.tensor_copy(rec[:, :, TL:2 * TL], dint[:, :, :]).then_inc(s_tab, 1)
            nc.vector.tensor_copy(pf[:, :, :], pint[:, :, :]).then_inc(s_tab, 1)
            dve.wait_ge(s_tab, 3)
            nc.vector.tensor_tensor(ne[:, :, 1:TL], rec[:, :, TL + 1:2 * TL], rec[:, :, TL:2 * TL - 1], ALU.not_equal).then_inc(s_tab, 1)
            nc.vector.tensor_tensor(ne[:, :, 0:1], rec[:, :, TL:TL + 1], pf[:, :, :], ALU.not_equal).then_inc(s_tab, 1)
            dve.wait_ge(s_tab, 5)
            nc.vector.tensor_scalar(rec[:, :, 2 * TL:3 * TL], ne[:, :, :], NEG, None, ALU.mult).then_inc(s_tab, 1)
            nc.vector.tensor_copy(io25f[:, :], io25[:, :]).then_inc(s_const, 1)
            nc.vector.tensor_copy(ioSf[:, :], ioS[:, :]).then_inc(s_const, 1)
            nc.vector.tensor_copy(ioGf[:, :], ioG[:, :]).then_inc(s_const, 1)
            dve.wait_ge(s_const, 7)
            nc.vector.tensor_tensor(before[:, :, :], io25f[:, :].unsqueeze(1).broadcast_to([TP, TG, NB]),
                                    rec[:, :, 2 * TL - 1:2 * TL].broadcast_to([TP, TG, NB]), ALU.is_gt).then_inc(s_tab, 1)
            dve.wait_ge(s_tabpe, 1)
            nc.vector.tensor_tensor(first[:, :], psX[0][0:NB, 0:1], iotaP[0:NB, :], ALU.add).then_inc(s_tab, 1)
            dve.wait_ge(s_tab, 8)
            nc.vector.tensor_scalar(begun[:, :], ioSf[:, :], first[:, 0:1], None, ALU.is_ge).then_inc(s_tab, 1)
            dve.wait_ge(s_tabpe, 2)
            nc.vector.tensor_scalar(bs[:, :], psX[1][0:SP_, 0:SG], -1.0, None, ALU.add).then_inc(s_tab, 1)
            nc.vector.tensor_scalar(keep["brow"][:, :], psX[0][0:1, 0:STEPS], -1.0, None, ALU.add).then_inc(s_tab, 1)
            dve.wait_ge(s_tab, 11)
            nc.vector.tensor_tensor(tidx[:, :], ioGf[:, :], bs[:, :], ALU.subtract).then_inc(s_tab, 1)
            nc.vector.tensor_scalar(bm[:, :], bs[:, :], -float(BP), None, ALU.mult).then_inc(s_tab, 1)
            nc.vector.memset(n0row[:, :], NEG).then_inc(s_tab, 1)
            nc.vector.memset(one[:, :], 1.0).then_inc(s_tab, 1)

            dve.wait_ge(s_x, 16)
            with dve.Fori(0, NB) as t:
                nc.vector.bn_stats(st[:, t, :], xs[:, t, :]).then_inc(s_st, 1)
            dve.wait_ge(s_st, NB)
            for t in range(NB):
                nc.vector.bn_aggr(mv[:, t, :], st[:, t, :]).then_inc(s_mv, 1)
            dve.wait_ge(s_b, 64)
            dve.wait_ge(s_pad, 2)
            dve.wait_ge(s_rs, 1)

            def norm(t, b):
                nc.vector.tensor_scalar(xn[:, b, :], xs[:, t, :], mv[:, t, 0:1], rs[:, bass.ds(t, 1)],
                                        ALU.subtract, ALU.mult).then_inc(s_xn, 1)

            def rows(t, b, fresh):
                dve.wait_ge(s_pr, t + 1)
                if not fresh:
                    dve.wait_ge(s_r1, t - 1)
                    if b == 0:
                        dve.wait_ge(s_kvo[0], 8 * t)
                        dve.wait_ge(s_reso[0], 8 * t)
                    else:
                        dve.wait_ge(s_kvo[1], 8 * t - 8)
                        dve.wait_ge(s_reso[1], 8 * t - 8)
                nc.vector.tensor_tensor(rest[:, b, :], psW[b][1][0:BP, HID:2 * HID], xn[:, b, :], ALU.add).then_inc(s_rest, 1)
                nc.vector.tensor_tensor(q32[:, b, :], psW[b][0][0:BP, 0:HID], bqk[:, 0:HID], ALU.add).then_inc(s_q, 1)
                nc.vector.tensor_tensor(kvst[:, b, HALFW:HALFW + HID], psW[b][0][0:BP, HID:2 * HID], bqk[:, HID:2 * HID], ALU.add)
                nc.vector.tensor_tensor(kvst[:, b, 0:HALFW].rearrange("p (h e) -> p h e", h=H)[:, :, 0:D],
                                        psW[b][1][0:BP, 0:HID].rearrange("p (h d) -> p h d", h=H),
                                        bvs[:, 0:HID].rearrange("p (h d) -> p h d", h=H), ALU.add)
                dve.wait_ge(s_rest, t + 1)
                nc.vector.tensor_tensor(resst[:, b, :], rest[:, b, :], bvs[:, HID:2 * HID], ALU.add).then_inc(s_row, 1)

            norm(0, 0)
            norm(1, 1)
            rows(0, 0, True)
            norm(2, 0)
            rows(1, 1, True)
            norm(3, 1)
            with dve.Fori(2, NB - 3, 2) as t:
                rows(t, 0, False)
                norm(t + 2, 0)
                rows(t + 1, 1, False)
                norm(t + 3, 1)
            rows(NB - 3, 0, False)
            norm(NB - 1, 0)
            rows(NB - 2, 1, False)
            rows(NB - 1, 0, False)

            dve.wait_ge(s_grec, 16 * SG)
            dve.wait_ge(s_tab, 15)
            for g in range(SG):
                nc.vector.tensor_scalar(drel[:, g, :], grec[:, g, TL:2 * TL], bm[:, g:g + 1], None, ALU.add).then_inc(s_tab, 1)
            dve.wait_ge(s_tab, 17)
            nc.vector.tensor_copy(drelb[:, :, :], drel[:, :, :]).then_inc(s_tab, 1)
            for l in range(LT):
                at = 2 * TL + l * P
                nc.vector.tensor_reduce(mins[:, 0, l, :], grec[:, :, at:at + P], AX.X, ALU.min).then_inc(s_tab, 1)
                nc.vector.tensor_reduce(mins[:, 1, l, :], grec[:, :, at + 1:at + P], AX.X, ALU.min).then_inc(s_tab, 1)
                nc.vector.tensor_copy(mins[:, 2, l, :], grec[:, :, at]).then_inc(s_tab, 1)
            nc.vector.memset(keep["fwd"][:, :, :, :], NEG).then_inc(s_tab, 1)
            nc.vector.memset(keep["bwd"][:, :, :, :], NEG).then_inc(s_tab, 1)
            dve.wait_ge(s_tabpe, 3)

            def by_step(row):
                return row.rearrange("p (s l) -> p l s", l=LT)

            def as_made(ps, n):
                return ps[0:n, 0:LT * STEPS].rearrange("p (l s) -> p l s", l=LT)

            nc.vector.tensor_copy(by_step(keep["srcI"][:, :]), as_made(psW[0][0], P))
            nc.vector.tensor_copy(by_step(keep["dstR"][:, :]), as_made(psW[0][1], P))
            nc.vector.tensor_copy(by_step(keep["startN"][:, :]), as_made(psW[1][0], P))
            nc.vector.tensor_scalar(by_step(v1[:, :]), as_made(psW[0][1], P), 0.0, NEG, ALU.is_lt, ALU.mult).then_inc(s_tab, 1)
            nc.vector.tensor_scalar(by_step(v2[:, :]), as_made(psW[0][1], P), BP - 1.0, NEG, ALU.is_gt, ALU.mult).then_inc(s_tab, 1)
            nc.vector.tensor_copy(by_step(n0row[:, 0:LT * STEPS]), as_made(psW[1][1], 1)).then_inc(s_tab, 1)
            nc.vector.tensor_copy(by_step(pbrow[:, :]), as_made(psT[1], 1)).then_inc(s_tab, 1)
            dve.wait_ge(s_tab, 30)
            nc.vector.tensor_tensor(keep["valN"][:, :], v1[:, :], v2[:, :], ALU.add)
            nxt = n0row[:, 1:LT * STEPS + 1].rearrange("p (c w) -> p c w", w=W)
            pasts = pbrow[:, :].rearrange("p (c w) -> p c w", w=W)
            for h in range(H):
                for l in range(LT):
                    nc.vector.tensor_copy(keep["fwd"][:, :, h, 1 + l:W + 1:LT],
                                          psT[0][0:1, l * STEPS:(l + 1) * STEPS].rearrange("p (c j) -> p c j", c=C))
                nc.vector.tensor_tensor(keep["bwd"][:, :, h, 1:W + 1], pasts[:, :, ::-1], nxt[:, :, ::-1], ALU.add)
                nc.vector.tensor_copy(keep["nxt"][:, :, h, :], nxt)


(V_ALPHA, V_F1, V_TAIL, V_CARRY, V_INH, V_CIN, V_F2, V_B1, V_HEAD, V_BACK, V_IV, V_FD, V_FMIN, V_NEXT, V_OH0, V_BIN, V_G,
 V_DIFF, V_FAC) = range(1, 20)
NV = 19
(T_IN, T_TAIL, T_CARRY, T_HEAD, T_IV, T_OUT, T_FAC) = range(1, 8)
NT = 7


def attend(nc, ctx, io, keep):
    c = ExitStack()
    with c:
        def sb(name, shape, dt=F32):
            return c.enter_context(nc.sbuf_tensor(name, shape, dt))

        def pb(name, shape):
            return c.enter_context(nc.psum_tensor(name, shape, F32))

        def sem(name):
            return ctx.enter_context(nc.semaphore(name))

        ident, iotaF, iotaP, one = keep["ident"], keep["iotaF"], keep["iotaP"], keep["one"]
        q3, acc, brow = keep["q3"], keep["acc"], keep["brow"]
        dstR, valN = keep["dstR"], keep["valN"]

        ring = sb("ring", [P, W, CR + 1, HALFW])
        idx = sb("idx", [P, 2, W], I32)
        stc = sb("stc", [P, 2, H, W])
        ohT = [sb(f"ohT{b}", [BP, W * P], BF16) for b in range(2)]
        noh = sb("noh", [BP, CR])
        oh = sb("oh", [P, NO, LT, BP])
        oh0 = sb("oh0", [1, BP])
        prod = sb("prod", [P, 2, LT * HID])
        alpha = sb("alpha", [P, 2, H, W])
        alm = sb("alm", [P, H, W])
        dif = sb("dif", [P, H, W])
        nrow = sb("nrow", [R, P + 1])
        F1 = sb("F1", [R, P])
        F2 = sb("F2", [R, P])
        B1 = sb("B1", [R, P])
        Gm = sb("Gm", [R, P])
        cin = sb("cin", [R, 1])
        bin_ = sb("bin_", [R, 1])
        tails = sb("tails", [1, H, W + 1])
        heads = sb("heads", [1, H, W + 1])
        carry = sb("carry", [1, H, W + 1])
        back = sb("back", [1, H, W + 1])
        iv = sb("iv", [1, H, W])
        inh = sb("inh", [1, H, W])
        fd = sb("fd", [1, H])
        fm = sb("fm", [1, H])
        fx = sb("fx", [1, H])
        fac = sb("fac", [BP, H])

        psQ = [pb(f"psQ{b}", [P, 512]) for b in range(NQ)]
        psA = [pb(f"psA{b}", [P, 512]) for b in range(NA)]
        psM = pb("psM", [P, 512])
        psR = pb("psR", [P, 512])

        s_set = sem("s_set")
        s_turn = [sem("s_turn_sp"), sem("s_turn_pool"), sem("s_turn_pe")]
        s_idx = sem("s_idx")
        s_kv = [sem(f"s_kv{k}") for k in range(RING)]
        s_bc = [sem(f"s_bc{b}") for b in range(2)]
        s_oht, s_noh = sem("s_oht"), sem("s_noh")
        s_qe, s_prod, s_alpha = sem("s_qe"), sem("s_prod"), sem("s_alpha")
        s_mv, s_mp = sem("s_maxv"), sem("s_maxp")
        s_nrow, s_exp, s_fx, s_resc = sem("s_nrow"), sem("s_exp"), sem("s_fx"), sem("s_rescaled")
        s_pv, s_oh, s_agg, s_acc = sem("s_pv"), sem("s_oh"), sem("s_agg"), sem("s_acc")

        drel_row = io["drel"].rearrange("s l -> (s l)")
        block = c.enter_context(nc.Block())

        ROUNDS = STEPS // RING

        def walk(eng, at):
            for j in range(RING):
                at(0, j, True)
            with eng.Fori(1, ROUNDS) as i:
                for j in range(RING):
                    at(i, j, False)
            for place in range(RING * ROUNDS, STEPS + ADD_LAG):
                at(place // RING, place % RING, False)

        def live(i, j, fresh, lag=0):
            if fresh:
                return j >= lag
            return not isinstance(i, int) or RING * i + j - lag < STEPS

        def staged(i, j, fresh):
            return live(i, j - j % CP, fresh, CP)

        @block.sync
        def _(sp):
            def fetch(cc, par, fresh):
                if not fresh:
                    sp.wait_ge(s_qe, CP * (cc - 1))
                    held(sp, s_turn[0])
                    sp.wait_ge(s_noh, cc - 1)
                    held(sp, s_turn[0])
                sp.dma_start(ohT[par][:, :], drel_row[bass.ds(cc * (W * P), W * P)].partition_broadcast(BP)
                             ).then_inc(s_bc[par], 16)

            for cc in range(CR):
                fetch(cc, cc % 2, cc < 2)
            with sp.Fori(1, ROUNDS) as i:
                for par in range(CR):
                    fetch(CR * i + par, par % 2, False)
            for cc in range(CR * ROUNDS, C):
                fetch(cc, cc % 2, False)

        @block.gpsimd
        def _(pool):
            def at(i, j, fresh):
                if not live(i, j, fresh):
                    return
                step = RING * i + j
                cc, par = CR * i + j // CP, j // CP % 2
                if j % CP == 0:
                    if not (fresh and j < 2 * CP):
                        pool.wait_ge(s_alpha, CP * (cc - 1))
                        held(pool, s_turn[1])
                        pool.wait_ge(s_mp, NT * (cc - 2) + T_IN)
                        held(pool, s_turn[1])
                    nc.gpsimd.tensor_copy(idx[:, par, :], keep["srcI"][:, bass.ds(W * cc, W)]).then_inc(s_idx, 1)
                    nc.gpsimd.tensor_copy(stc[:, par, :, :], keep["startN"][:, bass.ds(W * cc, W)].unsqueeze(1)
                                          .broadcast_to([P, H, W])).then_inc(s_idx, 1)
                    pool.wait_ge(s_idx, 2 * cc + 2)
                    held(pool, s_turn[1])
                if not (fresh and j < CP):
                    pool.wait_ge(s_prod, step - CP + 1)
                    held(pool, s_turn[1])
                if not (fresh and j < RING - CP):
                    pool.wait_ge(s_agg, step - (RING - CP) + 1)
                    held(pool, s_turn[1])
                for k in range(LT):
                    nc.gpsimd.indirect_dma_start(
                        out=ring[:, LT * (j % CP) + k, j // CP:j // CP + 2, :].rearrange("p t e -> p (t e)"),
                        out_offset=None, in_=io["kv"],
                        in_offset=bass.IndirectOffsetOnAxis(ap=idx[:, par, LT * (j % CP) + k:LT * (j % CP) + k + 1], axis=0)
                    ).then_inc(s_kv[j], 16)

            walk(pool, at)

        @block.scalar
        def _(act):
            def at(i, j, fresh):
                m = CR * i + j // CP - 1
                jj = j % CP
                if staged(i, j, fresh):
                    if jj == 0:
                        act.wait_ge(s_mp, NT * m + T_IN)
                        nc.scalar.activation(nrow[:, 0:P], psM[0:R, P:2 * P], ACT.Copy).then_inc(s_nrow, 1)
                    if jj == 6:
                        act.wait_ge(s_mv, NV * m + V_FMIN)
                        nc.scalar.activation(fx[:, :], fm[:, :], ACT.Exp, scale=SCALE).then_inc(s_fx, 1)
                        act.wait_ge(s_mv, NV * m + V_DIFF)
                        out = ring[:, :, (j // CP - 1) % CR, :].rearrange("p w (h e) -> p h w e", h=H)[:, :, :, D]
                        nc.scalar.activation(out, dif[:, :, :], ACT.Exp, scale=SCALE).then_inc(s_exp, 1)
                if live(i, j, fresh, PV_LAG):
                    sj = (j - PV_LAG) % RING
                    bc = CR * i + (j - PV_LAG) // CP
                    act.wait_ge(s_exp, bc + 1)
                    for k in range(LT):
                        for h in range(H):
                            row = ring[:, LT * (sj % CP) + k, sj // CP, h * HW_:(h + 1) * HW_]
                            last = nc.scalar.activation(row[:, 0:D], row[:, 0:D], ACT.Copy, scale=row[:, D:HW_])
                    last.then_inc(s_pv, 1)

            walk(act, at)

        @block.tensor
        def _(pe):
            pe.wait_ge(s_set, 5)

            def expand(i, j, fresh):
                step, cc, par, jj = RING * i + j, CR * i + j // CP, j // CP % 2, j % CP
                if jj == 0:
                    pe.wait_ge(s_oht, cc + 1)
                if not (fresh and j < NQ):
                    pe.wait_ge(s_prod, step - NQ + 1)
                blk = nc.tensor.value_load(brow[0:1, bass.ds(step, 1)], min_val=0, max_val=NB - 1)
                for k in range(LT):
                    w = LT * jj + k
                    for part in range(3):
                        last = nc.tensor.matmul(psQ[j % NQ][:, k * HID:(k + 1) * HID], ohT[par][:, w * P:(w + 1) * P],
                                                q3[:, part, bass.ds(blk, 1), :].rearrange("p a d -> p (a d)"),
                                                start=(part == 0), stop=(part == 2))
                last.then_inc(s_qe, 1)

            def rest(i, j, fresh):
                m = CR * i + j // CP - 1
                mpar = (j // CP - 1) % 2
                jj = j % CP if staged(i, j, fresh) else None
                if live(i, j, fresh, SUM_LAG):
                    b = RING * i + j - SUM_LAG
                    sj = (j - SUM_LAG) % RING
                    pe.wait_ge(s_pv, b + 1)
                    pe.wait_ge(s_oh, b + 1)
                    if not (fresh and j < SUM_LAG + NA):
                        pe.wait_ge(s_acc, b - NA + 1)
                    for k in range(LT):
                        last = nc.tensor.matmul(psA[sj % NA][0:BP, 0:HALFW], oh[:, sj % NO, k, :],
                                                ring[:, LT * (sj % CP) + k, sj // CP, :], start=(k == 0), stop=(k == LT - 1))
                    last.then_inc(s_agg, 1)
                if jj == 0:
                    pe.wait_ge(s_mv, NV * m + V_ALPHA)
                    pe.wait_ge(s_idx, 2 * m + 2)
                    held(pe, s_turn[2])
                    nc.tensor.transpose(psM[0:R, 0:P], alm[:, :, :].rearrange("p h w -> p (h w)"), ident[:, :])
                    nc.tensor.transpose(psM[0:R, P:2 * P], stc[:, mpar, :, :].rearrange("p h w -> p (h w)"),
                                        ident[:, :]).then_inc(s_mp, 1)
                if jj == 1:
                    pe.wait_ge(s_mv, NV * m + V_F1)
                    held(pe, s_turn[2])
                    nc.tensor.matmul(psR[0:1, 0:R], F1[:, P - 1:P], ident[0:R, 0:R], start=True, stop=True).then_inc(s_mp, 1)
                if jj == 2:
                    pe.wait_ge(s_mv, NV * m + V_INH)
                    nc.tensor.matmul(psR[0:R, 128:129], inh[:, :, :].rearrange("p h w -> p (h w)"), one[0:1, 0:1],
                                     start=True, stop=True).then_inc(s_mp, 1)
                if jj == 3:
                    pe.wait_ge(s_mv, NV * m + V_B1)
                    held(pe, s_turn[2])
                    nc.tensor.matmul(psR[0:1, 256:256 + R], B1[:, 0:1], ident[0:R, 0:R], start=True, stop=True).then_inc(s_mp, 1)
                if jj == 4:
                    pe.wait_ge(s_mv, NV * m + V_IV)
                    nc.tensor.matmul(psR[0:R, 384:385], iv[:, :, :].rearrange("p h w -> p (h w)"), one[0:1, 0:1],
                                     start=True, stop=True).then_inc(s_mp, 1)
                if jj == 5:
                    pe.wait_ge(s_mv, NV * m + V_G)
                    held(pe, s_turn[2])
                    nc.tensor.transpose(psM[:, 256:256 + R], Gm[:, :], ident[0:R, 0:R]).then_inc(s_mp, 1)
                if jj == 6:
                    pe.wait_ge(s_fx, m + 1)
                    pe.wait_ge(s_mv, NV * m + V_DIFF)
                    nc.tensor.matmul(psM[0:BP, 400:400 + H], oh0[:, :], fx[:, :], start=True, stop=True).then_inc(s_mp, 1)

            def at(i, j, fresh):
                if live(i, j, fresh):
                    expand(i, j, fresh)
                if j > 0:
                    rest(i, j - 1, fresh)
                elif not fresh:
                    rest(i - 1, RING - 1, False)

            walk(pe, at)

        @block.vector
        def _(dve):
            nc.vector.memset(acc[:, 0:12, :], 0.0).then_inc(s_set, 1)
            nc.vector.memset(acc[:, 12:NB, :], 0.0).then_inc(s_set, 1)
            nc.vector.memset(nrow[:, P:P + 1], 0.0).then_inc(s_set, 1)
            nc.vector.memset(tails[:, :, :], NEG).then_inc(s_set, 1)
            nc.vector.memset(heads[:, :, :], NEG).then_inc(s_set, 1)
            dve.wait_ge(s_set, 5)

            def build(turn, cc, q):
                dve.wait_ge(s_bc[q % 2], 16 * turn + 16)
                nc.vector.tensor_scalar(ohT[q % 2][:, :], ohT[q % 2][:, :], iotaP[0:BP, 0:1], None, ALU.is_equal).then_inc(s_oht, 1)
                dve.wait_ge(s_oht, cc + 1)
                nc.vector.tensor_scalar(noh[:, q:q + 1], ohT[q % 2][:, 0:1], -1.0, 1.0, ALU.mult, ALU.add).then_inc(s_noh, 1)

            build(0, 0, 0)

            def maximum(i, j, part):
                m = CR * i + j // CP - 1
                mpar = (j // CP - 1) % 2
                mv, mp = NV * m, NT * m
                at = (j % CP, part)

                def seen(n):
                    dve.wait_ge(s_mv, mv + n)

                if at == (0, 0):
                    dve.wait_ge(s_alpha, CP * m + CP)
                    nc.vector.tensor_tensor(alm[:, :, :], alpha[:, mpar, :, :],
                                            valN[:, bass.ds(W * m, W)].unsqueeze(1).broadcast_to([P, H, W]), ALU.add).then_inc(s_mv, 1)
                if at == (1, 0):
                    dve.wait_ge(s_mp, mp + T_IN)
                    dve.wait_ge(s_nrow, m + 1)
                    nc.vector.tensor_tensor_scan(out=F1[:, :], data0=nrow[:, 0:P], data1=psM[0:R, 0:P], initial=NEG,
                                                 op0=ALU.add, op1=ALU.max).then_inc(s_mv, 1)
                if at == (2, 0):
                    dve.wait_ge(s_mp, mp + T_TAIL)
                    nc.vector.tensor_copy(tails[:, :, 1:W + 1], psR[0:1, 0:R].rearrange("p (h w) -> p h w", h=H)).then_inc(s_mv, 1)
                if at == (2, 1):
                    seen(V_TAIL)
                    nc.vector.tensor_tensor_scan(out=carry[:, :, :].rearrange("p h w -> p (h w)"),
                                                 data0=keep["fwd"][:, bass.ds(m, 1), :, :].rearrange("p c h w -> p (c h w)"),
                                                 data1=tails[:, :, :].rearrange("p h w -> p (h w)"),
                                                 initial=NEG, op0=ALU.add, op1=ALU.max).then_inc(s_mv, 1)
                if at == (2, 2):
                    seen(V_CARRY)
                    nc.vector.tensor_copy(inh[:, :, :], carry[:, :, 0:W]).then_inc(s_mv, 1)
                if at == (3, 0):
                    dve.wait_ge(s_mp, mp + T_CARRY)
                    nc.vector.tensor_copy(cin[:, :], psR[0:R, 128:129]).then_inc(s_mv, 1)
                if at == (3, 1):
                    seen(V_CIN)
                    nc.vector.tensor_tensor_scan(out=F2[:, :], data0=nrow[:, 0:P], data1=psM[0:R, 0:P], initial=cin[:, 0:1],
                                                 op0=ALU.add, op1=ALU.max).then_inc(s_mv, 1)
                if at == (3, 2):
                    seen(V_F2)
                    nc.vector.tensor_tensor_scan(out=B1[:, ::-1], data0=nrow[:, 1:P + 1][:, ::-1], data1=F2[:, ::-1], initial=NEG,
                                                 op0=ALU.add, op1=ALU.max).then_inc(s_mv, 1)
                if at == (4, 0):
                    dve.wait_ge(s_mp, mp + T_HEAD)
                    nc.vector.tensor_copy(heads[:, :, 0:W], psR[0:1, 256:256 + R].rearrange("p (h w) -> p h w", h=H)).then_inc(s_mv, 1)
                if at == (4, 1):
                    seen(V_HEAD)
                    nc.vector.tensor_tensor_scan(out=back[:, :, :].rearrange("p h w -> p (h w)")[:, ::-1],
                                                 data0=keep["bwd"][:, bass.ds(m, 1), :, :].rearrange("p c h w -> p (c h w)"),
                                                 data1=heads[:, :, :].rearrange("p h w -> p (h w)")[:, ::-1],
                                                 initial=NEG, op0=ALU.add, op1=ALU.max).then_inc(s_mv, 1)
                if at == (4, 2):
                    seen(V_BACK)
                    nc.vector.tensor_tensor(iv[:, :, :], back[:, :, 1:W + 1],
                                            keep["nxt"][:, bass.ds(m, 1), :, :].rearrange("p c h w -> p (c h) w"), ALU.add).then_inc(s_mv, 1)
                    nc.vector.tensor_tensor(fd[:, :], tails[:, :, 0], back[:, :, 0], ALU.subtract).then_inc(s_mv, 1)
                if at == (5, 0):
                    seen(V_FD)
                    nc.vector.tensor_scalar(fm[:, :], fd[:, :], 0.0, None, ALU.min).then_inc(s_mv, 1)
                    nc.vector.tensor_copy(tails[:, :, 0], carry[:, :, W]).then_inc(s_mv, 1)
                    nc.vector.tensor_scalar(oh0[:, :], iotaF[0:1, 0:BP], dstR[0:1, bass.ds(W * m, 1)], None,
                                            ALU.is_equal).then_inc(s_mv, 1)
                    dve.wait_ge(s_mp, mp + T_IV)
                    nc.vector.tensor_copy(bin_[:, :], psR[0:R, 384:385]).then_inc(s_mv, 1)
                if at == (5, 1):
                    seen(V_BIN)
                    nc.vector.tensor_tensor_scan(out=Gm[:, ::-1], data0=nrow[:, 1:P + 1][:, ::-1], data1=F2[:, ::-1],
                                                 initial=bin_[:, 0:1], op0=ALU.add, op1=ALU.max).then_inc(s_mv, 1)
                if at == (6, 0):
                    dve.wait_ge(s_mp, mp + T_OUT)
                    nc.vector.tensor_tensor(dif[:, :, :], alm[:, :, :], psM[:, 256:256 + R].rearrange("p (h w) -> p h w", h=H),
                                            ALU.subtract).then_inc(s_mv, 1)
                if at == (7, 0):
                    dve.wait_ge(s_mp, mp + T_FAC)
                    at_noh = (j // CP - 1) % CR
                    nc.vector.tensor_scalar(fac[:, :], psM[0:BP, 400:400 + H], noh[:, at_noh:at_noh + 1], None,
                                            ALU.add).then_inc(s_mv, 1)

            def at(i, j, fresh):
                step = RING * i + j
                cc, q, jj = CR * i + j // CP, j // CP, j % CP
                now = staged(i, j, fresh)
                if live(i, j, fresh, ADD_LAG):
                    b = step - ADD_LAG
                    blk = nc.vector.value_load(brow[0:1, bass.ds(b, 1)], min_val=0, max_val=NB - 1)
                if live(i, j, fresh):
                    dve.wait_ge(s_kv[j], 32 * i + 32)
                    dve.wait_ge(s_qe, step + 1)
                    if not (fresh and j < 2):
                        dve.wait_ge(s_alpha, step - 1)
                    nc.vector.tensor_tensor(prod[:, j % 2, :].rearrange("p (k d) -> p k d", k=LT),
                                            psQ[j % NQ][:, :].rearrange("p (k d) -> p k d", k=LT),
                                            ring[:, LT * jj:LT * jj + LT, q + 1, 0:HID], ALU.mult).then_inc(s_prod, 1)
                if now:
                    maximum(i, j, 0)
                if live(i, j, fresh, SUM_LAG - 1):
                    bo = step - SUM_LAG + 1
                    sj = (j - SUM_LAG + 1) % RING
                    if not (fresh and j < SUM_LAG - 1 + NO):
                        dve.wait_ge(s_agg, bo - NO + 1)
                    nc.vector.tensor_tensor(oh[:, sj % NO, :, :], iotaF[:, 0:BP].unsqueeze(1).broadcast_to([P, LT, BP]),
                                            dstR[:, bass.ds(LT * bo, LT)].unsqueeze(2).broadcast_to([P, LT, BP]),
                                            ALU.is_equal).then_inc(s_oh, 1)
                if now:
                    maximum(i, j, 1)
                if jj == 6 and live(i, j, fresh, -CP):
                    build(2 * i + (q + 1) // 2, cc + 1, (q + 1) % CR)
                if live(i, j, fresh, ADD_LAG):
                    sj = (j - ADD_LAG) % RING
                    dve.wait_ge(s_agg, b + 1)
                    if not (fresh and j < ADD_LAG + 1):
                        dve.wait_ge(s_acc, b)
                    if sj % CP == 0:
                        dve.wait_ge(s_resc, CR * i + (j - ADD_LAG) // CP + 1)
                    row = acc[:, bass.ds(blk, 1), :].rearrange("p a d -> p (a d)")
                    nc.vector.tensor_tensor(row, row, psA[sj % NA][0:BP, 0:HALFW], ALU.add).then_inc(s_acc, 1)
                if now:
                    maximum(i, j, 2)
                if live(i, j, fresh):
                    dve.wait_ge(s_prod, step + 1)
                    nc.vector.tensor_reduce(alpha[:, q % 2, :, LT * jj:LT * jj + LT].rearrange("p h w -> p w h"),
                                            prod[:, j % 2, :].rearrange("p (k h d) -> p k h d", k=LT, h=H), AX.X, ALU.add
                                            ).then_inc(s_alpha, 1)
                if (j - ADD_LAG + 1) % CP == 0 and live(i, j, fresh, ADD_LAG - 1):
                    br = step - ADD_LAG + 1
                    m = CR * i + (j - ADD_LAG + 1) // CP
                    blk = nc.vector.value_load(brow[0:1, bass.ds(br, 1)], min_val=0, max_val=NB - 1)
                    dve.wait_ge(s_mv, NV * m + V_FAC)
                    if not (fresh and j < ADD_LAG):
                        dve.wait_ge(s_acc, br)
                    row = acc[:, bass.ds(blk, 1), :].rearrange("p a (h e) -> p (a h) e", h=H)
                    nc.vector.tensor_tensor(row, row, fac[:, :].unsqueeze(2).broadcast_to([BP, H, HW_]), ALU.mult).then_inc(s_resc, 1)

            walk(dve, at)


def mlp(nc, ctx, io, keep):
    c = ExitStack()
    with c:
        def sb(name, shape, dt=F32):
            return c.enter_context(nc.sbuf_tensor(name, shape, dt))

        def pb(name, shape):
            return c.enter_context(nc.psum_tensor(name, shape, F32))

        def sem(name):
            return ctx.enter_context(nc.semaphore(name))

        ident, acc, x1, mv3 = keep["ident"], keep["acc"], keep["x1"], keep["mv3"]
        FC = FF // P
        w1 = sb("w1", [P, KC, FF])
        w2 = sb("w2", [P, FC, HID])
        b1r = sb("b1r", [FC, P])
        b1c = sb("b1c", [P, FC])
        g1b = sb("g1b", [BP, HID])
        be1 = sb("be1", [BP, HID])
        b2b = sb("b2b", [BP, HID])
        g2b = sb("g2b", [BP, HID])
        be2 = sb("be2", [BP, HID])
        rec = sb("recden", [BP, NB, H])
        den = sb("den", [BP, NB, H])
        res = sb("resin", [BP, GU, HID])
        xin = sb("xin", [BP, GU, HID])
        y = sb("y", [BP, GU, HID])
        z = sb("z", [BP, GU, HID])
        h = sb("h", [BP, GU, HID])
        hT = sb("hT", [P, KC, GN])
        gT = sb("gT", [P, FC, GN])
        st = sb("st1", [BP, GU, 6])
        mv = sb("mv1", [BP, GU, 2])
        ve = sb("ve1", [BP, 3, GU])
        rs = sb("rs1", [BP, 3, GU])
        mh = sb("mh1", [BP, GU])
        st2 = sb("st2", [BP, GU, 6])
        mv2 = sb("mv2", [BP, GU, 2])
        mvs = sb("mvs", [BP, GU, 2])

        psT = [pb(f"psT2{b}", [P, 512]) for b in range(2)]
        psF = [pb(f"psF{b}", [P, 512]) for b in range(3)]
        psO = [pb(f"psO{b}", [P, 512]) for b in range(2)]
        psB = pb("psB", [P, 512])

        s_w1, s_w2, s_row, s_half = sem("m_w1"), sem("m_w2"), sem("m_row"), sem("m_half")
        s_res, s_xin = sem("m_res"), sem("m_xin")
        s_den, s_resu, s_xinu = sem("m_den"), sem("m_resu"), sem("m_xinu")
        s_ln1, s_mv1, s_rs1, s_h, s_hb = sem("m_ln1"), sem("m_mv1"), sem("m_rs1"), sem("m_h"), sem("m_hb")
        s_ve1, s_ve2 = sem("m_ve1"), sem("m_ve2")
        s_tr, s_hT, s_ff, s_ge, s_fo = sem("m_tr"), sem("m_hT"), sem("m_ff"), sem("m_ge"), sem("m_fo")
        s_y, s_ln2, s_mv2, s_rs2, s_x1, s_mv3 = sem("m_y"), sem("m_ln2"), sem("m_mv2"), sem("m_rs2"), sem("m_x1"), sem("m_mv3")
        s_turn = [sem("m_turn_pool"), sem("m_turn_dve")]
        s_mvs = sem("m_mvs")
        s_bt, s_bc, s_st3, s_we = sem("m_bt"), sem("m_bc"), sem("m_st3"), sem("m_we")

        res_v = io["res"].rearrange("(g u p) d -> p g u d", p=BP, u=GU)
        x_v = io["x"].rearrange("(g u p) d -> p g u d", p=BP, u=GU)
        block = c.enter_context(nc.Block())

        @block.sync
        def _(sp):
            def group(g, fresh):
                if not fresh:
                    sp.wait_ge(s_resu, g)
                sp.dma_start(res[:, :, :], res_v[:, bass.ds(g, 1), :, :].rearrange("p g u d -> p (g u) d")).then_inc(s_res, 16)
                if not fresh:
                    sp.wait_ge(s_xinu, g)
                sp.dma_start(xin[:, :, :], x_v[:, bass.ds(g, 1), :, :].rearrange("p g u d -> p (g u) d")).then_inc(s_xin, 16)

            group(0, True)
            for t, a in ((g1b, "ln1_g"), (be1, "ln1_b"), (b2b, "b2"), (g2b, "ln2_g"), (be2, "ln2_b")):
                sp.dma_start(t[:, :], io["L0_gnn_" + a].partition_broadcast(BP)).then_inc(s_row, 16)
            sp.dma_start(b1r[:, :], io["L0_gnn_b1"].rearrange("(c p) -> c p", p=P)).then_inc(s_row, 16)
            sp.dma_start(w1[:, :, :], io["L0_gnn_W1"].rearrange("(k p) n -> p k n", p=P)).then_inc(s_w1, 16)
            sp.dma_start(w2[:, :, :], io["L0_gnn_W2"].rearrange("(k p) n -> p k n", p=P)).then_inc(s_w2, 16)
            with sp.Fori(1, G) as g:
                group(g, False)
            for l, n in enumerate(("W1", "W2", "Wo")):
                sp.dma_start(keep["we"][l][:, :, :, :], io["L0_ffn_" + n].rearrange("e (k p) n -> p e k n", p=P)).then_inc(s_we, 16)
            sp.wait_ge(s_we, 48)

        @block.gpsimd
        def _(pool):
            nc.gpsimd.memset(mh[:, :], -0.5).then_inc(s_half, 1)
            pool.wait_ge(s_half, 1)

            def root(g, k, m, s_m, s_v, s_r):
                pool.wait_ge(s_m, GU * g + GU)
                held(pool, s_turn[0])
                nc.gpsimd.tensor_scalar(ve[:, k, :], m[:, :, 1], LN_EPS, None, ALU.add).then_inc(s_v, 1)
                pool.wait_ge(s_v, g + 1)
                nc.gpsimd.tensor_tensor(rs[:, k, :], ve[:, k, :], mh[:, :], ALU.pow).then_inc(s_r, 1)

            root(0, 0, mv, s_mv1, s_ve1, s_rs1)
            with pool.Fori(0, G - 1) as g:
                root(g + 1, 0, mv, s_mv1, s_ve1, s_rs1)
                root(g, 1, mv2, s_mv2, s_ve2, s_rs2)
            root(G - 1, 1, mv2, s_mv2, s_ve2, s_rs2)

        @block.scalar
        def _(act):
            def columns(g):
                for u in range(GU):
                    act.wait_ge(s_tr, GU * g + u + 1)
                    nc.scalar.activation(hT[:, :, u * BP:(u + 1) * BP],
                                         psT[u % 2][:, 0:KC * BP].rearrange("p (k n) -> p k n", k=KC), ACT.Copy).then_inc(s_hT, 1)

            def gelu(g, fresh):
                if not fresh:
                    act.wait_ge(s_fo, GU * g)
                for n, (m, (a, b)) in enumerate((m, ab) for m in range(FC) for ab in HALVES):
                    act.wait_ge(s_ff, 2 * FC * g + n + 1)
                    nc.scalar.activation(gT[:, m, a:b], psF[n % 3][:, 0:b - a], ACT.Gelu, bias=b1c[:, m:m + 1]).then_inc(s_ge, 1)

            columns(0)
            act.wait_ge(s_bc, 1)
            gelu(0, True)
            with act.Fori(1, G) as g:
                columns(g)
                gelu(g, False)

        @block.tensor
        def _(pe):
            def columns(g, fresh):
                pe.wait_ge(s_h, g + 1)
                for u in range(GU):
                    if not (fresh and u < 2):
                        pe.wait_ge(s_hT, GU * g + max(u - 1, 0))
                    for k in range(KC):
                        last = nc.tensor.transpose(psT[u % 2][:, k * BP:(k + 1) * BP], h[:, u, k * P:(k + 1) * P],
                                                   ident[0:BP, 0:BP])
                    last.then_inc(s_tr, 1)

            def first(g, fresh):
                pe.wait_ge(s_hT, GU * g + GU)
                for n, (m, (a, b)) in enumerate((m, ab) for m in range(FC) for ab in HALVES):
                    if not (fresh and n < 3):
                        pe.wait_ge(s_ge, 2 * FC * g + n - 2)
                    for k in range(KC):
                        last = nc.tensor.matmul(psF[n % 3][:, 0:b - a], w1[:, k, m * P:(m + 1) * P], hT[:, k, a:b],
                                                start=(k == 0), stop=(k == KC - 1))
                    last.then_inc(s_ff, 1)

            def second(g, fresh):
                pe.wait_ge(s_ge, 2 * FC * g + 2 * FC)
                for u in range(GU):
                    if not (fresh and u < 2):
                        pe.wait_ge(s_y, GU * g + max(u - 1, 0))
                    for m in range(FC):
                        last = nc.tensor.matmul(psO[u % 2][0:BP, 0:HID], gT[:, m, u * BP:(u + 1) * BP], w2[:, m, :],
                                                start=(m == 0), stop=(m == FC - 1))
                    last.then_inc(s_fo, 1)

            pe.wait_ge(s_row, 96)
            nc.tensor.transpose(psB[:, 0:FC], b1r[:, :], ident[0:FC, 0:FC]).then_inc(s_bt, 1)
            columns(0, True)
            pe.wait_ge(s_w1, 16)
            first(0, True)
            pe.wait_ge(s_w2, 16)
            columns(1, False)
            second(0, True)
            with pe.Fori(1, G - 1) as g:
                first(g, False)
                columns(g + 1, False)
                second(g, False)
            first(G - 1, False)
            second(G - 1, False)

        @block.vector
        def _(dve):
            wide = acc[:, :, :].rearrange("p t (h e) -> p t h e", h=H)
            nc.vector.tensor_scalar(den[:, :, :], wide[:, :, :, D], 1e-16, None, ALU.add).then_inc(s_den, 1)
            dve.wait_ge(s_den, 1)
            nc.vector.reciprocal(rec[:, :, :], den[:, :, :]).then_inc(s_den, 1)
            dve.wait_ge(s_row, 96)
            dve.wait_ge(s_bt, 1)
            nc.vector.tensor_copy(b1c[:, :], psB[:, 0:FC]).then_inc(s_bc, 1)
            dve.wait_ge(s_den, 2)

            def rows(t):
                return t[:, :].unsqueeze(1).broadcast_to([BP, GU, HID])

            K1, K2 = 2 * GU + 2, GU + 3

            def norm1(g, fresh):
                for u in range(GU):
                    nc.vector.tensor_tensor(
                        y[:, u, :].rearrange("p (h d) -> p h d", h=H),
                        acc[:, bass.ds(GU * g + u, 1), :].rearrange("p t (h e) -> p (t h) e", h=H)[:, :, 0:D],
                        rec[:, bass.ds(GU * g + u, 1), :].rearrange("p t h -> p (t h)").unsqueeze(2).broadcast_to([BP, H, D]),
                        ALU.mult).then_inc(s_ln1, 1)
                dve.wait_ge(s_res, 16 * g + 16)
                dve.wait_ge(s_ln1, K1 * g + GU)
                nc.vector.tensor_tensor(y[:, :, :], y[:, :, :], res[:, :, :], ALU.add).then_inc(s_resu, 1)
                dve.wait_ge(s_resu, g + 1)
                for u in range(GU):
                    nc.vector.bn_stats(st[:, u, :], y[:, u, :]).then_inc(s_ln1, 1)
                dve.wait_ge(s_ln1, K1 * g + 2 * GU)
                held(dve, s_turn[1])
                for u in range(GU):
                    nc.vector.bn_aggr(mv[:, u, :], st[:, u, :]).then_inc(s_mv1, 1)
                dve.wait_ge(s_rs1, g + 1)
                for u in range(GU):
                    last = nc.vector.tensor_scalar(y[:, u, :], y[:, u, :], mv[:, u, 0:1], rs[:, 0, u:u + 1],
                                                   ALU.subtract, ALU.mult)
                last.then_inc(s_ln1, 1)
                dve.wait_ge(s_ln1, K1 * g + 2 * GU + 1)
                nc.vector.tensor_tensor(y[:, :, :], y[:, :, :], rows(g1b), ALU.mult).then_inc(s_ln1, 1)
                dve.wait_ge(s_ln1, K1 * g + 2 * GU + 2)
                if not fresh:
                    dve.wait_ge(s_tr, GU * g)
                nc.vector.tensor_tensor(h[:, :, :], y[:, :, :], rows(be1), ALU.add).then_inc(s_h, 1)
                dve.wait_ge(s_h, g + 1)
                nc.vector.tensor_tensor(x1[:, bass.ds(GU * g, GU), :], h[:, :, :], rows(b2b), ALU.add).then_inc(s_hb, 1)

            def norm2(g):
                dve.wait_ge(s_hb, g + 1)
                for u in range(GU):
                    dve.wait_ge(s_fo, GU * g + u + 1)
                    nc.vector.tensor_tensor(z[:, u, :], psO[u % 2][0:BP, 0:HID],
                                            x1[:, bass.ds(GU * g + u, 1), :].rearrange("p t d -> p (t d)"), ALU.add).then_inc(s_y, 1)
                for u in range(GU):
                    dve.wait_ge(s_y, GU * g + u + 1)
                    nc.vector.bn_stats(st2[:, u, :], z[:, u, :]).then_inc(s_ln2, 1)
                dve.wait_ge(s_ln2, K2 * g + GU)
                held(dve, s_turn[1])
                for u in range(GU):
                    nc.vector.bn_aggr(mv2[:, u, :], st2[:, u, :]).then_inc(s_mv2, 1)
                dve.wait_ge(s_rs2, g + 1)
                for u in range(GU):
                    last = nc.vector.tensor_scalar(z[:, u, :], z[:, u, :], mv2[:, u, 0:1], rs[:, 1, u:u + 1],
                                                   ALU.subtract, ALU.mult)
                last.then_inc(s_ln2, 1)
                dve.wait_ge(s_ln2, K2 * g + GU + 1)
                nc.vector.tensor_tensor(z[:, :, :], z[:, :, :], rows(g2b), ALU.mult).then_inc(s_ln2, 1)
                dve.wait_ge(s_ln2, K2 * g + GU + 2)
                nc.vector.tensor_tensor(z[:, :, :], z[:, :, :], rows(be2), ALU.add).then_inc(s_ln2, 1)
                dve.wait_ge(s_ln2, K2 * g + GU + 3)
                dve.wait_ge(s_xin, 16 * g + 16)
                nc.vector.tensor_tensor(x1[:, bass.ds(GU * g, GU), :], z[:, :, :], xin[:, :, :], ALU.add).then_inc(s_xinu, 1)
                dve.wait_ge(s_xinu, g + 1)
                held(dve, s_turn[1])
                for u in range(GU):
                    nc.vector.bn_stats(st2[:, u, :], x1[:, bass.ds(GU * g + u, 1), :].rearrange("p t d -> p (t d)")).then_inc(s_st3, 1)
                dve.wait_ge(s_st3, GU * g + GU)
                held(dve, s_turn[1])
                for u in range(GU):
                    nc.vector.bn_aggr(mvs[:, u, :], st2[:, u, :]).then_inc(s_mvs, 1)
                dve.wait_ge(s_mvs, GU * g + GU)
                nc.vector.tensor_copy(mv3[:, bass.ds(GU * g, GU), :], mvs[:, :, :]).then_inc(s_mv3, 1)

            norm1(0, True)
            with dve.Fori(0, G - 1) as g:
                norm1(g + 1, False)
                norm2(g)
            norm2(G - 1)


def experts(nc, ctx, io, keep):
    c = ExitStack()
    with c:
        def sb(name, shape, dt=F32):
            return c.enter_context(nc.sbuf_tensor(name, shape, dt))

        def pb(name, shape):
            return c.enter_context(nc.psum_tensor(name, shape, F32))

        def sem(name):
            return ctx.enter_context(nc.semaphore(name))

        ident, x1, mv3 = keep["ident"], keep["x1"], keep["mv3"]
        we = keep["we"]
        NP = 2 * NE
        prm = sb("prm", [NP, 10, P])
        sc = sb("sc", [NP, 4, P])
        tmp = sb("tmp", [NP, 2, P])
        hv = sb("hv", [NP, 2, P])
        scT = sb("scT", [P, 4, NP])
        wr = sb("wr", [P, KC, NE])
        br = sb("br", [BP, NE])
        bo = sb("bo", [NE, HID])
        ve3 = sb("ve3", [BP, NB])
        rs3 = sb("rs3", [BP, NB])
        mh3 = sb("mh3", [BP, NB])
        xg = sb("xg", [BP, GU, HID])
        xT = sb("xT", [P, KC, GN])
        lg = sb("lg", [BP, GU, NE])
        mx = sb("mx", [BP, GU])
        ex = sb("ex", [BP, GU, NE])
        sm = sb("sm", [BP, GU])
        wt = sb("wt", [BP, GU, NE])
        wT = sb("wT", [NE, GN])
        h1 = sb("h1", [P, 2, KC, GN])
        h2 = sb("h2", [P, 2, KC, GN])
        o = sb("o", [BP, GU, HID])

        psT = [pb(f"psT3{b}", [P, 512]) for b in range(2)]
        psF = [pb(f"psF3{b}", [P, 512]) for b in range(4)]
        psO = [pb(f"psO3{b}", [P, 512]) for b in range(2)]

        s_prm, s_wr, s_half = sem("e_prm"), sem("e_wr"), sem("e_half")
        s_ve, s_rs, s_sc, s_hv, s_scp, s_scT = sem("e_ve"), sem("e_rs"), sem("e_sc"), sem("e_hv"), sem("e_scp"), sem("e_scT")
        s_xg, s_tr, s_xT, s_lg = sem("e_xg"), sem("e_tr"), sem("e_xT"), sem("e_lg")
        s_sx, s_ex, s_wt, s_wtp, s_wT = sem("e_sx"), sem("e_ex"), sem("e_wt"), sem("e_wtp"), sem("e_wT")
        s_sm, s_tm = sem("e_sm"), sem("e_tm")
        s_f, s_r, s_l3, s_cb, s_out = sem("e_f"), sem("e_r"), sem("e_l3"), sem("e_cb"), sem("e_out")

        out_v = io["out"].rearrange("(g u p) d -> p g u d", p=BP, u=GU)
        jobs = [(1, 0)] + [j for e in range(NE) for j in (([(1, e + 1)] if e + 1 < NE else []) + [(2, e)])]
        NJ = len(jobs)
        JF = 4
        parts = [(m, a, b) for m in range(KC) for a, b in HALVES]
        IT = GU * (NE + 1)

        block = c.enter_context(nc.Block())

        @block.sync
        def _(sp):
            for k, n in enumerate(("b1", "g1", "be1", "m1", "v1", "b2", "g2", "be2", "m2", "v2")):
                sp.dma_start(prm[:, k, :], io["L0_ffn_" + n].rearrange("e (m p) -> (e m) p", p=P)).then_inc(s_prm, 16)
            sp.dma_start(wr[:, :, :], io["L0_ffn_Wr"].rearrange("(k p) e -> p k e", p=P)).then_inc(s_wr, 16)
            sp.dma_start(br[:, :], io["L0_ffn_br"].partition_broadcast(BP)).then_inc(s_wr, 16)
            sp.dma_start(bo[:, :], io["L0_ffn_bo"]).then_inc(s_wr, 16)
            with sp.Fori(0, G) as g:
                sp.wait_ge(s_cb, IT * g + IT)
                sp.dma_start(out_v[:, bass.ds(g, 1), :, :].rearrange("p g u d -> p (g u) d"), o[:, :, :]).then_inc(s_out, 16)
            sp.wait_ge(s_out, 16 * G)

        @block.gpsimd
        def _(pool):
            nc.gpsimd.memset(mh3[:, :], -0.5).then_inc(s_half, 1)
            nc.gpsimd.memset(hv[:, :, :], -0.5).then_inc(s_half, 1)
            nc.gpsimd.tensor_scalar(ve3[:, :], mv3[:, :, 1], LN_EPS, None, ALU.add).then_inc(s_ve, 1)
            pool.wait_ge(s_half, 2)
            pool.wait_ge(s_ve, 1)
            nc.gpsimd.tensor_tensor(rs3[:, :], ve3[:, :], mh3[:, :], ALU.pow).then_inc(s_rs, 1)
            pool.wait_ge(s_prm, 160)
            for l in range(2):
                nc.gpsimd.tensor_scalar(tmp[:, l, :], prm[:, 5 * l + 4, :], BN_EPS, None, ALU.add).then_inc(s_ve, 1)
            pool.wait_ge(s_ve, 3)
            nc.gpsimd.tensor_tensor(hv[:, :, :], tmp[:, :, :], hv[:, :, :], ALU.pow).then_inc(s_hv, 1)

        @block.scalar
        def _(act):
            def columns(g):
                for u in range(GU):
                    act.wait_ge(s_tr, GU * g + u + 1)
                    nc.scalar.activation(xT[:, :, u * BP:(u + 1) * BP],
                                         psT[u % 2][:, 0:KC * BP].rearrange("p (k n) -> p k n", k=KC), ACT.Copy).then_inc(s_xT, 1)

            def router(g):
                act.wait_ge(s_sx, 3 * g + 3)
                nc.scalar.activation(ex[:, :, :], lg[:, :, :], ACT.Exp).then_inc(s_ex, 1)

            def group(g, last_group):
                for q, (layer, e) in enumerate(jobs):
                    if q == 1:
                        router(g)
                    if q == NJ - 2 and not last_group:
                        columns(g + 1)
                    for n, (m, a, b) in enumerate(parts):
                        act.wait_ge(s_f, JF * NJ * g + JF * q + n + 1)
                        to = (h1 if layer == 1 else h2)[:, e % 2, m, a:b]
                        col = 2 * e + m
                        nc.scalar.activation(to, psF[n][:, 0:b - a], ACT.Relu, bias=scT[:, 2 * layer - 1, col:col + 1],
                                             scale=scT[:, 2 * layer - 2, col:col + 1]).then_inc(s_r, 1)

            columns(0)
            act.wait_ge(s_scT, 1)
            with act.Fori(0, G - 1) as g:
                group(g, False)
            group(G - 1, True)

        @block.tensor
        def _(pe):
            def columns(g):
                pe.wait_ge(s_xg, g + 1)
                for u in range(GU):
                    if u < 2 and not (isinstance(g, int) and g == 0):
                        pe.wait_ge(s_wT, 2 * g)
                    if u >= 2:
                        pe.wait_ge(s_xT, GU * g + u - 1)
                    for k in range(KC):
                        last = nc.tensor.transpose(psT[u % 2][:, k * BP:(k + 1) * BP], xg[:, u, k * P:(k + 1) * P],
                                                   ident[0:BP, 0:BP])
                    last.then_inc(s_tr, 1)

            def router(g):
                pe.wait_ge(s_xT, GU * g + GU)
                for u in range(GU):
                    for k in range(KC):
                        last = nc.tensor.matmul(psT[0][0:BP, 256 + u * NE:256 + (u + 1) * NE], xT[:, k, u * BP:(u + 1) * BP],
                                                wr[:, k, :], start=(k == 0), stop=(k == KC - 1))
                last.then_inc(s_lg, 1)

            def weights(g):
                pe.wait_ge(s_wt, g + 1)
                for b, us in ((0, (0, 1, 2)), (1, (3, 4))):
                    for n, u in enumerate(us):
                        last = nc.tensor.transpose(psT[b][0:NE, n * BP:(n + 1) * BP], wt[:, u, :], ident[0:BP, 0:BP])
                    last.then_inc(s_wtp, 1)

            def biases(g):
                pe.wait_ge(s_wT, 2 * g + 2)
                for u in range(GU):
                    if u < 2:
                        if not (isinstance(g, int) and g == 0):
                            pe.wait_ge(s_cb, IT * g)
                    else:
                        pe.wait_ge(s_cb, IT * g + u - 1)
                    nc.tensor.matmul(psO[u % 2][0:BP, 0:HID], wT[:, u * BP:(u + 1) * BP], bo[:, :], start=True, stop=True
                                     ).then_inc(s_l3, 1)

            def third(g, e):
                q = jobs.index((2, e))
                pe.wait_ge(s_r, JF * NJ * g + JF * q + JF)
                for u in range(GU):
                    n = GU * (e + 1) + u
                    pe.wait_ge(s_cb, IT * g + n - 1)
                    for k in range(KC):
                        last = nc.tensor.matmul(psO[n % 2][0:BP, 0:HID], h2[:, e % 2, k, u * BP:(u + 1) * BP],
                                                we[2][:, e, k, :], start=(k == 0), stop=(k == KC - 1))
                    last.then_inc(s_l3, 1)

            def group(g, fresh, last_group):
                for q, (layer, e) in enumerate(jobs):
                    if layer == 2 and e >= 1:
                        third(g, e - 1)
                    if layer == 2:
                        pe.wait_ge(s_r, JF * NJ * g + JF * jobs.index((1, e)) + JF)
                    for n, (m, a, b) in enumerate(parts):
                        if q or not fresh:
                            pe.wait_ge(s_r, JF * NJ * g + JF * (q - 1) + n + 1)
                        for k in range(KC):
                            x = xT[:, k, a:b] if layer == 1 else h1[:, e % 2, k, a:b]
                            last = nc.tensor.matmul(psF[n][:, 0:b - a], we[layer - 1][:, e, k, m * P:(m + 1) * P], x,
                                                    start=(k == 0), stop=(k == KC - 1))
                        last.then_inc(s_f, 1)
                    if q == 1:
                        weights(g)
                    if q == 2:
                        biases(g)
                    if (layer, e) == (1, NE - 1) and not last_group:
                        columns(g + 1)
                third(g, NE - 1)
                if not last_group:
                    router(g + 1)

            columns(0)
            pe.wait_ge(s_wr, 48)
            router(0)
            pe.wait_ge(s_sc, 6)
            for k in range(4):
                last = nc.tensor.transpose(psO[0][:, k * NP:(k + 1) * NP], sc[:, k, :], ident[0:NP, 0:NP])
            last.then_inc(s_scp, 1)
            pe.wait_ge(s_scT, 1)
            group(0, True, False)
            with pe.Fori(1, G - 1) as g:
                group(g, False, False)
            group(G - 1, False, True)

        @block.vector
        def _(dve):
            dve.wait_ge(s_rs, 1)

            def normal(g, fresh):
                if not fresh:
                    dve.wait_ge(s_tr, GU * g)
                for u in range(GU):
                    row = x1[:, bass.ds(GU * g + u, 1), :].rearrange("p t d -> p (t d)")
                    last = nc.vector.tensor_scalar(xg[:, u, :], row,
                                                   mv3[:, bass.ds(GU * g + u, 1), 0:1].rearrange("p t s -> p (t s)"),
                                                   rs3[:, bass.ds(GU * g + u, 1)], ALU.subtract, ALU.mult)
                last.then_inc(s_xg, 1)

            def softmax(g):
                dve.wait_ge(s_lg, g + 1)
                nc.vector.tensor_tensor(lg[:, :, :], psT[0][0:BP, 256:256 + GU * NE].rearrange("p (u e) -> p u e", u=GU),
                                        br[:, :].unsqueeze(1).broadcast_to([BP, GU, NE]), ALU.add).then_inc(s_sx, 1)
                dve.wait_ge(s_sx, 3 * g + 1)
                nc.vector.tensor_reduce(mx[:, :], lg[:, :, :], AX.X, ALU.max).then_inc(s_sx, 1)
                dve.wait_ge(s_sx, 3 * g + 2)
                nc.vector.tensor_tensor(lg[:, :, :], lg[:, :, :], mx[:, :].unsqueeze(2).broadcast_to([BP, GU, NE]),
                                        ALU.subtract).then_inc(s_sx, 1)
                dve.wait_ge(s_ex, g + 1)
                nc.vector.tensor_reduce(sm[:, :], ex[:, :, :], AX.X, ALU.add).then_inc(s_sm, 1)
                dve.wait_ge(s_sm, 2 * g + 1)
                nc.vector.reciprocal(mx[:, :], sm[:, :]).then_inc(s_sm, 1)
                dve.wait_ge(s_sm, 2 * g + 2)
                nc.vector.tensor_tensor(wt[:, :, :], ex[:, :, :], mx[:, :].unsqueeze(2).broadcast_to([BP, GU, NE]),
                                        ALU.mult).then_inc(s_wt, 1)
                dve.wait_ge(s_wtp, 2 * g + 1)
                nc.vector.tensor_copy(wT[:, 0:3 * BP], psT[0][0:NE, 0:3 * BP]).then_inc(s_wT, 1)
                dve.wait_ge(s_wtp, 2 * g + 2)
                nc.vector.tensor_copy(wT[:, 3 * BP:GN], psT[1][0:NE, 0:2 * BP]).then_inc(s_wT, 1)

            def sums(g, fresh):
                if not fresh:
                    dve.wait_ge(s_out, 16 * g)
                for n in range(IT):
                    u, e = n % GU, n // GU - 1
                    dve.wait_ge(s_l3, IT * g + n + 1)
                    ps = psO[n % 2][0:BP, 0:HID]
                    if e < 0:
                        nc.vector.tensor_tensor(o[:, u, :], ps, x1[:, bass.ds(GU * g + u, 1), :].rearrange("p t d -> p (t d)"),
                                                ALU.add).then_inc(s_cb, 1)
                    else:
                        dve.wait_ge(s_cb, IT * g + n + 1 - GU)
                        nc.vector.scalar_tensor_tensor(out=o[:, u, :], in0=ps, scalar=wt[:, u, e:e + 1], in1=o[:, u, :],
                                                       op0=ALU.mult, op1=ALU.add).then_inc(s_cb, 1)

            normal(0, True)
            dve.wait_ge(s_hv, 1)
            dve.wait_ge(s_prm, 160)
            for l in range(2):
                nc.vector.tensor_tensor(sc[:, 2 * l, :], prm[:, 5 * l + 1, :], hv[:, l, :], ALU.mult).then_inc(s_sc, 1)
                nc.vector.tensor_tensor(tmp[:, l, :], prm[:, 5 * l, :], prm[:, 5 * l + 3, :], ALU.subtract).then_inc(s_sc, 1)
            dve.wait_ge(s_sc, 4)
            for l in range(2):
                nc.vector.tensor_tensor(tmp[:, l, :], tmp[:, l, :], sc[:, 2 * l, :], ALU.mult).then_inc(s_tm, 1)
            dve.wait_ge(s_tm, 2)
            for l in range(2):
                nc.vector.tensor_tensor(sc[:, 2 * l + 1, :], tmp[:, l, :], prm[:, 5 * l + 2, :], ALU.add).then_inc(s_sc, 1)
            dve.wait_ge(s_scp, 1)
            nc.vector.tensor_copy(scT[:, :, :], psO[0][:, 0:4 * NP].rearrange("p (k n) -> p k n", k=4)).then_inc(s_scT, 1)
            dve.wait_ge(s_wr, 48)
            softmax(0)
            normal(1, False)
            sums(0, True)
            with dve.Fori(1, G - 1) as g:
                softmax(g)
                normal(g + 1, False)
                sums(g, False)
            softmax(G - 1)
            sums(G - 1, False)


def build(nc, io):
    io = dict(io)
    io["kv"] = nc.dram_tensor("kv_rows", [N, KVW], F32, kind="Internal").ap()
    io["res"] = nc.dram_tensor("residual", [N, HID], F32, kind="Internal").ap()
    io["rec"] = nc.dram_tensor("tile_records", [TILES, 3 * TL], F32, kind="Internal").ap()
    io["drel"] = nc.dram_tensor("step_destinations", [STEPS, TL], BF16, kind="Internal").ap()
    with ExitStack() as ctx:
        keep = {}

        def sb(stack, name, shape, dt=F32):
            keep[name] = stack.enter_context(nc.sbuf_tensor("k_" + name, shape, dt))

        sb(ctx, "ident", [P, P])
        sb(ctx, "iotaF", [P, P])
        sb(ctx, "iotaP", [P, 1])
        sb(ctx, "one", [1, 1])
        sb(ctx, "ones", [P, 1])
        sb(ctx, "acc", [BP, NB, H * HW_])
        with ExitStack() as graph:
            sb(graph, "q3", [BP, 3, NB, HID], BF16)
            sb(graph, "brow", [1, STEPS], I32)
            sb(graph, "srcI", [P, LT * STEPS], I32)
            for n in ("dstR", "startN", "valN"):
                sb(graph, n, [P, LT * STEPS])
            for n in ("fwd", "bwd"):
                sb(graph, n, [1, C, H, W + 1], BF16)
            sb(graph, "nxt", [1, C, H, W], BF16)
            project(nc, ctx, io, keep)
            attend(nc, ctx, io, keep)
        with ExitStack() as dense:
            sb(dense, "x1", [BP, NB, HID])
            sb(dense, "mv3", [BP, NB, 2])
            keep["we"] = [dense.enter_context(nc.sbuf_tensor(f"k_we{l}", [P, NE, KC, HID], F32)) for l in range(3)]
            mlp(nc, ctx, io, keep)
            experts(nc, ctx, io, keep)


_INS = ["x", "src", "dst"] + ["L0_gnn_" + n for n in (
    "Wq", "bq", "Wk", "bk", "Wv", "bv", "Wskip", "bskip", "ln1_g", "ln1_b", "W1", "b1", "W2", "b2", "ln2_g", "ln2_b")] + [
    "L0_ffn_" + n for n in ("Wr", "br", "W1", "b1", "g1", "be1", "m1", "v1", "W2", "b2", "g2", "be2", "m2", "v2", "Wo", "bo")]


def kernel(**inputs):
    import numpy as _np
    import concourse.bacc as _bacc
    from concourse import mybir as _mybir
    from concourse.bass_utils import run_bass_kernel_spmd as _run

    nc = _bacc.Bacc("TRN2", target_bir_lowering=False, num_devices=1)
    arrays, io = {}, {}
    for name in _INS:
        a = _np.ascontiguousarray(inputs[name])
        arrays[f"in_{name}"] = a
        io[name] = nc.dram_tensor(f"in_{name}", a.shape, _mybir.dt.from_np(a.dtype), kind="ExternalInput").ap()
    io["out"] = nc.dram_tensor("out_0", (N, HID), _mybir.dt.float32, kind="ExternalOutput").ap()
    build(nc, io)
    r = _run(nc, [arrays], core_ids=[0])
    return r.results[0]["out_0"]
```

```python
from contextlib import ExitStack

import concourse.bass as bass
from concourse import mybir

F32 = mybir.dt.float32
BF16 = mybir.dt.bfloat16
F32R = mybir.dt.float32r
I32 = mybir.dt.int32
ALU = mybir.AluOpType
ACT = mybir.ActivationFunctionType
AX = mybir.AxisListType

P = 128
N, HID, E = 3125, 256, 53125
H, D = 4, 64
FF = 4 * HID
NB, BP = 25, 125
KC = HID // P
LT = 2
TL = LT * P
TILES = (E + TL - 1) // TL
TG, TP = 2, TILES // 2
STEPS = TILES + NB - 1
CP = 8
C = STEPS // CP
SG, SP_ = 2, STEPS // 2
W = LT * CP
CR = 4
RING = CR * CP
R = H * W
HW_ = D + 1
HALFW = H * HW_
KVW = 2 * HALFW
NEG = -1.0e30
FAR = 8192.0
PV_LAG = CP + 6
SUM_LAG = CP + 8
ADD_LAG = SUM_LAG + 1
NQ, NA, NO = 4, 2, 4
GU = 5
G = NB // GU
GN = GU * BP
HALF = (GN + 1) // 2
HALVES = [(0, HALF), (HALF, GN)]
NE = 8
GNP = GN + 1
HALF_P = HALF + HALF % 2
HALVES_P = [(0, HALF_P), (HALF_P, GNP)]
NP = 2 * NE
LN_EPS = 1e-5
BN_EPS = 1e-3
SCALE = float(D) ** -0.5


def held(eng, turn):
    eng.sem_inc(turn, 1)


def project(nc, ctx, io, keep):
    c = ExitStack()
    with c:
        def sb(name, shape, dt=F32):
            return c.enter_context(nc.sbuf_tensor(name, shape, dt))

        def pb(name, shape):
            return c.enter_context(nc.psum_tensor(name, shape, F32))

        def sem(name):
            return ctx.enter_context(nc.semaphore(name))

        xs = sb("xs", [BP, NB, HID])
        wqk = sb("wqk", [P, KC, 2 * HID])
        wvs = sb("wvs", [P, KC, 2 * HID])
        bqk = sb("bqk", [BP, 2 * HID])
        bvs = sb("bvs", [BP, 2 * HID])
        st = sb("st", [BP, NB, 6])
        mv = sb("mv", [BP, NB, 2])
        ve = sb("ve", [BP, NB])
        mh = sb("mh", [BP, NB])
        rs = sb("rs", [BP, NB])
        xn = sb("xn", [BP, 4, HID])
        xnT = sb("xnT", [P, 2, KC, BP])
        q32 = sb("q32", [BP, 2, HID])
        r32 = sb("r32", [BP, 2, HID])
        kvst = sb("kvst", [BP, 2, KVW])
        resst = sb("resst", [BP, 2, HID])
        rest = sb("rest", [BP, 2, HID])
        dint = sb("dint", [TP, TG, TL], I32)
        sint = sb("sint", [TP, TG, TL], I32)
        pint = sb("pint", [TP, TG, 1], I32)
        pf = sb("pf", [TP, TG, 1])
        ne = sb("ne", [TP, TG, TL])
        rec = sb("rec", [TP, TG, 3 * TL])
        io25 = sb("io25", [TP, NB], I32)
        io25f = sb("io25f", [TP, NB])
        before = sb("before", [TP, TG, NB])
        ioS = sb("ioS", [NB, STEPS], I32)
        ioSf = sb("ioSf", [NB, STEPS])
        ioG = sb("ioG", [SP_, SG], I32)
        ioGf = sb("ioGf", [SP_, SG])
        first = sb("first", [NB, 1])
        begun = sb("begun", [NB, STEPS])
        bs = sb("bs", [SP_, SG])
        bm = sb("bm", [SP_, SG])
        tidx = sb("tidx", [SP_, SG], I32)
        grec = sb("grec", [SP_, SG, 3 * TL])
        drel = sb("drel", [SP_, SG, TL])
        drelb = sb("drelb", [SP_, SG, TL], BF16)
        mins = sb("mins", [SP_, 3, LT, SG])
        n0row = sb("n0row", [1, LT * STEPS + 1])
        pbrow = sb("pbrow", [1, LT * STEPS])
        v1 = sb("v1", [P, LT * STEPS])
        v2 = sb("v2", [P, LT * STEPS])
        iop = sb("iop", [P, 1], I32)
        iof = sb("iof", [P, P], I32)

        psW = [[pb(f"psW{b}{k}", [P, 512]) for k in range(2)] for b in range(2)]
        psT = [pb(f"psT{b}", [P, 512]) for b in range(2)]
        psX = [pb(f"psX{b}", [P, 512]) for b in range(2)]

        s_x, s_w, s_b = [sem("s_x_first"), sem("s_x_rest")], sem("s_w"), sem("s_b")
        s_ed, s_rec, s_grec = sem("s_ed"), sem("s_rec"), sem("s_grec")
        s_drel = sem("s_drel")
        s_kvo = [sem("s_kvo0"), sem("s_kvo1")]
        s_reso = [sem("s_reso0"), sem("s_reso1")]
        s_init, s_iota, s_const = sem("s_init"), sem("s_iota"), sem("s_const")
        s_tab, s_tabpe = sem("s_tab"), sem("s_tabpe")
        s_st, s_mv, s_ve, s_rs = sem("s_st"), sem("s_mv"), sem("s_ve"), sem("s_rs")
        s_xn, s_tr, s_xt, s_pr = sem("s_xn"), sem("s_tr"), sem("s_xt"), sem("s_pr")
        s_q, s_rest, s_row, s_pad = sem("s_q"), sem("s_rest"), sem("s_row"), sem("s_pad")
        s_qh, s_r1, s_qm, s_ql = sem("s_qh"), sem("s_r1"), sem("s_qm"), sem("s_ql")

        ident, iotaF, iotaP, one = keep["ident"], keep["iotaF"], keep["iotaP"], keep["one"]
        ones = keep["ones"]
        q3 = keep["q3"]
        x_v = io["x"].rearrange("(t p) d -> p t d", p=BP)
        kv_v = io["kv"].rearrange("(t p) d -> p t d", p=BP)
        res_v = io["res"].rearrange("(t p) d -> p t d", p=BP)
        rec_v = io["rec"].rearrange("(g p) d -> p g d", p=TP)
        drel_v = io["drel"].rearrange("(g p) d -> p g d", p=SP_)
        dst, src = io["dst"], io["src"]
        FULL = TP * TL
        LAST = (TILES - 1) * TL

        FB = 5
        NR = 4

        def tour(eng, at):
            for p in range(2 * NR):
                at(p // NR, p % NR)
            with eng.Fori(2, NB // NR - 1) as i:
                for j in range(NR):
                    at(i, j)
            for p in range(NR * (NB // NR - 1), NB):
                at(p // NR, p % NR)

        def exists(i, j, ahead):
            return not isinstance(i, int) or NR * i + j + ahead < NB

        def is_place(i, j, p):
            return isinstance(i, int) and NR * i + j == p

        def by_step(row):
            return row.rearrange("p (s l) -> p l s", l=LT)

        def as_made(ps, n):
            return ps[0:n, 0:LT * STEPS].rearrange("p (l s) -> p l s", l=LT)

        block = c.enter_context(nc.Block())

        @block.sync
        def _(sp):
            sp.dma_start(xs[:, 0:FB, :], x_v[:, 0:FB, :]).then_inc(s_x[0], 16)
            for w, a, b in ((wqk, "L0_gnn_Wq", "L0_gnn_Wk"), (wvs, "L0_gnn_Wv", "L0_gnn_Wskip")):
                sp.dma_start(w[:, :, 0:HID], io[a].rearrange("(k p) n -> p k n", p=P)).then_inc(s_w, 16)
                sp.dma_start(w[:, :, HID:2 * HID], io[b].rearrange("(k p) n -> p k n", p=P)).then_inc(s_w, 16)
            for t, a, b in ((bqk, "L0_gnn_bq", "L0_gnn_bk"), (bvs, "L0_gnn_bv", "L0_gnn_bskip")):
                sp.dma_start(t[:, 0:HID], io[a].partition_broadcast(BP)).then_inc(s_b, 16)
                sp.dma_start(t[:, HID:2 * HID], io[b].partition_broadcast(BP)).then_inc(s_b, 16)
            sp.dma_start(xs[:, FB:NB, :], x_v[:, FB:NB, :]).then_inc(s_x[1], 16)
            sp.wait_ge(s_init, 3)
            for t, a in ((dint, dst), (sint, src)):
                sp.dma_start(t[:, 0, :], a[0:FULL].rearrange("(p l) -> p l", l=TL)).then_inc(s_ed, 16)
                sp.dma_start(t[0:TP - 1, 1, :], a[FULL:LAST].rearrange("(p l) -> p l", l=TL)).then_inc(s_ed, 16)
                sp.dma_start(t[TP - 1:TP, 1, 0:E - LAST], a[LAST:E].rearrange("(p l) -> p l", p=1)).then_inc(s_ed, 16)
            lasts = dst[0:LAST].rearrange("(t l) -> t l", l=TL)[:, TL - 1:TL]
            with nc.allow_non_contiguous_dma(reason="one word per edge tile"):
                sp.dma_start(pint[1:TP, 0, :], lasts[0:TP - 1, :]).then_inc(s_ed, 16)
                for g in range(1, TG):
                    sp.dma_start(pint[0:TP, g, :], lasts[g * TP - 1:(g + 1) * TP - 1, :]).then_inc(s_ed, 16)

            def store(t, b):
                sp.wait_ge(s_row, t + 1)
                sp.dma_start(kv_v[:, t, :], kvst[:, b, :]).then_inc(s_kvo[b], 16)
                sp.dma_start(res_v[:, t, :], resst[:, b, :]).then_inc(s_reso[b], 16)

            store(0, 0)
            store(1, 1)
            sp.wait_ge(s_tab, 6)
            sp.dma_start(rec_v, rec[:, :, :]).then_inc(s_rec, 16)
            with sp.Fori(2, NB - 1, 2) as t:
                store(t, 0)
                store(t + 1, 1)
            store(NB - 1, 0)
            sp.wait_ge(s_tab, 18)
            sp.dma_start(drel_v, drelb[:, :, :]).then_inc(s_drel, 16)
            sp.wait_ge(s_drel, 16)
            for b in range(2):
                sp.wait_ge(s_kvo[b], 16 * ((NB + 1 - b) // 2))
                sp.wait_ge(s_reso[b], 16 * ((NB + 1 - b) // 2))

        @block.gpsimd
        def _(pool):
            nc.gpsimd.memset(dint[:, :, :], int(FAR)).then_inc(s_init, 1)
            nc.gpsimd.memset(sint[:, :, :], 0).then_inc(s_init, 1)
            nc.gpsimd.memset(pint[:, :, :], -1).then_inc(s_init, 1)
            nc.gpsimd.iota(io25[:, :], pattern=[[BP, NB]], base=0, channel_multiplier=0).then_inc(s_iota, 1)
            nc.gpsimd.iota(ioS[:, :], pattern=[[1, STEPS]], base=0, channel_multiplier=0).then_inc(s_iota, 1)
            nc.gpsimd.iota(ioG[:, :], pattern=[[SP_, SG]], base=0, channel_multiplier=1).then_inc(s_iota, 1)
            nc.gpsimd.iota(iop[:, :], pattern=[[0, 1]], base=0, channel_multiplier=1).then_inc(s_iota, 1)
            nc.gpsimd.iota(iof[:, :], pattern=[[1, P]], base=0, channel_multiplier=0).then_inc(s_iota, 1)
            nc.gpsimd.memset(mh[:, :], -0.5).then_inc(s_pad, 1)
            nc.gpsimd.memset(kvst[:, :, :], 0.0).then_inc(s_pad, 1)
            pool.wait_ge(s_pad, 1)
            for k, (a, b) in enumerate(((0, FB), (FB, NB))):
                pool.wait_ge(s_mv, b)
                nc.gpsimd.tensor_scalar(ve[:, a:b], mv[:, a:b, 1], LN_EPS, None, ALU.add).then_inc(s_ve, 1)
                pool.wait_ge(s_ve, k + 1)
                nc.gpsimd.tensor_tensor(rs[:, a:b], ve[:, a:b], mh[:, a:b], ALU.pow).then_inc(s_rs, 1)

            def split(t, b):
                pool.wait_ge(s_qh, t + 1)
                nc.gpsimd.tensor_tensor(r32[:, b, :], q32[:, b, :], q3[:, 0, bass.ds(t, 1), :].rearrange("p a d -> p (a d)"),
                                        ALU.subtract).then_inc(s_r1, 1)
                pool.wait_ge(s_qm, t + 1)
                nc.gpsimd.tensor_tensor(q3[:, 2, bass.ds(t, 1), :].rearrange("p a d -> p (a d)"), r32[:, b, :],
                                        q3[:, 1, bass.ds(t, 1), :].rearrange("p a d -> p (a d)"),
                                        ALU.subtract).then_inc(s_ql, 1)

            for t in range(2 * NR):
                split(t, t % 2)
            pool.wait_ge(s_tab, 15)
            pool.wait_ge(s_rec, 16)
            for g in range(SG):
                nc.gpsimd.indirect_dma_start(
                    out=grec[:, g, :], out_offset=None, in_=io["rec"],
                    in_offset=bass.IndirectOffsetOnAxis(ap=tidx[:, g:g + 1], axis=0)).then_inc(s_grec, 16)
            nc.gpsimd.memset(keep["acc"][:, :, :], 0.0)
            with pool.Fori(2 * NR, NB - 1, 2) as t:
                split(t, 0)
                split(t + 1, 1)
            split(NB - 1, 0)

        @block.scalar
        def _(act):
            def part(t, b):
                act.wait_ge(s_tr, t + 1)
                nc.scalar.activation(xnT[:, b, :, :], psT[b][:, 0:KC * BP].rearrange("p (k n) -> p k n", k=KC),
                                     ACT.Copy).then_inc(s_xt, 1)

            def high(t, b):
                act.wait_ge(s_q, t + 1)
                nc.scalar.activation(q3[:, 0, bass.ds(t, 1), :].rearrange("p a d -> p (a d)"), q32[:, b, :],
                                     ACT.Copy).then_inc(s_qh, 1)

            def middle(t, b):
                act.wait_ge(s_r1, t + 1)
                nc.scalar.activation(q3[:, 1, bass.ds(t, 1), :].rearrange("p a d -> p (a d)"), r32[:, b, :],
                                     ACT.Copy).then_inc(s_qm, 1)

            def at(i, j):
                t, b = NR * i + j, j % 2
                if exists(i, j, 2):
                    part(t + 2, b)
                high(t, b)
                middle(t, b)

            part(0, 0)
            part(1, 1)
            tour(act, at)
            act.wait_ge(s_tabpe, 3)
            nc.scalar.activation(by_step(keep["srcI"][:, :]), as_made(psW[0][0], P), ACT.Copy)
            nc.scalar.activation(by_step(keep["startN"][:, :]), as_made(psW[1][0], P), ACT.Copy)
            act.wait_ge(s_tab, 26)
            for h in range(H):
                for l in range(LT):
                    nc.scalar.activation(keep["fwd"][:, :, h, 1 + l:W + 1:LT],
                                         psT[0][0:1, l * STEPS:(l + 1) * STEPS].rearrange("p (c j) -> p c j", c=C), ACT.Copy)

        @block.tensor
        def _(pe):
            pe.wait_ge(s_w, 64)

            def rows(t, n):
                pe.wait_ge(s_xn, t + 1)
                for k in range(KC):
                    last = nc.tensor.transpose(psT[n % 2][:, k * BP:(k + 1) * BP], xn[:, n, k * P:(k + 1) * P],
                                               ident[0:BP, 0:BP])
                last.then_inc(s_tr, 1)

            def products(t, b, fresh):
                pe.wait_ge(s_xt, t + 1)
                if not fresh:
                    pe.wait_ge(s_row, t - 1)
                for w, ps in ((wqk, psW[b][0]), (wvs, psW[b][1])):
                    for k in range(KC):
                        last = nc.tensor.matmul(ps[0:BP, :], xnT[:, b, k, :], w[:, k, :], start=(k == 0), stop=(k == KC - 1))
                last.then_inc(s_pr, 1)

            def at(i, j):
                if exists(i, j, 1):
                    rows(NR * i + j + 1, (j + 1) % NR)
                products(NR * i + j, j % 2, isinstance(i, int) and NR * i + j < 2)
                if is_place(i, j, 3):
                    pe.wait_ge(s_tab, 7)
                    for g in range(TG):
                        last = nc.tensor.matmul(psX[0][0:NB, 0:1], before[:, g, :], ones[0:TP, 0:1],
                                                start=(g == 0), stop=(g == TG - 1))
                    last.then_inc(s_tabpe, 1)
                if is_place(i, j, 5):
                    pe.wait_ge(s_tab, 9)
                    for g in range(SG):
                        nc.tensor.matmul(psX[1][0:SP_, g:g + 1], begun[:, g * SP_:(g + 1) * SP_], ones[0:NB, 0:1],
                                         start=True, stop=True)
                    nc.tensor.matmul(psX[0][0:1, 0:STEPS], ones[0:NB, 0:1], begun[:, :], start=True, stop=True).then_inc(s_tabpe, 1)

            pe.wait_ge(s_const, 4)
            rows(0, 0)
            tour(pe, at)

            pe.wait_ge(s_tab, 24)
            pe.wait_ge(s_row, NB)
            for k, ps in ((0, psW[0][0]), (1, psW[0][1]), (2, psW[1][0])):
                for l in range(LT):
                    for g in range(SG):
                        a = drel[:, g, l * P:(l + 1) * P] if k == 1 else grec[:, g, k * TL + l * P:k * TL + (l + 1) * P]
                        at = l * STEPS + g * SP_
                        nc.tensor.transpose(ps[:, at:at + SP_], a, ident[0:SP_, 0:SP_])
            for k, ps in ((0, psT[0]), (1, psT[1]), (2, psW[1][1])):
                for l in range(LT):
                    for g in range(SG):
                        at = l * STEPS + g * SP_
                        last = nc.tensor.matmul(ps[0:1, at:at + SP_], mins[:, k, l, g:g + 1], ident[0:SP_, 0:SP_],
                                                start=True, stop=True)
            last.then_inc(s_tabpe, 1)

        @block.vector
        def _(dve):
            dve.wait_ge(s_iota, 5)
            nc.vector.tensor_copy(iotaP[:, :], iop[:, :]).then_inc(s_const, 1)
            nc.vector.tensor_copy(iotaF[:, :], iof[:, :]).then_inc(s_const, 1)
            nc.vector.memset(ones[:, :], 1.0).then_inc(s_const, 1)
            dve.wait_ge(s_const, 3)
            nc.vector.tensor_scalar(ident[:, :], iotaF[:, :], iotaP[:, 0:1], None, ALU.is_equal).then_inc(s_const, 1)
            def statistics(k, a, b):
                dve.wait_ge(s_x[k], 16)
                for t in range(a, b):
                    nc.vector.bn_stats(st[:, t, :], xs[:, t, :]).then_inc(s_st, 1)
                dve.wait_ge(s_st, b)
                for t in range(a, b):
                    nc.vector.bn_aggr(mv[:, t, :], st[:, t, :]).then_inc(s_mv, 1)

            def rest_of_statistics():
                statistics(1, FB, NB)

            def records():
                dve.wait_ge(s_ed, 128)
                nc.vector.tensor_copy(rec[:, :, 0:TL], sint[:, :, :]).then_inc(s_tab, 1)
                nc.vector.tensor_copy(rec[:, :, TL:2 * TL], dint[:, :, :]).then_inc(s_tab, 1)
                nc.vector.tensor_copy(pf[:, :, :], pint[:, :, :]).then_inc(s_tab, 1)
                dve.wait_ge(s_tab, 3)
                nc.vector.tensor_tensor(ne[:, :, 1:TL], rec[:, :, TL + 1:2 * TL], rec[:, :, TL:2 * TL - 1], ALU.not_equal).then_inc(s_tab, 1)
                nc.vector.tensor_tensor(ne[:, :, 0:1], rec[:, :, TL:TL + 1], pf[:, :, :], ALU.not_equal).then_inc(s_tab, 1)
                dve.wait_ge(s_tab, 5)
                nc.vector.tensor_scalar(rec[:, :, 2 * TL:3 * TL], ne[:, :, :], NEG, None, ALU.mult).then_inc(s_tab, 1)
                nc.vector.tensor_copy(io25f[:, :], io25[:, :]).then_inc(s_const, 1)
                nc.vector.tensor_copy(ioSf[:, :], ioS[:, :]).then_inc(s_const, 1)
                nc.vector.tensor_copy(ioGf[:, :], ioG[:, :]).then_inc(s_const, 1)
                dve.wait_ge(s_const, 7)
                nc.vector.tensor_tensor(before[:, :, :], io25f[:, :].unsqueeze(1).broadcast_to([TP, TG, NB]),
                                        rec[:, :, 2 * TL - 1:2 * TL].broadcast_to([TP, TG, NB]), ALU.is_gt).then_inc(s_tab, 1)

            def firsts():
                dve.wait_ge(s_tabpe, 1)
                nc.vector.tensor_tensor(first[:, :], psX[0][0:NB, 0:1], iotaP[0:NB, :], ALU.add).then_inc(s_tab, 1)
                dve.wait_ge(s_tab, 8)
                nc.vector.tensor_scalar(begun[:, :], ioSf[:, :], first[:, 0:1], None, ALU.is_ge).then_inc(s_tab, 1)

            def tiles():
                dve.wait_ge(s_tabpe, 2)
                nc.vector.tensor_scalar(bs[:, :], psX[1][0:SP_, 0:SG], -1.0, None, ALU.add).then_inc(s_tab, 1)
                nc.vector.tensor_scalar(keep["brow"][:, :], psX[0][0:1, 0:STEPS], -1.0, None, ALU.add).then_inc(s_tab, 1)
                dve.wait_ge(s_tab, 11)
                nc.vector.tensor_tensor(tidx[:, :], ioGf[:, :], bs[:, :], ALU.subtract).then_inc(s_tab, 1)
                nc.vector.tensor_scalar(bm[:, :], bs[:, :], -float(BP), None, ALU.mult).then_inc(s_tab, 1)
                nc.vector.memset(n0row[:, :], NEG).then_inc(s_tab, 1)
                nc.vector.memset(one[:, :], 1.0).then_inc(s_tab, 1)


            def norm(t, b):
                nc.vector.tensor_scalar(xn[:, b, :], xs[:, t, :], mv[:, t, 0:1], rs[:, bass.ds(t, 1)],
                                        ALU.subtract, ALU.mult).then_inc(s_xn, 1)

            def rows(t, n, fresh):
                b = n % 2
                dve.wait_ge(s_pr, t + 1)
                if not fresh:
                    dve.wait_ge(s_r1, t - 1)
                    if b == 0:
                        dve.wait_ge(s_kvo[0], 8 * t)
                        dve.wait_ge(s_reso[0], 8 * t)
                    else:
                        dve.wait_ge(s_kvo[1], 8 * t - 8)
                        dve.wait_ge(s_reso[1], 8 * t - 8)
                nc.vector.tensor_tensor(rest[:, b, :], psW[b][1][0:BP, HID:2 * HID], xn[:, n, :], ALU.add).then_inc(s_rest, 1)
                nc.vector.tensor_tensor(q32[:, b, :], psW[b][0][0:BP, 0:HID], bqk[:, 0:HID], ALU.add).then_inc(s_q, 1)
                nc.vector.tensor_tensor(kvst[:, b, HALFW:HALFW + HID], psW[b][0][0:BP, HID:2 * HID], bqk[:, HID:2 * HID], ALU.add)
                nc.vector.tensor_tensor(kvst[:, b, 0:HALFW].rearrange("p (h e) -> p h e", h=H)[:, :, 0:D],
                                        psW[b][1][0:BP, 0:HID].rearrange("p (h d) -> p h d", h=H),
                                        bvs[:, 0:HID].rearrange("p (h d) -> p h d", h=H), ALU.add)
                dve.wait_ge(s_rest, t + 1)
                nc.vector.tensor_tensor(resst[:, b, :], rest[:, b, :], bvs[:, HID:2 * HID], ALU.add).then_inc(s_row, 1)

            def relative():
                dve.wait_ge(s_grec, 16 * SG)
                dve.wait_ge(s_tab, 15)
                for g in range(SG):
                    nc.vector.tensor_scalar(drel[:, g, :], grec[:, g, TL:2 * TL], bm[:, g:g + 1], None, ALU.add).then_inc(s_tab, 1)
                dve.wait_ge(s_tab, 17)
                nc.vector.tensor_copy(drelb[:, :, :], drel[:, :, :]).then_inc(s_tab, 1)
                for l in range(LT):
                    at = 2 * TL + l * P
                    nc.vector.tensor_reduce(mins[:, 0, l, :], grec[:, :, at:at + P], AX.X, ALU.min).then_inc(s_tab, 1)
                    nc.vector.tensor_reduce(mins[:, 1, l, :], grec[:, :, at + 1:at + P], AX.X, ALU.min).then_inc(s_tab, 1)
                    nc.vector.tensor_copy(mins[:, 2, l, :], grec[:, :, at]).then_inc(s_tab, 1)
                nc.vector.memset(keep["fwd"][:, :, :, 0:1], NEG).then_inc(s_tab, 1)
                nc.vector.memset(keep["bwd"][:, :, :, 0:1], NEG).then_inc(s_tab, 1)

            def at(i, j):
                t = NR * i + j
                if is_place(i, j, FB - 2):
                    dve.wait_ge(s_rs, 2)
                if exists(i, j, 2):
                    norm(t + 2, (j + 2) % NR)
                rows(t, j, isinstance(i, int) and t < 2)
                for p, work in ((1, rest_of_statistics), (2, records), (4, firsts), (6, tiles), (NB - 4, relative)):
                    if is_place(i, j, p):
                        work()

            statistics(0, 0, FB)
            dve.wait_ge(s_rs, 1)
            norm(0, 0)
            norm(1, 1)
            dve.wait_ge(s_b, 64)
            dve.wait_ge(s_pad, 2)
            tour(dve, at)

            dve.wait_ge(s_tabpe, 3)
            nc.vector.tensor_copy(by_step(keep["dstR"][:, :]), as_made(psW[0][1], P))
            nc.vector.tensor_scalar(by_step(v1[:, :]), as_made(psW[0][1], P), 0.0, NEG, ALU.is_lt, ALU.mult).then_inc(s_tab, 1)
            nc.vector.tensor_scalar(by_step(v2[:, :]), as_made(psW[0][1], P), BP - 1.0, NEG, ALU.is_gt, ALU.mult).then_inc(s_tab, 1)
            nc.vector.tensor_copy(by_step(n0row[:, 0:LT * STEPS]), as_made(psW[1][1], 1)).then_inc(s_tab, 1)
            nc.vector.tensor_copy(by_step(pbrow[:, :]), as_made(psT[1], 1)).then_inc(s_tab, 1)
            dve.wait_ge(s_tab, 30)
            nc.vector.tensor_tensor(keep["valN"][:, :], v1[:, :], v2[:, :], ALU.add)
            nxt = n0row[:, 1:LT * STEPS + 1].rearrange("p (c w) -> p c w", w=W)
            pasts = pbrow[:, :].rearrange("p (c w) -> p c w", w=W)
            nc.vector.tensor_copy(keep["nxt"][:, :, :], nxt)
            for h in range(H):
                nc.vector.tensor_tensor(keep["bwd"][:, :, h, 1:W + 1], pasts[:, :, ::-1], nxt[:, :, ::-1], ALU.add)


(V_ALPHA, V_F1, V_TAIL, V_CARRY, V_INH, V_CIN, V_F2, V_B1, V_HEAD, V_BACK, V_IV, V_FD, V_FMIN, V_NEXT, V_OH0, V_BIN, V_G,
 V_DIFF, V_FAC) = range(1, 20)
NV = 19
(T_IN, T_TAIL, T_CARRY, T_HEAD, T_IV, T_OUT, T_FAC) = range(1, 8)
NT = 7


def attend(nc, ctx, io, keep):
    c = ExitStack()
    with c:
        def sb(name, shape, dt=F32):
            return c.enter_context(nc.sbuf_tensor(name, shape, dt))

        def pb(name, shape):
            return c.enter_context(nc.psum_tensor(name, shape, F32))

        def sem(name):
            return ctx.enter_context(nc.semaphore(name))

        ident, iotaF, iotaP, one = keep["ident"], keep["iotaF"], keep["iotaP"], keep["one"]
        q3, acc, brow = keep["q3"], keep["acc"], keep["brow"]
        dstR, valN = keep["dstR"], keep["valN"]

        ring = sb("ring", [P, W, CR + 1, HALFW])
        idx = sb("idx", [P, 2, W], I32)
        stc = sb("stc", [P, 2, H, W])
        ohT = [sb(f"ohT{b}", [BP, W * P], BF16) for b in range(2)]
        noh = sb("noh", [BP, CR])
        oh = sb("oh", [P, NO, LT, BP])
        oh0 = sb("oh0", [1, BP])
        prod = sb("prod", [P, 2, LT * HID])
        alpha = sb("alpha", [P, 2, H, W])
        alm = sb("alm", [P, H, W])
        dif = sb("dif", [P, H, W])
        nrow = sb("nrow", [R, P + 1])
        F1 = sb("F1", [R, P])
        F2 = sb("F2", [R, P])
        B1 = sb("B1", [R, P])
        Gm = sb("Gm", [R, P])
        cin = sb("cin", [R, 1])
        bin_ = sb("bin_", [R, 1])
        tails = sb("tails", [1, H, W + 1])
        heads = sb("heads", [1, H, W + 1])
        carry = sb("carry", [1, H, W + 1])
        back = sb("back", [1, H, W + 1])
        iv = sb("iv", [1, H, W])
        inh = sb("inh", [1, H, W])
        fd = sb("fd", [1, H])
        fm = sb("fm", [1, H])
        fx = sb("fx", [1, H])
        fac = sb("fac", [BP, H])

        psQ = [pb(f"psQ{b}", [P, 512]) for b in range(NQ)]
        psA = [pb(f"psA{b}", [P, 512]) for b in range(NA)]
        psM = pb("psM", [P, 512])
        psR = pb("psR", [P, 512])

        s_set = sem("s_set")
        s_turn = [sem("s_turn_sp"), sem("s_turn_pool"), sem("s_turn_pe")]
        s_idx = sem("s_idx")
        s_kv = [sem(f"s_kv{k}") for k in range(CP)]
        s_bc = [sem(f"s_bc{b}") for b in range(2)]
        s_oht, s_noh = sem("s_oht"), sem("s_noh")
        s_qe, s_prod, s_alpha = sem("s_qe"), sem("s_prod"), sem("s_alpha")
        s_mv, s_mp = sem("s_maxv"), sem("s_maxp")
        s_nrow, s_exp, s_fx, s_resc = sem("s_nrow"), sem("s_exp"), sem("s_fx"), sem("s_rescaled")
        s_pvd = sem("s_pv_dve")
        s_pv, s_oh, s_agg, s_acc = sem("s_pv"), sem("s_oh"), sem("s_agg"), sem("s_acc")

        drel_row = io["drel"].rearrange("s l -> (s l)")
        block = c.enter_context(nc.Block())

        ROUNDS = STEPS // RING

        def walk(eng, at):
            for j in range(RING):
                at(0, j, True)
            with eng.Fori(1, ROUNDS) as i:
                for j in range(RING):
                    at(i, j, False)
            for place in range(RING * ROUNDS, STEPS + ADD_LAG):
                at(place // RING, place % RING, False)

        def live(i, j, fresh, lag=0):
            if fresh:
                return j >= lag
            return not isinstance(i, int) or RING * i + j - lag < STEPS

        def staged(i, j, fresh):
            return live(i, j - j % CP, fresh, CP)

        def shared(i, j):
            return isinstance(i, int) and RING * i + j >= STEPS

        @block.sync
        def _(sp):
            def fetch(cc, par, fresh):
                if not fresh:
                    sp.wait_ge(s_qe, CP * (cc - 1))
                    held(sp, s_turn[0])
                    sp.wait_ge(s_noh, cc - 1)
                    held(sp, s_turn[0])
                sp.dma_start(ohT[par][:, :], drel_row[bass.ds(cc * (W * P), W * P)].partition_broadcast(BP)
                             ).then_inc(s_bc[par], 16)

            for cc in range(CR):
                fetch(cc, cc % 2, cc < 2)
            with sp.Fori(1, ROUNDS) as i:
                for par in range(CR):
                    fetch(CR * i + par, par % 2, False)
            for cc in range(CR * ROUNDS, C):
                fetch(cc, cc % 2, False)

        @block.gpsimd
        def _(pool):
            def at(i, j, fresh):
                if not live(i, j, fresh):
                    return
                step = RING * i + j
                cc, par = CR * i + j // CP, j // CP % 2
                if j % CP == 0:
                    if not (fresh and j < 2 * CP):
                        pool.wait_ge(s_alpha, CP * (cc - 1))
                        held(pool, s_turn[1])
                        pool.wait_ge(s_mp, NT * (cc - 2) + T_IN)
                        held(pool, s_turn[1])
                    nc.gpsimd.tensor_copy(idx[:, par, :], keep["srcI"][:, bass.ds(W * cc, W)]).then_inc(s_idx, 1)
                    nc.gpsimd.tensor_copy(stc[:, par, :, :], keep["startN"][:, bass.ds(W * cc, W)].unsqueeze(1)
                                          .broadcast_to([P, H, W])).then_inc(s_idx, 1)
                    pool.wait_ge(s_idx, 2 * cc + 2)
                    held(pool, s_turn[1])
                if not (fresh and j < CP):
                    pool.wait_ge(s_prod, step - CP + 1)
                    held(pool, s_turn[1])
                if not (fresh and j < RING - CP):
                    pool.wait_ge(s_agg, step - (RING - CP) + 1)
                    held(pool, s_turn[1])
                for k in range(LT):
                    nc.gpsimd.indirect_dma_start(
                        out=ring[:, LT * (j % CP) + k, j // CP:j // CP + 2, :].rearrange("p t e -> p (t e)"),
                        out_offset=None, in_=io["kv"],
                        in_offset=bass.IndirectOffsetOnAxis(ap=idx[:, par, LT * (j % CP) + k:LT * (j % CP) + k + 1], axis=0)
                    ).then_inc(s_kv[j % CP], 16)

            walk(pool, at)

        @block.scalar
        def _(act):
            def at(i, j, fresh):
                m = CR * i + j // CP - 1
                jj = j % CP
                if staged(i, j, fresh):
                    if jj == 0:
                        act.wait_ge(s_mp, NT * m + T_IN)
                        nc.scalar.activation(nrow[:, 0:P], psM[0:R, P:2 * P], ACT.Copy).then_inc(s_nrow, 1)
                    if jj == 6:
                        act.wait_ge(s_mv, NV * m + V_FMIN)
                        nc.scalar.activation(fx[:, :], fm[:, :], ACT.Exp, scale=SCALE).then_inc(s_fx, 1)
                        act.wait_ge(s_mv, NV * m + V_DIFF)
                        out = ring[:, :, (j // CP - 1) % CR, :].rearrange("p w (h e) -> p h w e", h=H)[:, :, :, D]
                        nc.scalar.activation(out, dif[:, :, :], ACT.Exp, scale=SCALE).then_inc(s_exp, 1)
                if live(i, j, fresh, PV_LAG):
                    sj = (j - PV_LAG) % RING
                    bc = CR * i + (j - PV_LAG) // CP
                    act.wait_ge(s_exp, bc + 1)
                    for k in range(LT if shared(i, j) is False else 1):
                        for h in range(H):
                            row = ring[:, LT * (sj % CP) + k, sj // CP, h * HW_:(h + 1) * HW_]
                            last = nc.scalar.activation(row[:, 0:D], row[:, 0:D], ACT.Copy, scale=row[:, D:HW_])
                    last.then_inc(s_pv, 1)

            walk(act, at)

        @block.tensor
        def _(pe):
            def expand(i, j, fresh):
                step, cc, par, jj = RING * i + j, CR * i + j // CP, j // CP % 2, j % CP
                if jj == 0:
                    pe.wait_ge(s_oht, cc + 1)
                if not (fresh and j < NQ):
                    pe.wait_ge(s_prod, step - NQ + 1)
                blk = nc.tensor.value_load(brow[0:1, bass.ds(step, 1)], min_val=0, max_val=NB - 1)
                for k in range(LT):
                    w = LT * jj + k
                    for part in range(3):
                        last = nc.tensor.matmul(psQ[j % NQ][:, k * HID:(k + 1) * HID], ohT[par][:, w * P:(w + 1) * P],
                                                q3[:, part, bass.ds(blk, 1), :].rearrange("p a d -> p (a d)"),
                                                start=(part == 0), stop=(part == 2))
                last.then_inc(s_qe, 1)

            def rest(i, j, fresh):
                m = CR * i + j // CP - 1
                mpar = (j // CP - 1) % 2
                jj = j % CP if staged(i, j, fresh) else None
                if live(i, j, fresh, SUM_LAG):
                    b = RING * i + j - SUM_LAG
                    sj = (j - SUM_LAG) % RING
                    pe.wait_ge(s_pv, b + 1)
                    if isinstance(b, int) and b >= STEPS - PV_LAG:
                        pe.wait_ge(s_pvd, b - (STEPS - PV_LAG) + 1)
                    pe.wait_ge(s_oh, b + 1)
                    if not (fresh and j < SUM_LAG + NA):
                        pe.wait_ge(s_acc, b - NA + 1)
                    for k in range(LT):
                        last = nc.tensor.matmul(psA[sj % NA][0:BP, 0:HALFW], oh[:, sj % NO, k, :],
                                                ring[:, LT * (sj % CP) + k, sj // CP, :], start=(k == 0), stop=(k == LT - 1))
                    last.then_inc(s_agg, 1)
                if jj == 0:
                    pe.wait_ge(s_mv, NV * m + V_ALPHA)
                    pe.wait_ge(s_idx, 2 * m + 2)
                    held(pe, s_turn[2])
                    nc.tensor.transpose(psM[0:R, 0:P], alm[:, :, :].rearrange("p h w -> p (h w)"), ident[:, :])
                    nc.tensor.transpose(psM[0:R, P:2 * P], stc[:, mpar, :, :].rearrange("p h w -> p (h w)"),
                                        ident[:, :]).then_inc(s_mp, 1)
                if jj == 1:
                    pe.wait_ge(s_mv, NV * m + V_F1)
                    held(pe, s_turn[2])
                    nc.tensor.matmul(psR[0:1, 0:R], F1[:, P - 1:P], ident[0:R, 0:R], start=True, stop=True).then_inc(s_mp, 1)
                if jj == 2:
                    pe.wait_ge(s_mv, NV * m + V_INH)
                    nc.tensor.matmul(psR[0:R, 128:129], inh[:, :, :].rearrange("p h w -> p (h w)"), one[0:1, 0:1],
                                     start=True, stop=True).then_inc(s_mp, 1)
                if jj == 3:
                    pe.wait_ge(s_mv, NV * m + V_B1)
                    held(pe, s_turn[2])
                    nc.tensor.matmul(psR[0:1, 256:256 + R], B1[:, 0:1], ident[0:R, 0:R], start=True, stop=True).then_inc(s_mp, 1)
                if jj == 4:
                    pe.wait_ge(s_mv, NV * m + V_IV)
                    nc.tensor.matmul(psR[0:R, 384:385], iv[:, :, :].rearrange("p h w -> p (h w)"), one[0:1, 0:1],
                                     start=True, stop=True).then_inc(s_mp, 1)
                if jj == 5:
                    pe.wait_ge(s_mv, NV * m + V_G)
                    held(pe, s_turn[2])
                    nc.tensor.transpose(psM[:, 256:256 + R], Gm[:, :], ident[0:R, 0:R]).then_inc(s_mp, 1)
                if jj == 6:
                    pe.wait_ge(s_fx, m + 1)
                    pe.wait_ge(s_mv, NV * m + V_DIFF)
                    nc.tensor.matmul(psM[0:BP, 400:400 + H], oh0[:, :], fx[:, :], start=True, stop=True).then_inc(s_mp, 1)

            def at(i, j, fresh):
                if live(i, j, fresh):
                    expand(i, j, fresh)
                if j > 0:
                    rest(i, j - 1, fresh)
                elif not fresh:
                    rest(i - 1, RING - 1, False)

            walk(pe, at)

        @block.vector
        def _(dve):
            nc.vector.memset(nrow[:, P:P + 1], 0.0).then_inc(s_set, 1)
            nc.vector.memset(tails[:, :, :], NEG).then_inc(s_set, 1)
            nc.vector.memset(heads[:, :, :], NEG).then_inc(s_set, 1)
            dve.wait_ge(s_set, 3)

            def build(turn, cc, q):
                dve.wait_ge(s_bc[q % 2], 16 * turn + 16)
                nc.vector.tensor_scalar(ohT[q % 2][:, :], ohT[q % 2][:, :], iotaP[0:BP, 0:1], None, ALU.is_equal).then_inc(s_oht, 1)
                dve.wait_ge(s_oht, cc + 1)
                nc.vector.tensor_scalar(noh[:, q:q + 1], ohT[q % 2][:, 0:1], -1.0, 1.0, ALU.mult, ALU.add).then_inc(s_noh, 1)

            build(0, 0, 0)

            def maximum(i, j, part):
                m = CR * i + j // CP - 1
                mpar = (j // CP - 1) % 2
                mv, mp = NV * m, NT * m
                at = (j % CP, part)

                def seen(n):
                    dve.wait_ge(s_mv, mv + n)

                if at == (0, 0):
                    dve.wait_ge(s_alpha, CP * m + CP)
                    nc.vector.tensor_tensor(alm[:, :, :], alpha[:, mpar, :, :],
                                            valN[:, bass.ds(W * m, W)].unsqueeze(1).broadcast_to([P, H, W]), ALU.add).then_inc(s_mv, 1)
                if at == (1, 0):
                    dve.wait_ge(s_mp, mp + T_IN)
                    dve.wait_ge(s_nrow, m + 1)
                    nc.vector.tensor_tensor_scan(out=F1[:, :], data0=nrow[:, 0:P], data1=psM[0:R, 0:P], initial=NEG,
                                                 op0=ALU.add, op1=ALU.max).then_inc(s_mv, 1)
                if at == (2, 0):
                    dve.wait_ge(s_mp, mp + T_TAIL)
                    nc.vector.tensor_copy(tails[:, :, 1:W + 1], psR[0:1, 0:R].rearrange("p (h w) -> p h w", h=H)).then_inc(s_mv, 1)
                if at == (2, 1):
                    seen(V_TAIL)
                    nc.vector.tensor_tensor_scan(out=carry[:, :, :].rearrange("p h w -> p (h w)"),
                                                 data0=keep["fwd"][:, bass.ds(m, 1), :, :].rearrange("p c h w -> p (c h w)"),
                                                 data1=tails[:, :, :].rearrange("p h w -> p (h w)"),
                                                 initial=NEG, op0=ALU.add, op1=ALU.max).then_inc(s_mv, 1)
                if at == (2, 2):
                    seen(V_CARRY)
                    nc.vector.tensor_copy(inh[:, :, :], carry[:, :, 0:W]).then_inc(s_mv, 1)
                if at == (3, 0):
                    dve.wait_ge(s_mp, mp + T_CARRY)
                    nc.vector.tensor_copy(cin[:, :], psR[0:R, 128:129]).then_inc(s_mv, 1)
                if at == (3, 1):
                    seen(V_CIN)
                    nc.vector.tensor_tensor_scan(out=F2[:, :], data0=nrow[:, 0:P], data1=psM[0:R, 0:P], initial=cin[:, 0:1],
                                                 op0=ALU.add, op1=ALU.max).then_inc(s_mv, 1)
                if at == (3, 2):
                    seen(V_F2)
                    nc.vector.tensor_tensor_scan(out=B1[:, ::-1], data0=nrow[:, 1:P + 1][:, ::-1], data1=F2[:, ::-1], initial=NEG,
                                                 op0=ALU.add, op1=ALU.max).then_inc(s_mv, 1)
                if at == (4, 0):
                    dve.wait_ge(s_mp, mp + T_HEAD)
                    nc.vector.tensor_copy(heads[:, :, 0:W], psR[0:1, 256:256 + R].rearrange("p (h w) -> p h w", h=H)).then_inc(s_mv, 1)
                if at == (4, 1):
                    seen(V_HEAD)
                    nc.vector.tensor_tensor_scan(out=back[:, :, :].rearrange("p h w -> p (h w)")[:, ::-1],
                                                 data0=keep["bwd"][:, bass.ds(m, 1), :, :].rearrange("p c h w -> p (c h w)"),
                                                 data1=heads[:, :, :].rearrange("p h w -> p (h w)")[:, ::-1],
                                                 initial=NEG, op0=ALU.add, op1=ALU.max).then_inc(s_mv, 1)
                if at == (4, 2):
                    seen(V_BACK)
                    nc.vector.tensor_tensor(iv[:, :, :], back[:, :, 1:W + 1],
                                            keep["nxt"][:, bass.ds(m, 1), :].broadcast_to([1, H, W]), ALU.add).then_inc(s_mv, 1)
                    nc.vector.tensor_tensor(fd[:, :], tails[:, :, 0], back[:, :, 0], ALU.subtract).then_inc(s_mv, 1)
                if at == (5, 0):
                    seen(V_FD)
                    nc.vector.tensor_scalar(fm[:, :], fd[:, :], 0.0, None, ALU.min).then_inc(s_mv, 1)
                    nc.vector.tensor_copy(tails[:, :, 0], carry[:, :, W]).then_inc(s_mv, 1)
                    nc.vector.tensor_scalar(oh0[:, :], iotaF[0:1, 0:BP], dstR[0:1, bass.ds(W * m, 1)], None,
                                            ALU.is_equal).then_inc(s_mv, 1)
                    dve.wait_ge(s_mp, mp + T_IV)
                    nc.vector.tensor_copy(bin_[:, :], psR[0:R, 384:385]).then_inc(s_mv, 1)
                if at == (5, 1):
                    seen(V_BIN)
                    nc.vector.tensor_tensor_scan(out=Gm[:, ::-1], data0=nrow[:, 1:P + 1][:, ::-1], data1=F2[:, ::-1],
                                                 initial=bin_[:, 0:1], op0=ALU.add, op1=ALU.max).then_inc(s_mv, 1)
                if at == (6, 0):
                    dve.wait_ge(s_mp, mp + T_OUT)
                    nc.vector.tensor_tensor(dif[:, :, :], alm[:, :, :], psM[:, 256:256 + R].rearrange("p (h w) -> p h w", h=H),
                                            ALU.subtract).then_inc(s_mv, 1)
                if at == (7, 0):
                    dve.wait_ge(s_mp, mp + T_FAC)
                    at_noh = (j // CP - 1) % CR
                    nc.vector.tensor_scalar(fac[:, :], psM[0:BP, 400:400 + H], noh[:, at_noh:at_noh + 1], None,
                                            ALU.add).then_inc(s_mv, 1)

            def at(i, j, fresh):
                step = RING * i + j
                cc, q, jj = CR * i + j // CP, j // CP, j % CP
                now = staged(i, j, fresh)
                if live(i, j, fresh, ADD_LAG):
                    b = step - ADD_LAG
                    blk = nc.vector.value_load(brow[0:1, bass.ds(b, 1)], min_val=0, max_val=NB - 1)
                if live(i, j, fresh):
                    dve.wait_ge(s_kv[jj], 16 * LT * (cc + 1))
                    dve.wait_ge(s_qe, step + 1)
                    if not (fresh and j < 2):
                        dve.wait_ge(s_alpha, step - 1)
                    nc.vector.tensor_tensor(prod[:, j % 2, :].rearrange("p (k d) -> p k d", k=LT),
                                            psQ[j % NQ][:, :].rearrange("p (k d) -> p k d", k=LT),
                                            ring[:, LT * jj:LT * jj + LT, q + 1, 0:HID], ALU.mult).then_inc(s_prod, 1)
                if now:
                    maximum(i, j, 0)
                if shared(i, j) and live(i, j, fresh, PV_LAG):
                    bp = step - PV_LAG
                    sp_ = (j - PV_LAG) % RING
                    dve.wait_ge(s_exp, bp // CP + 1)
                    row = ring[:, LT * (sp_ % CP) + 1, sp_ // CP, :].rearrange("p (h e) -> p h e", h=H)
                    nc.vector.tensor_tensor(row[:, :, 0:D], row[:, :, 0:D], row[:, :, D:HW_].broadcast_to([P, H, D]),
                                            ALU.mult).then_inc(s_pvd, 1)
                if live(i, j, fresh, SUM_LAG - 1):
                    bo = step - SUM_LAG + 1
                    sj = (j - SUM_LAG + 1) % RING
                    if not (fresh and j < SUM_LAG - 1 + NO):
                        dve.wait_ge(s_agg, bo - NO + 1)
                    nc.vector.tensor_tensor(oh[:, sj % NO, :, :], iotaF[:, 0:BP].unsqueeze(1).broadcast_to([P, LT, BP]),
                                            dstR[:, bass.ds(LT * bo, LT)].unsqueeze(2).broadcast_to([P, LT, BP]),
                                            ALU.is_equal).then_inc(s_oh, 1)
                if now:
                    maximum(i, j, 1)
                if jj == 6 and live(i, j, fresh, -CP):
                    build(2 * i + (q + 1) // 2, cc + 1, (q + 1) % CR)
                if live(i, j, fresh, ADD_LAG):
                    sj = (j - ADD_LAG) % RING
                    dve.wait_ge(s_agg, b + 1)
                    if not (fresh and j < ADD_LAG + 1):
                        dve.wait_ge(s_acc, b)
                    if sj % CP == 0:
                        dve.wait_ge(s_resc, CR * i + (j - ADD_LAG) // CP + 1)
                    row = acc[:, bass.ds(blk, 1), :].rearrange("p a d -> p (a d)")
                    nc.vector.tensor_tensor(row, row, psA[sj % NA][0:BP, 0:HALFW], ALU.add).then_inc(s_acc, 1)
                if now:
                    maximum(i, j, 2)
                if live(i, j, fresh):
                    dve.wait_ge(s_prod, step + 1)
                    nc.vector.tensor_reduce(alpha[:, q % 2, :, LT * jj:LT * jj + LT].rearrange("p h w -> p w h"),
                                            prod[:, j % 2, :].rearrange("p (k h d) -> p k h d", k=LT, h=H), AX.X, ALU.add
                                            ).then_inc(s_alpha, 1)
                if (j - ADD_LAG + 1) % CP == 0 and live(i, j, fresh, ADD_LAG - 1):
                    br = step - ADD_LAG + 1
                    m = CR * i + (j - ADD_LAG + 1) // CP
                    blk = nc.vector.value_load(brow[0:1, bass.ds(br, 1)], min_val=0, max_val=NB - 1)
                    dve.wait_ge(s_mv, NV * m + V_FAC)
                    if not (fresh and j < ADD_LAG):
                        dve.wait_ge(s_acc, br)
                    row = acc[:, bass.ds(blk, 1), :].rearrange("p a (h e) -> p (a h) e", h=H)
                    nc.vector.tensor_tensor(row, row, fac[:, :].unsqueeze(2).broadcast_to([BP, H, HW_]), ALU.mult).then_inc(s_resc, 1)

            walk(dve, at)


def mlp(nc, ctx, io, keep):
    c = ExitStack()
    with c:
        def sb(name, shape, dt=F32):
            return c.enter_context(nc.sbuf_tensor(name, shape, dt))

        def pb(name, shape):
            return c.enter_context(nc.psum_tensor(name, shape, F32))

        def sem(name):
            return ctx.enter_context(nc.semaphore(name))

        ident, acc, mv3 = keep["ident"], keep["acc"], keep["mv3"]
        FC = FF // P
        x1 = sb("x1", [BP, NB, HID])
        w1 = sb("w1", [P, KC, FF])
        w2 = sb("w2", [P, FC, HID])
        b1r = sb("b1r", [FC, P])
        b1c = sb("b1c", [P, FC])
        g1b = sb("g1b", [BP, HID])
        be1 = sb("be1", [BP, HID])
        b2b = sb("b2b", [BP, HID])
        g2b = sb("g2b", [BP, HID])
        be2 = sb("be2", [BP, HID])
        rec = sb("recden", [BP, NB, H])
        den = sb("den", [BP, NB, H])
        res = sb("resin", [BP, GU, HID])
        xin = sb("xin", [BP, GU, HID])
        y = sb("y", [BP, GU, HID])
        z = sb("z", [BP, GU, HID])
        h = sb("h", [BP, GU, HID])
        hT = sb("hT", [P, KC, GN])
        gT = sb("gT", [P, FC, GN])
        st = sb("st1", [BP, GU, 6])
        mv = sb("mv1", [BP, GU, 2])
        ve = sb("ve1", [BP, 3, GU])
        rs = sb("rs1", [BP, 3, GU])
        mh = sb("mh1", [BP, GU])
        st2 = sb("st2", [BP, GU, 6])
        prm = sb("prm", [NP, 8, P])
        vf = sb("vf", [P, 2, 16])
        mhv = sb("mhv", [P, 2, 16])
        hv = sb("hv", [NP, 2, P])
        tmp = sb("tmp", [NP, 2, P])
        sc = sb("sc", [NP, 4, P])
        mv2 = sb("mv2", [BP, GU, 2])
        mvs = sb("mvs", [BP, GU, 2])

        psT = [pb(f"psT2{b}", [P, 512]) for b in range(2)]
        psF = [pb(f"psF{b}", [P, 512]) for b in range(3)]
        psO = [pb(f"psO{b}", [P, 512]) for b in range(2)]
        psB = pb("psB", [P, 512])

        s_w1, s_w2, s_row, s_half = sem("m_w1"), sem("m_w2"), sem("m_row"), sem("m_half")
        s_res, s_xin = sem("m_res"), sem("m_xin")
        s_den, s_resu, s_xinu = sem("m_den"), sem("m_resu"), sem("m_xinu")
        s_ln1, s_mv1, s_rs1, s_h, s_hb = sem("m_ln1"), sem("m_mv1"), sem("m_rs1"), sem("m_h"), sem("m_hb")
        s_ve1, s_ve2 = sem("m_ve1"), sem("m_ve2")
        s_tr, s_hT, s_ff, s_ge, s_fo = sem("m_tr"), sem("m_hT"), sem("m_ff"), sem("m_ge"), sem("m_fo")
        s_y, s_ln2, s_mv2, s_rs2, s_x1, s_mv3 = sem("m_y"), sem("m_ln2"), sem("m_mv2"), sem("m_rs2"), sem("m_x1"), sem("m_mv3")
        s_turn = [sem("m_turn_pool"), sem("m_turn_dve")]
        s_mvs, s_ve3, s_rs3, s_xb, s_xg0 = sem("m_mvs"), sem("m_ve3"), sem("m_rs3"), sem("m_xb"), sem("m_xg0")
        s_prm, s_vf, s_vs, s_hv, s_hvd, s_hvl = sem("m_prm"), sem("m_vf"), sem("m_vs"), sem("m_hv"), sem("m_hvd"), sem("m_hvl")
        s_sc, s_tm, s_scp, s_scT = sem("m_sc"), sem("m_tm"), sem("m_scp"), sem("m_scT")
        s_bt, s_bc, s_st3, s_x1o = sem("m_bt"), sem("m_bc"), sem("m_st3"), sem("m_x1o")

        res_v = io["res"].rearrange("(g u p) d -> p g u d", p=BP, u=GU)
        x_v = io["x"].rearrange("(g u p) d -> p g u d", p=BP, u=GU)
        x1_v = io["x1"].rearrange("(g u p) d -> p g u d", p=BP, u=GU)
        block = c.enter_context(nc.Block())

        @block.sync
        def _(sp):
            def group(g, fresh):
                if not fresh:
                    sp.wait_ge(s_resu, g)
                sp.dma_start(res[:, :, :], res_v[:, bass.ds(g, 1), :, :].rearrange("p g u d -> p (g u) d")).then_inc(s_res, 16)
                if not fresh:
                    sp.wait_ge(s_xinu, g)
                sp.dma_start(xin[:, :, :], x_v[:, bass.ds(g, 1), :, :].rearrange("p g u d -> p (g u) d")).then_inc(s_xin, 16)

            group(0, True)
            for k, a in enumerate(("v1", "v2")):
                sp.dma_start(vf[:, k, :], io["L0_ffn_" + a].rearrange("e (a b) -> (e a) b", b=16)).then_inc(s_vf, 16)
            for t, a in ((g1b, "ln1_g"), (be1, "ln1_b"), (b2b, "b2"), (g2b, "ln2_g"), (be2, "ln2_b")):
                sp.dma_start(t[:, :], io["L0_gnn_" + a].partition_broadcast(BP)).then_inc(s_row, 16)
            sp.dma_start(b1r[:, :], io["L0_gnn_b1"].rearrange("(c p) -> c p", p=P)).then_inc(s_row, 16)
            sp.dma_start(w1[:, :, :], io["L0_gnn_W1"].rearrange("(k p) n -> p k n", p=P)).then_inc(s_w1, 16)
            sp.dma_start(w2[:, :, :], io["L0_gnn_W2"].rearrange("(k p) n -> p k n", p=P)).then_inc(s_w2, 16)
            for k, a in enumerate(("b1", "g1", "be1", "m1", "b2", "g2", "be2", "m2")):
                sp.dma_start(prm[:, k, :], io["L0_ffn_" + a].rearrange("e (m p) -> (e m) p", p=P)).then_inc(s_prm, 16)
            sp.wait_ge(s_hv, 1)
            sp.dma_start(io["roots"].rearrange("l (q b) -> q l b", b=16), vf[:, :, :]).then_inc(s_hvd, 16)
            sp.wait_ge(s_hvd, 16)
            sp.dma_start(hv[:, :, :], io["roots"].rearrange("l (r p) -> r l p", p=P)).then_inc(s_hvl, 16)

            def store(g):
                sp.wait_ge(s_xinu, g + 1)
                sp.dma_start(x1_v[:, bass.ds(g, 1), :, :].rearrange("p g u d -> p (g u) d"),
                             x1[:, bass.ds(GU * g, GU), :]).then_inc(s_x1o, 16)

            with sp.Fori(1, G) as g:
                group(g, False)
                store(g - 1)
            store(G - 1)
            sp.wait_ge(s_x1o, 16 * G)

        @block.gpsimd
        def _(pool):
            nc.gpsimd.memset(mh[:, :], -0.5).then_inc(s_half, 1)
            nc.gpsimd.memset(mhv[:, :, :], -0.5).then_inc(s_half, 1)
            pool.wait_ge(s_half, 2)

            def root(g, k, m, s_m, s_v, s_r, out=None):
                pool.wait_ge(s_m, GU * g + GU)
                held(pool, s_turn[0])
                nc.gpsimd.tensor_scalar(ve[:, k, :], m[:, :, 1], LN_EPS, None, ALU.add).then_inc(s_v, 1)
                pool.wait_ge(s_v, g + 1)
                nc.gpsimd.tensor_tensor(rs[:, k, :] if out is None else out, ve[:, k, :], mh[:, :], ALU.pow).then_inc(s_r, 1)

            def root3(g):
                root(g, 2, mvs, s_mvs, s_ve3, s_rs3, keep["rs3"][:, bass.ds(GU * g, GU)])

            root(0, 0, mv, s_mv1, s_ve1, s_rs1)
            pool.wait_ge(s_vf, 32)
            nc.gpsimd.tensor_scalar(vf[:, :, :], vf[:, :, :], BN_EPS, None, ALU.add).then_inc(s_vs, 1)
            pool.wait_ge(s_vs, 1)
            nc.gpsimd.tensor_tensor(vf[:, :, :], vf[:, :, :], mhv[:, :, :], ALU.pow).then_inc(s_hv, 1)
            with pool.Fori(0, G - 1) as g:
                root(g + 1, 0, mv, s_mv1, s_ve1, s_rs1)
                root(g, 1, mv2, s_mv2, s_ve2, s_rs2)
                root3(g)
            root(G - 1, 1, mv2, s_mv2, s_ve2, s_rs2)
            root3(G - 1)

        @block.scalar
        def _(act):
            def columns(g):
                for u in range(GU):
                    act.wait_ge(s_tr, GU * g + u + 1)
                    nc.scalar.activation(hT[:, :, u * BP:(u + 1) * BP],
                                         psT[u % 2][:, 0:KC * BP].rearrange("p (k n) -> p k n", k=KC), ACT.Copy).then_inc(s_hT, 1)

            def gelu(g, fresh):
                if not fresh:
                    act.wait_ge(s_fo, GU * g)
                for n, (m, (a, b)) in enumerate((m, ab) for m in range(FC) for ab in HALVES):
                    act.wait_ge(s_ff, 2 * FC * g + n + 1)
                    nc.scalar.activation(gT[:, m, a:b], psF[n % 3][:, 0:b - a], ACT.Gelu, bias=b1c[:, m:m + 1]).then_inc(s_ge, 1)

            columns(0)
            act.wait_ge(s_bc, 1)
            gelu(0, True)
            with act.Fori(1, G) as g:
                columns(g)
                gelu(g, False)

        @block.tensor
        def _(pe):
            def columns(g, fresh):
                for u in range(GU):
                    pe.wait_ge(s_h, GU * g + u + 1)
                    if not (fresh and u < 2):
                        pe.wait_ge(s_hT, GU * g + max(u - 1, 0))
                    for k in range(KC):
                        last = nc.tensor.transpose(psT[u % 2][:, k * BP:(k + 1) * BP], h[:, u, k * P:(k + 1) * P],
                                                   ident[0:BP, 0:BP])
                    last.then_inc(s_tr, 1)

            def first(g, fresh):
                pe.wait_ge(s_hT, GU * g + GU)
                for n, (m, (a, b)) in enumerate((m, ab) for m in range(FC) for ab in HALVES):
                    if not (fresh and n < 3):
                        pe.wait_ge(s_ge, 2 * FC * g + n - 2)
                    for k in range(KC):
                        last = nc.tensor.matmul(psF[n % 3][:, 0:b - a], w1[:, k, m * P:(m + 1) * P], hT[:, k, a:b],
                                                start=(k == 0), stop=(k == KC - 1))
                    last.then_inc(s_ff, 1)

            def second(g, fresh):
                pe.wait_ge(s_ge, 2 * FC * g + 2 * FC)
                for u in range(GU):
                    if not (fresh and u < 2):
                        pe.wait_ge(s_y, GU * g + max(u - 1, 0))
                    for m in range(FC):
                        last = nc.tensor.matmul(psO[u % 2][0:BP, 0:HID], gT[:, m, u * BP:(u + 1) * BP], w2[:, m, :],
                                                start=(m == 0), stop=(m == FC - 1))
                    last.then_inc(s_fo, 1)

            pe.wait_ge(s_row, 96)
            nc.tensor.transpose(psB[:, 0:FC], b1r[:, :], ident[0:FC, 0:FC]).then_inc(s_bt, 1)
            columns(0, True)
            pe.wait_ge(s_w1, 16)
            first(0, True)
            pe.wait_ge(s_w2, 16)
            pe.wait_ge(s_bc, 1)
            pe.wait_ge(s_sc, 6)
            for k in range(4):
                last = nc.tensor.transpose(psB[:, 64 + k * NP:64 + (k + 1) * NP], sc[:, k, :], ident[0:NP, 0:NP])
            last.then_inc(s_scp, 1)
            second(0, True)
            with pe.Fori(1, G) as g:
                columns(g, False)
                first(g, False)
                second(g, False)

        @block.vector
        def _(dve):
            wide = acc[:, :, :].rearrange("p t (h e) -> p t h e", h=H)
            nc.vector.tensor_scalar(den[:, :, :], wide[:, :, :, D], 1e-16, None, ALU.add).then_inc(s_den, 1)
            dve.wait_ge(s_den, 1)
            nc.vector.reciprocal(rec[:, :, :], den[:, :, :]).then_inc(s_den, 1)
            dve.wait_ge(s_den, 2)

            def rows(t):
                return t[:, :].unsqueeze(1).broadcast_to([BP, GU, HID])

            K1, K2 = 3 * GU, 2 * GU

            def norm1(g, part, fresh):
                if part == 0:
                    for u in range(GU):
                        nc.vector.tensor_tensor(
                            y[:, u, :].rearrange("p (h d) -> p h d", h=H),
                            acc[:, bass.ds(GU * g + u, 1), :].rearrange("p t (h e) -> p (t h) e", h=H)[:, :, 0:D],
                            rec[:, bass.ds(GU * g + u, 1), :].rearrange("p t h -> p (t h)").unsqueeze(2).broadcast_to([BP, H, D]),
                            ALU.mult).then_inc(s_ln1, 1)
                if part == 1:
                    dve.wait_ge(s_res, 16 * g + 16)
                    dve.wait_ge(s_ln1, K1 * g + GU)
                    nc.vector.tensor_tensor(y[:, :, :], y[:, :, :], res[:, :, :], ALU.add).then_inc(s_resu, 1)
                    dve.wait_ge(s_resu, g + 1)
                    for u in range(GU):
                        nc.vector.bn_stats(st[:, u, :], y[:, u, :]).then_inc(s_ln1, 1)
                if part == 2:
                    dve.wait_ge(s_ln1, K1 * g + 2 * GU)
                    held(dve, s_turn[1])
                    for u in range(GU):
                        nc.vector.bn_aggr(mv[:, u, :], st[:, u, :]).then_inc(s_mv1, 1)
                if part == 3:
                    dve.wait_ge(s_mv1, GU * g + GU)
                    if fresh:
                        dve.wait_ge(s_row, 96)
                    for u in range(GU):
                        nc.vector.scalar_tensor_tensor(out=y[:, u, :], in0=y[:, u, :], scalar=mv[:, u, 0:1], in1=g1b[:, :],
                                                       op0=ALU.subtract, op1=ALU.mult).then_inc(s_ln1, 1)
                if part == 4:
                    dve.wait_ge(s_ln1, K1 * g + 3 * GU)
                    dve.wait_ge(s_rs1, g + 1)
                    if not fresh:
                        dve.wait_ge(s_tr, GU * g)
                    for u in range(GU):
                        nc.vector.scalar_tensor_tensor(out=h[:, u, :], in0=y[:, u, :], scalar=rs[:, 0, u:u + 1], in1=be1[:, :],
                                                       op0=ALU.mult, op1=ALU.add).then_inc(s_h, 1)
                    dve.wait_ge(s_h, GU * g + GU)
                    nc.vector.tensor_tensor(x1[:, bass.ds(GU * g, GU), :], h[:, :, :], rows(b2b), ALU.add).then_inc(s_hb, 1)

            def statistics(g, u):
                dve.wait_ge(s_y, GU * g + u + 1)
                nc.vector.bn_stats(st2[:, u, :], z[:, u, :]).then_inc(s_ln2, 1)

            def added(g, u):
                if u == 0:
                    dve.wait_ge(s_hb, g + 1)
                dve.wait_ge(s_fo, GU * g + u + 1)
                nc.vector.tensor_tensor(z[:, u, :], psO[u % 2][0:BP, 0:HID],
                                        x1[:, bass.ds(GU * g + u, 1), :].rearrange("p t d -> p (t d)"), ALU.add).then_inc(s_y, 1)
                if u == 1:
                    dve.wait_ge(s_xin, 16 * g + 16)
                    nc.vector.tensor_tensor(xin[:, :, :], xin[:, :, :], rows(be2), ALU.add).then_inc(s_xb, 1)
                if u >= 1:
                    statistics(g, u - 1)

            def norm2(g):
                statistics(g, GU - 1)
                dve.wait_ge(s_ln2, K2 * g + GU)
                held(dve, s_turn[1])
                for u in range(GU):
                    nc.vector.bn_aggr(mv2[:, u, :], st2[:, u, :]).then_inc(s_mv2, 1)
                dve.wait_ge(s_mv2, GU * g + GU)
                for u in range(GU):
                    nc.vector.scalar_tensor_tensor(out=z[:, u, :], in0=z[:, u, :], scalar=mv2[:, u, 0:1], in1=g2b[:, :],
                                                   op0=ALU.subtract, op1=ALU.mult).then_inc(s_ln2, 1)
                dve.wait_ge(s_rs2, g + 1)
                dve.wait_ge(s_xb, g + 1)
                dve.wait_ge(s_ln2, K2 * g + 2 * GU)
                for u in range(GU):
                    last = nc.vector.scalar_tensor_tensor(
                        out=x1[:, bass.ds(GU * g + u, 1), :].rearrange("p t d -> p (t d)"), in0=z[:, u, :],
                        scalar=rs[:, 1, u:u + 1], in1=xin[:, u, :], op0=ALU.mult, op1=ALU.add)
                last.then_inc(s_xinu, 1)
                dve.wait_ge(s_xinu, g + 1)
                held(dve, s_turn[1])
                for u in range(GU):
                    nc.vector.bn_stats(st2[:, u, :], x1[:, bass.ds(GU * g + u, 1), :].rearrange("p t d -> p (t d)")).then_inc(s_st3, 1)
                dve.wait_ge(s_st3, GU * g + GU)
                held(dve, s_turn[1])
                for u in range(GU):
                    nc.vector.bn_aggr(mvs[:, u, :], st2[:, u, :]).then_inc(s_mvs, 1)
                dve.wait_ge(s_mvs, GU * g + GU)
                nc.vector.tensor_copy(mv3[:, bass.ds(GU * g, GU), :], mvs[:, :, :]).then_inc(s_mv3, 1)

            for part in range(5):
                norm1(0, part, True)
            dve.wait_ge(s_bt, 1)
            nc.vector.tensor_copy(b1c[:, :], psB[:, 0:FC]).then_inc(s_bc, 1)
            dve.wait_ge(s_prm, 128)
            dve.wait_ge(s_hvl, 16)
            for l in range(2):
                nc.vector.tensor_tensor(sc[:, 2 * l, :], prm[:, 4 * l + 1, :], hv[:, l, :], ALU.mult).then_inc(s_sc, 1)
                nc.vector.tensor_tensor(tmp[:, l, :], prm[:, 4 * l, :], prm[:, 4 * l + 3, :], ALU.subtract).then_inc(s_sc, 1)
            dve.wait_ge(s_sc, 4)
            for l in range(2):
                nc.vector.tensor_tensor(tmp[:, l, :], tmp[:, l, :], sc[:, 2 * l, :], ALU.mult).then_inc(s_tm, 1)
            dve.wait_ge(s_tm, 2)
            for l in range(2):
                nc.vector.tensor_tensor(sc[:, 2 * l + 1, :], tmp[:, l, :], prm[:, 4 * l + 2, :], ALU.add).then_inc(s_sc, 1)
            dve.wait_ge(s_scp, 1)
            nc.vector.tensor_copy(keep["scT"][:, :, :], psB[:, 64:64 + 4 * NP].rearrange("p (k n) -> p k n", k=4)).then_inc(s_scT, 1)
            with dve.Fori(0, G - 1) as g:
                for u in range(GU):
                    norm1(g + 1, u, False)
                    added(g, u)
                norm2(g)
            dve.wait_ge(s_rs3, 1)
            dve.wait_ge(s_mv3, 1)
            for u in range(GU):
                added(G - 1, u)
                nc.vector.tensor_scalar(keep["xg"][:, u, :], x1[:, u, :], mv3[:, u, 0:1], keep["rs3"][:, u:u + 1],
                                        ALU.subtract, ALU.mult).then_inc(s_xg0, 1)
            norm2(G - 1)


def experts(nc, ctx, io, keep):
    c = ExitStack()
    with c:
        def sb(name, shape, dt=F32):
            return c.enter_context(nc.sbuf_tensor(name, shape, dt))

        def pb(name, shape):
            return c.enter_context(nc.psum_tensor(name, shape, F32))

        def sem(name):
            return ctx.enter_context(nc.semaphore(name))

        ident, mv3, rs3, scT = keep["ident"], keep["mv3"], keep["rs3"], keep["scT"]
        wh = [sb(f"wh{l}", [P, NE, KC, HID], F32R) for l in range(3)]
        wl = [sb(f"wl{l}", [P, NE, KC, HID], F32R) for l in range(3)]
        we = sb("we", [P, 2, 3, KC, HID])
        wr = sb("wr", [P, KC, NE])
        wrh = sb("wrh", [P, KC, NE], F32R)
        wrl = sb("wrl", [P, KC, NE], F32R)
        br = sb("br", [BP, NE])
        bo = sb("bo", [NE, HID])
        xg = keep["xg"]
        xres = sb("xres", [BP, GU, HID])
        xf = sb("xf", [P, 2, KC, BP])
        xh = sb("xh", [P, KC, GNP], F32R)
        xl = sb("xl", [P, KC, GNP], F32R)
        lg = sb("lg", [BP, GU, NE])
        mx = sb("mx", [BP, GU])
        ex = sb("ex", [BP, GU, NE])
        sm = sb("sm", [BP, GU])
        wt = sb("wt", [BP, GU, NE])
        wT = sb("wT", [NE, GN])
        hf = sb("hf", [P, 4, HALF_P])
        h1h = sb("h1h", [P, 2, KC, GNP], F32R)
        h1l = sb("h1l", [P, 2, KC, GNP], F32R)
        h2h = sb("h2h", [P, 2, KC, GNP], F32R)
        h2l = sb("h2l", [P, 2, KC, GNP], F32R)
        o = sb("o", [BP, GU, HID])

        psT = pb("psT3", [P, 512])
        psF = [pb(f"psF3{b}", [P, 512]) for b in range(4)]
        psO = [pb(f"psO3{b}", [P, 512]) for b in range(3)]

        s_wr, s_pad, s_wh, s_wl, s_wrs = sem("e_wr"), sem("e_pad"), sem("e_wh"), sem("e_wl"), sem("e_wrs")
        s_xh, s_xl, s_rh, s_rl = sem("e_xh"), sem("e_xl"), sem("e_rh"), sem("e_rl")
        s_we, s_xgl, s_xrl = [sem("e_we0"), sem("e_we1")], sem("e_xgl"), sem("e_xrl")
        s_xg, s_tr, s_xT, s_lg = sem("e_xg"), sem("e_tr"), sem("e_xT"), sem("e_lg")
        s_sx, s_ex, s_wt, s_wtp, s_wT = sem("e_sx"), sem("e_ex"), sem("e_wt"), sem("e_wtp"), sem("e_wT")
        s_sm, s_tm = sem("e_sm"), sem("e_tm")
        s_turn = sem("e_turn_pool")
        s_f, s_r, s_l3, s_cb, s_out = sem("e_f"), sem("e_r"), sem("e_l3"), sem("e_cb"), sem("e_out")

        x1_v = io["x1"].rearrange("(g u p) d -> p g u d", p=BP, u=GU)
        out_v = io["out"].rearrange("(g u p) d -> p g u d", p=BP, u=GU)
        jobs = [(1, 0)] + [j for e in range(NE) for j in (([(1, e + 1)] if e + 1 < NE else []) + [(2, e)])]
        NJ = len(jobs)
        JF = 4
        parts = [(m, a, b) for m in range(KC) for a, b in HALVES_P]
        IT = GU * (NE + 1)

        def in_turn(g, job, columns, thirds, last_group):
            for q, (layer, e) in enumerate(jobs):
                if layer == 2 and 1 <= e < NE - 1:
                    thirds(e - 1)
                    if q == NJ - 2 and not last_group:
                        columns(g + 1, 1)
                job(q)
                if q == 3:
                    thirds(-1)
                if q >= NJ - 3 and not last_group:
                    columns(g + 1, (0, 2, 3)[q - (NJ - 3)])
            thirds(NE - 2)
            if not last_group:
                columns(g + 1, 4)
            thirds(NE - 1)

        block = c.enter_context(nc.Block())

        @block.sync
        def _(sp):
            def load(g, to, s):
                sp.dma_start(to[:, :, :], x1_v[:, bass.ds(g, 1), :, :].rearrange("p g u d -> p (g u) d")).then_inc(s, 16)

            def weights(e):
                if e >= 2:
                    sp.wait_ge(s_wl, 3 * e - 3)
                for l, a in enumerate(("W1", "W2", "Wo")):
                    sp.dma_start(we[:, e % 2, l, :, :], io["L0_ffn_" + a][e].rearrange("(k p) n -> p k n", p=P)).then_inc(s_we[e % 2], 16)

            weights(0)
            sp.dma_start(wr[:, :, :], io["L0_ffn_Wr"].rearrange("(k p) e -> p k e", p=P)).then_inc(s_wr, 16)
            sp.dma_start(br[:, :], io["L0_ffn_br"].partition_broadcast(BP)).then_inc(s_wr, 16)
            sp.dma_start(bo[:, :], io["L0_ffn_bo"]).then_inc(s_wr, 16)
            weights(1)
            load(0, xres, s_xrl)
            sp.wait_ge(s_tr, GU)
            load(1, xg, s_xgl)
            for e in range(2, NE):
                weights(e)

            def group(g, left):
                if left >= 1:
                    sp.wait_ge(s_cb, IT * g + GU)
                    load(g + 1, xres, s_xrl)
                if left >= 2:
                    sp.wait_ge(s_tr, GU * g + 2 * GU)
                    load(g + 2, xg, s_xgl)
                sp.wait_ge(s_cb, IT * g + IT)
                sp.dma_start(out_v[:, bass.ds(g, 1), :, :].rearrange("p g u d -> p (g u) d"), o[:, :, :]).then_inc(s_out, 16)

            with sp.Fori(0, G - 2) as g:
                group(g, 2)
            group(G - 2, 1)
            group(G - 1, 0)
            sp.wait_ge(s_out, 16 * G)

        @block.gpsimd
        def _(pool):
            nc.gpsimd.memset(xf[:, 0, 0, 0:2], 0.0).then_inc(s_pad, 1)
            pool.wait_ge(s_pad, 1)
            for t in (xh, xl):
                nc.gpsimd.tensor_copy(t[:, :, GN:GNP], xf[:, 0, 0:1, 0:2].rearrange("p a n -> p n a")).then_inc(s_pad, 1)

            def columns(g, u):
                pool.wait_ge(s_xh, GU * g + u + 1)
                held(pool, s_turn)
                nc.gpsimd.tensor_tensor(xl[:, :, u * BP:(u + 1) * BP], xf[:, u % 2, :, :], xh[:, :, u * BP:(u + 1) * BP],
                                        ALU.subtract).then_inc(s_xl, 1)

            def group(g, last_group):
                def job(q):
                    layer, e = jobs[q]
                    for n, (m, a, b) in enumerate(parts):
                        pool.wait_ge(s_rh, JF * NJ * g + JF * q + n + 1)
                        held(pool, s_turn)
                        high = h1h[:, e % 2, m, a:b] if layer == 1 else h2h[:, e % 2, m, a:b]
                        low = h1l[:, e % 2, m, a:b] if layer == 1 else h2l[:, e % 2, m, a:b]
                        nc.gpsimd.tensor_tensor(low, hf[:, n, 0:b - a], high, ALU.subtract).then_inc(s_rl, 1)

                in_turn(g, job, columns, lambda e: None, last_group)

            for u in range(GU):
                columns(0, u)
            with pool.Fori(0, G - 1) as g:
                group(g, False)
            group(G - 1, True)

        @block.scalar
        def _(act):
            def columns(g, u, fresh=False):
                act.wait_ge(s_tr, GU * g + u + 1)
                if not (fresh and u < 2):
                    act.wait_ge(s_xl, GU * g + u - 1)
                nc.scalar.activation(xf[:, u % 2, :, :], psT[:, 0:KC * BP].rearrange("p (k n) -> p k n", k=KC),
                                     ACT.Copy).then_inc(s_xT, 1)

            def router(g):
                act.wait_ge(s_sx, 3 * g + 3)
                nc.scalar.activation(ex[:, :, :], lg[:, :, :], ACT.Exp).then_inc(s_ex, 1)

            def group(g, fresh, last_group):
                def job(q):
                    layer, e = jobs[q]
                    if q == 0:
                        router(g)
                    col = 2 * e
                    for n, (m, a, b) in enumerate(parts):
                        act.wait_ge(s_f, JF * NJ * g + JF * q + n + 1)
                        if not (fresh and q == 0):
                            act.wait_ge(s_rl, JF * NJ * g + JF * (q - 1) + n + 1)
                        nc.scalar.activation(hf[:, n, 0:b - a], psF[n][:, 0:b - a], ACT.Relu,
                                             bias=scT[:, 2 * layer - 1, col + m:col + m + 1],
                                             scale=scT[:, 2 * layer - 2, col + m:col + m + 1]).then_inc(s_r, 1)

                in_turn(g, job, columns, lambda e: None, last_group)

            act.wait_ge(s_pad, 3)
            for u in range(GU):
                columns(0, u, True)
            group(0, True, False)
            with act.Fori(1, G - 1) as g:
                group(g, False, False)
            group(G - 1, False, True)

        @block.tensor
        def _(pe):
            def columns(g, u):
                if not (isinstance(g, int) and g == 0):
                    pe.wait_ge(s_xg, g)
                if u == 0:
                    if not (isinstance(g, int) and g == 0):
                        pe.wait_ge(s_wT, 2 * g)
                else:
                    pe.wait_ge(s_xT, GU * g + u)
                for k in range(KC):
                    last = nc.tensor.transpose(psT[:, k * BP:(k + 1) * BP], xg[:, u, k * P:(k + 1) * P],
                                               ident[0:BP, 0:BP])
                last.then_inc(s_tr, 1)

            def split_product(out, ws, xs, first=True, last=True):
                n = [(k, i) for k in range(KC) for i in ((1, 0), (0, 1), (0, 0))]
                n.sort(key=lambda ki: ki[1] == (0, 0))
                for at, (k, (iw, ix)) in enumerate(n):
                    mm = nc.tensor.matmul(out, ws(k)[iw], xs(k)[ix], start=(at == 0), stop=(at == len(n) - 1))
                return mm

            def router(g):
                pe.wait_ge(s_xT, GU * g + GU)
                pe.wait_ge(s_xl, GU * g + GU)
                for u in range(GU):
                    c0, c1 = u * BP, (u + 1) * BP
                    last = split_product(psT[0:BP, 400 + u * NE:400 + (u + 1) * NE],
                                         lambda k: (xh[:, k, c0:c1], xl[:, k, c0:c1]), lambda k: (wrh[:, k, :], wrl[:, k, :]))
                last.then_inc(s_lg, 1)

            def weights(g, part):
                if part == 0:
                    pe.wait_ge(s_wt, g + 1)
                else:
                    pe.wait_ge(s_wT, 2 * g + 1)
                for n, u in enumerate(((0, 1, 2), (3, 4))[part]):
                    last = nc.tensor.transpose(psT[0:NE, n * BP:(n + 1) * BP], wt[:, u, :], ident[0:BP, 0:BP])
                last.then_inc(s_wtp, 1)

            def free(g, n):
                if not (isinstance(g, int) and g == 0 and n < 3):
                    pe.wait_ge(s_cb, IT * g + n - 2)

            def biases(g):
                pe.wait_ge(s_wT, 2 * g + 2)
                for u in range(GU):
                    free(g, u)
                    nc.tensor.matmul(psO[u % 3][0:BP, 0:HID], wT[:, u * BP:(u + 1) * BP], bo[:, :], start=True, stop=True
                                     ).then_inc(s_l3, 1)

            def third(g, e):
                q = jobs.index((2, e))
                pe.wait_ge(s_rl, JF * NJ * g + JF * q + JF)
                if isinstance(g, int) and g == 0:
                    pe.wait_ge(s_wl, 3 * e + 3)
                for u in range(GU):
                    n = GU * (e + 1) + u
                    c0, c1 = u * BP, (u + 1) * BP
                    free(g, n)
                    split_product(psO[n % 3][0:BP, 0:HID], lambda k: (h2h[:, e % 2, k, c0:c1], h2l[:, e % 2, k, c0:c1]),
                                  lambda k: (wh[2][:, e, k, :], wl[2][:, e, k, :])).then_inc(s_l3, 1)

            def group(g, fresh, last_group):
                def job(q):
                    layer, e = jobs[q]
                    if layer == 2:
                        pe.wait_ge(s_rl, JF * NJ * g + JF * jobs.index((1, e)) + JF)
                    if fresh:
                        pe.wait_ge(s_wl, 3 * e + layer)
                    for n, (m, a, b) in enumerate(parts):
                        if q or not fresh:
                            pe.wait_ge(s_r, JF * NJ * g + JF * (q - 1) + n + 1)
                        split_product(
                            psF[n][:, 0:b - a],
                            lambda k: (wh[layer - 1][:, e, k, m * P:(m + 1) * P], wl[layer - 1][:, e, k, m * P:(m + 1) * P]),
                            lambda k: (xh[:, k, a:b], xl[:, k, a:b]) if layer == 1
                            else (h1h[:, e % 2, k, a:b], h1l[:, e % 2, k, a:b])).then_inc(s_f, 1)
                    if q in (1, 2):
                        weights(g, q - 1)

                in_turn(g, job, columns, lambda e: third(g, e) if e >= 0 else biases(g), last_group)
                if not last_group:
                    router(g + 1)

            for u in range(GU):
                columns(0, u)
            pe.wait_ge(s_wr, 48)
            pe.wait_ge(s_wrs, 2)
            router(0)
            group(0, True, False)
            with pe.Fori(1, G - 1) as g:
                group(g, False, False)
            group(G - 1, False, True)

        @block.vector
        def _(dve):
            def normal(g):
                dve.wait_ge(s_xgl, 16 * g)
                for u in range(GU):
                    last = nc.vector.tensor_scalar(xg[:, u, :], xg[:, u, :],
                                                   mv3[:, bass.ds(GU * g + u, 1), 0:1].rearrange("p t s -> p (t s)"),
                                                   rs3[:, bass.ds(GU * g + u, 1)], ALU.subtract, ALU.mult)
                last.then_inc(s_xg, 1)

            def logits(g):
                dve.wait_ge(s_lg, g + 1)
                nc.vector.tensor_tensor(lg[:, :, :], psT[0:BP, 400:400 + GU * NE].rearrange("p (u e) -> p u e", u=GU),
                                        br[:, :].unsqueeze(1).broadcast_to([BP, GU, NE]), ALU.add).then_inc(s_sx, 1)
                dve.wait_ge(s_sx, 3 * g + 1)
                nc.vector.tensor_reduce(mx[:, :], lg[:, :, :], AX.X, ALU.max).then_inc(s_sx, 1)
                dve.wait_ge(s_sx, 3 * g + 2)
                nc.vector.tensor_tensor(lg[:, :, :], lg[:, :, :], mx[:, :].unsqueeze(2).broadcast_to([BP, GU, NE]),
                                        ALU.subtract).then_inc(s_sx, 1)

            def softmax(g):
                dve.wait_ge(s_ex, g + 1)
                nc.vector.tensor_reduce(sm[:, :], ex[:, :, :], AX.X, ALU.add).then_inc(s_sm, 1)
                dve.wait_ge(s_sm, 2 * g + 1)
                nc.vector.reciprocal(mx[:, :], sm[:, :]).then_inc(s_sm, 1)
                dve.wait_ge(s_sm, 2 * g + 2)
                nc.vector.tensor_tensor(wt[:, :, :], ex[:, :, :], mx[:, :].unsqueeze(2).broadcast_to([BP, GU, NE]),
                                        ALU.mult).then_inc(s_wt, 1)

            def transposed(g, part):
                dve.wait_ge(s_wtp, 2 * g + part + 1)
                a, b = (0, 3 * BP) if part == 0 else (3 * BP, GN)
                nc.vector.tensor_copy(wT[:, a:b], psT[0:NE, 0:b - a]).then_inc(s_wT, 1)

            def columns(g, u):
                dve.wait_ge(s_xT, GU * g + u + 1)
                nc.vector.tensor_copy(xh[:, :, u * BP:(u + 1) * BP], xf[:, u % 2, :, :]).then_inc(s_xh, 1)

            def sums(g, e):
                if e < 0:
                    if not (isinstance(g, int) and g == 0):
                        dve.wait_ge(s_out, 16 * g)
                    dve.wait_ge(s_xrl, 16 * g + 16)
                for u in range(GU):
                    n = GU * (e + 1) + u
                    dve.wait_ge(s_l3, IT * g + n + 1)
                    ps = psO[n % 3][0:BP, 0:HID]
                    if e < 0:
                        nc.vector.tensor_tensor(o[:, u, :], ps, xres[:, u, :], ALU.add).then_inc(s_cb, 1)
                    else:
                        dve.wait_ge(s_cb, IT * g + n + 1 - GU)
                        nc.vector.scalar_tensor_tensor(out=o[:, u, :], in0=ps, scalar=wt[:, u, e:e + 1], in1=o[:, u, :],
                                                       op0=ALU.mult, op1=ALU.add).then_inc(s_cb, 1)

            def group(g, fresh, last_group):
                def job(q):
                    layer, e = jobs[q]
                    if q == 0:
                        logits(g)
                    for n, (m, a, b) in enumerate(parts):
                        dve.wait_ge(s_r, JF * NJ * g + JF * q + n + 1)
                        high = h1h[:, e % 2, m, a:b] if layer == 1 else h2h[:, e % 2, m, a:b]
                        nc.vector.tensor_copy(high, hf[:, n, 0:b - a]).then_inc(s_rh, 1)
                        if fresh and layer == 1 and 1 <= e < NE - 1:
                            split(e + 1, n)
                        if fresh and layer == 2 and e + 2 < NE and n < 2:
                            split(e + 2, JF + n)
                    if q == 0:
                        softmax(g)
                    if q in (1, 2):
                        transposed(g, q - 1)
                    if q == 4 and not last_group:
                        normal(g + 1)

                in_turn(g, job, columns, lambda e: sums(g, e), last_group)

            def split(e, step):
                l = step % 3
                if step < 3:
                    dve.wait_ge(s_we[e % 2], 48 * (e // 2) + 48)
                    nc.vector.tensor_copy(wh[l][:, e, :, :], we[:, e % 2, l, :, :]).then_inc(s_wh, 1)
                else:
                    dve.wait_ge(s_wh, 3 * e + l + 1)
                    nc.vector.tensor_tensor(wl[l][:, e, :, :], we[:, e % 2, l, :, :], wh[l][:, e, :, :], ALU.subtract).then_inc(s_wl, 1)

            for u in range(GU):
                columns(0, u)
            dve.wait_ge(s_wr, 48)
            nc.vector.tensor_copy(wrh[:, :, :], wr[:, :, :]).then_inc(s_wrs, 1)
            dve.wait_ge(s_wrs, 1)
            nc.vector.tensor_tensor(wrl[:, :, :], wr[:, :, :], wrh[:, :, :], ALU.subtract).then_inc(s_wrs, 1)
            for e in range(2):
                for step in range(6):
                    split(e, step)
            group(0, True, False)
            with dve.Fori(1, G - 1) as g:
                group(g, False, False)
            group(G - 1, False, True)


def build(nc, io):
    io = dict(io)
    io["kv"] = nc.dram_tensor("kv_rows", [N, KVW], F32, kind="Internal").ap()
    io["roots"] = nc.dram_tensor("variance_roots", [2, NE * HID], F32, kind="Internal").ap()
    io["x1"] = nc.dram_tensor("after_graph_layer", [N, HID], F32, kind="Internal").ap()
    io["res"] = nc.dram_tensor("residual", [N, HID], F32, kind="Internal").ap()
    io["rec"] = nc.dram_tensor("tile_records", [TILES, 3 * TL], F32, kind="Internal").ap()
    io["drel"] = nc.dram_tensor("step_destinations", [STEPS, TL], BF16, kind="Internal").ap()
    with ExitStack() as ctx:
        keep = {}

        def sb(stack, name, shape, dt=F32):
            keep[name] = stack.enter_context(nc.sbuf_tensor("k_" + name, shape, dt))

        sb(ctx, "ident", [P, P])
        sb(ctx, "iotaF", [P, P])
        sb(ctx, "iotaP", [P, 1])
        sb(ctx, "one", [1, 1])
        sb(ctx, "ones", [P, 1])
        sb(ctx, "mv3", [BP, NB, 2])
        sb(ctx, "rs3", [BP, NB])
        sb(ctx, "scT", [P, 4, NP])
        sb(ctx, "xg", [BP, GU, HID])
        with ExitStack() as summed:
            sb(summed, "acc", [BP, NB, HALFW])
            with ExitStack() as graph:
                sb(graph, "q3", [BP, 3, NB, HID], BF16)
                sb(graph, "brow", [1, STEPS], I32)
                sb(graph, "srcI", [P, LT * STEPS], I32)
                for n in ("dstR", "startN", "valN"):
                    sb(graph, n, [P, LT * STEPS])
                for n in ("fwd", "bwd"):
                    sb(graph, n, [1, C, H, W + 1], BF16)
                sb(graph, "nxt", [1, C, W], BF16)
                project(nc, ctx, io, keep)
                attend(nc, ctx, io, keep)
            mlp(nc, ctx, io, keep)
        experts(nc, ctx, io, keep)


_INS = ["x", "src", "dst"] + ["L0_gnn_" + n for n in (
    "Wq", "bq", "Wk", "bk", "Wv", "bv", "Wskip", "bskip", "ln1_g", "ln1_b", "W1", "b1", "W2", "b2", "ln2_g", "ln2_b")] + [
    "L0_ffn_" + n for n in ("Wr", "br", "W1", "b1", "g1", "be1", "m1", "v1", "W2", "b2", "g2", "be2", "m2", "v2", "Wo", "bo")]


def kernel(**inputs):
    import numpy as _np
    import concourse.bacc as _bacc
    from concourse import mybir as _mybir
    from concourse.bass_utils import run_bass_kernel_spmd as _run

    nc = _bacc.Bacc("TRN2", target_bir_lowering=False, num_devices=1)
    arrays, io = {}, {}
    for name in _INS:
        a = _np.ascontiguousarray(inputs[name])
        arrays[f"in_{name}"] = a
        io[name] = nc.dram_tensor(f"in_{name}", a.shape, _mybir.dt.from_np(a.dtype), kind="ExternalInput").ap()
    io["out"] = nc.dram_tensor("out_0", (N, HID), _mybir.dt.float32, kind="ExternalOutput").ap()
    build(nc, io)
    r = _run(nc, [arrays], core_ids=[0])
    return r.results[0]["out_0"]
```
